# Optimizing a Trainium2 kernel written in Bass

```python
import numpy as np
import jax
import jax.numpy as jnp

def _softmax(x, axis=-1):
    return jax.nn.softmax(x, axis=axis)

def _gelu(x):
    return jax.nn.gelu(x, approximate=True)

def _silu(x):
    return jax.nn.silu(x)

def _sigmoid(x):
    return jax.nn.sigmoid(x)

def _layernorm(x, axis=-1, eps=1e-05):
    m = jnp.mean(x, axis=axis, keepdims=True)
    v = jnp.var(x, axis=axis, keepdims=True)
    return (x - m) / jnp.sqrt(v + eps)

def _scatter_add(tgt, idx, src, axis=0):
    return tgt.at[idx].add(src)

def _segment_sum(src, seg, n):
    return jax.ops.segment_sum(src, seg, n)
kernel_name = 'mk_adaln_d1_jaxref_r2_ec4483'

def setup_inputs(seed: int=0):
    np.random.seed(seed)
    _w = jnp.asarray

    def _L0_attn_setup():
        import jax, jax.numpy as jnp
        import numpy as np
        B, S, DIN, DOUT, H, KVH = (2, 1024, 512, 512, 16, 16)
        HD = DOUT // H
        CB = 16
        CS = 16
        SB = 8
        TOPK = 2
        WIN = 128
        SCALE = 1.0 / np.sqrt(HD)

        def _rope(x, hd):
            b, s, d = x.shape
            xh = x.reshape(b, s, d // hd, hd)
            half = hd // 2
            inv = 1.0 / 10000.0 ** (jnp.arange(half, dtype=jnp.float32) * 2.0 / hd)
            ang = jnp.arange(s, dtype=jnp.float32)[:, None] * inv[None, :]
            cos = jnp.cos(ang)[None, :, None, :]
            sin = jnp.sin(ang)[None, :, None, :]
            x1, x2 = (xh[..., 0::2], xh[..., 1::2])
            out = jnp.stack([x1 * cos - x2 * sin, x1 * sin + x2 * cos], axis=-1)
            return out.reshape(b, s, d)

        def _masked_softmax(scores, mask):
            s = jnp.where(mask, scores, -jnp.inf)
            m = jnp.max(s, axis=-1, keepdims=True)
            m = jnp.where(jnp.isfinite(m), m, jnp.zeros_like(m))
            e = jnp.exp(s - m)
            den = jnp.sum(e, axis=-1, keepdims=True)
            return jnp.where(den > 0, e / jnp.where(den > 0, den, 1.0), jnp.zeros_like(e))
        key = jax.random.key(seed)
        ks = jax.random.split(key, 12)
        sc_in = 1.0 / np.sqrt(DIN)
        sc_out = 1.0 / np.sqrt(DOUT)
        return {'x': jax.random.normal(ks[0], (B, S, DIN), jnp.float32), 'Wq': jax.random.normal(ks[1], (DIN, DOUT), jnp.float32) * sc_in, 'Wk': jax.random.normal(ks[2], (DIN, KVH * HD), jnp.float32) * sc_in, 'Wv': jax.random.normal(ks[3], (DIN, KVH * HD), jnp.float32) * sc_in, 'Wo': jax.random.normal(ks[4], (DOUT, DOUT), jnp.float32) * sc_out, 'bo': jnp.zeros((DOUT,), jnp.float32), 'wk_comp': jax.random.normal(ks[5], (CB,), jnp.float32), 'wv_comp': jax.random.normal(ks[6], (CB,), jnp.float32), 'pe': jax.random.normal(ks[7], (CB, KVH * HD), jnp.float32), 'Wg': jax.random.normal(ks[8], (DIN, 3), jnp.float32) * sc_in, 'bg': jnp.zeros((3,), jnp.float32)}
    _L0_attn_in = _L0_attn_setup()

    def _L0_ffn_setup():
        import jax, jax.numpy as jnp
        import numpy as np
        B, S, D = (8, 2048, 512)
        E, R, K = (6, 16, 2)
        key = jax.random.key(seed)
        ks = jax.random.split(key, 9)
        sc = 0.02
        return {'x': jax.random.normal(ks[0], (B, S, D), jnp.float32), 'base_W': jax.random.normal(ks[1], (D, D), jnp.float32) * sc, 'base_b': jax.random.normal(ks[2], (D,), jnp.float32) * sc, 'shared_A': jax.random.normal(ks[3], (R, D), jnp.float32) * sc, 'shared_B': jax.random.normal(ks[4], (D, R), jnp.float32) * sc, 'routed_A': jax.random.normal(ks[5], (E, R, D), jnp.float32) * sc, 'routed_B': jax.random.normal(ks[6], (E, D, R), jnp.float32) * sc, 'router_W': jax.random.normal(ks[7], (E, D), jnp.float32) * sc, 'router_b': jax.random.normal(ks[8], (E,), jnp.float32) * sc}
    _L0_ffn_in = _L0_ffn_setup()
    _L0_c = _w((lambda *s: np.random.randn(*s).astype(np.float32) * 0.05)(8, 512))
    _L0_wmod = _w((lambda *s: np.random.randn(*s).astype(np.float32) * 0.05)(512, 6 * 512) * 512 ** (-0.5))
    _d = {'L0_attn_x': _L0_attn_in['x'], 'L0_attn_Wq': _L0_attn_in['Wq'], 'L0_attn_Wk': _L0_attn_in['Wk'], 'L0_attn_Wv': _L0_attn_in['Wv'], 'L0_attn_Wo': _L0_attn_in['Wo'], 'L0_attn_bo': _L0_attn_in['bo'], 'L0_attn_wk_comp': _L0_attn_in['wk_comp'], 'L0_attn_wv_comp': _L0_attn_in['wv_comp'], 'L0_attn_pe': _L0_attn_in['pe'], 'L0_attn_Wg': _L0_attn_in['Wg'], 'L0_attn_bg': _L0_attn_in['bg'], 'L0_ffn_base_W': _L0_ffn_in['base_W'], 'L0_ffn_base_b': _L0_ffn_in['base_b'], 'L0_ffn_shared_A': _L0_ffn_in['shared_A'], 'L0_ffn_shared_B': _L0_ffn_in['shared_B'], 'L0_ffn_routed_A': _L0_ffn_in['routed_A'], 'L0_ffn_routed_B': _L0_ffn_in['routed_B'], 'L0_ffn_router_W': _L0_ffn_in['router_W'], 'L0_ffn_router_b': _L0_ffn_in['router_b'], 'L0_c': _L0_c, 'L0_wmod': _L0_wmod}
    _x0 = _d['L0_attn_x']
    _d['L0_attn_x'] = jax.random.normal(jax.random.fold_in(jax.random.key(seed), 1), (8, 1024, 512), dtype=_x0.dtype)
    del _x0
    return _d

def reference(L0_attn_x, L0_attn_Wq, L0_attn_Wk, L0_attn_Wv, L0_attn_Wo, L0_attn_bo, L0_attn_wk_comp, L0_attn_wv_comp, L0_attn_pe, L0_attn_Wg, L0_attn_bg, L0_ffn_base_W, L0_ffn_base_b, L0_ffn_shared_A, L0_ffn_shared_B, L0_ffn_routed_A, L0_ffn_routed_B, L0_ffn_router_W, L0_ffn_router_b, L0_c, L0_wmod):

    def _L0_attn_ref(x, Wq, Wk, Wv, Wo, bo, wk_comp, wv_comp, pe, Wg, bg):
        import jax, jax.numpy as jnp
        import numpy as np
        B, S, DIN, DOUT, H, KVH = (2, 1024, 512, 512, 16, 16)
        HD = DOUT // H
        CB = 16
        CS = 16
        SB = 8
        TOPK = 2
        WIN = 128
        SCALE = 1.0 / np.sqrt(HD)

        def _rope(x, hd):
            b, s, d = x.shape
            xh = x.reshape(b, s, d // hd, hd)
            half = hd // 2
            inv = 1.0 / 10000.0 ** (jnp.arange(half, dtype=jnp.float32) * 2.0 / hd)
            ang = jnp.arange(s, dtype=jnp.float32)[:, None] * inv[None, :]
            cos = jnp.cos(ang)[None, :, None, :]
            sin = jnp.sin(ang)[None, :, None, :]
            x1, x2 = (xh[..., 0::2], xh[..., 1::2])
            out = jnp.stack([x1 * cos - x2 * sin, x1 * sin + x2 * cos], axis=-1)
            return out.reshape(b, s, d)

        def _masked_softmax(scores, mask):
            s = jnp.where(mask, scores, -jnp.inf)
            m = jnp.max(s, axis=-1, keepdims=True)
            m = jnp.where(jnp.isfinite(m), m, jnp.zeros_like(m))
            e = jnp.exp(s - m)
            den = jnp.sum(e, axis=-1, keepdims=True)
            return jnp.where(den > 0, e / jnp.where(den > 0, den, 1.0), jnp.zeros_like(e))
        b, s, _ = x.shape
        q = _rope(x @ Wq, HD)
        k = _rope(x @ Wk, HD)
        v = x @ Wv
        nb = (s - CB) // CS + 1
        kb = k[:, :nb * CS].reshape(b, nb, CB, -1) + pe[None, None]
        vb = v[:, :nb * CS].reshape(b, nb, CB, -1) + pe[None, None]
        ck = jnp.einsum('bnkd,k->bnd', kb, wk_comp)
        cv = jnp.einsum('bnkd,k->bnd', vb, wv_comp)
        q4 = q.reshape(b, s, H, HD).transpose(0, 2, 1, 3)
        k4 = k.reshape(b, s, KVH, HD).transpose(0, 2, 1, 3)
        v4 = v.reshape(b, s, KVH, HD).transpose(0, 2, 1, 3)
        ck4 = ck.reshape(b, nb, KVH, HD).transpose(0, 2, 1, 3)
        cv4 = cv.reshape(b, nb, KVH, HD).transpose(0, 2, 1, 3)
        sc = jnp.einsum('bhsd,bhnd->bhsn', q4, ck4) * SCALE
        comp_mask = (jnp.arange(nb) + 1) * CS <= jnp.arange(s)[:, None]
        a_comp = _masked_softmax(sc, comp_mask[None, None])
        out_comp = jnp.einsum('bhsn,bhnd->bhsd', a_comp, cv4).transpose(0, 2, 1, 3).reshape(b, s, DOUT)
        imp = sc.mean(axis=(1, 2))
        _, top_idx = jax.lax.top_k(imp, TOPK)
        pos = (top_idx * CS)[:, :, None] + jnp.arange(SB)[None, None, :]
        pos = pos.reshape(b, TOPK * SB)
        valid = pos < s
        posc = jnp.minimum(pos, s - 1)
        sel_k = jnp.take_along_axis(k, posc[..., None], axis=1) * valid[..., None]
        sel_v = jnp.take_along_axis(v, posc[..., None], axis=1) * valid[..., None]
        M = TOPK * SB
        ks4 = sel_k.reshape(b, M, KVH, HD).transpose(0, 2, 1, 3)
        vs4 = sel_v.reshape(b, M, KVH, HD).transpose(0, 2, 1, 3)
        ss = jnp.einsum('bhsd,bhmd->bhsm', q4, ks4) * SCALE
        causal_sel = jnp.arange(s)[None, :, None] >= pos[:, None, :]
        a_sel = _masked_softmax(ss, (causal_sel & valid[:, None, :])[:, None])
        out_sel = jnp.einsum('bhsm,bhmd->bhsd', a_sel, vs4).transpose(0, 2, 1, 3).reshape(b, s, DOUT)
        sw = jnp.einsum('bhsd,bhtd->bhst', q4, k4) * SCALE
        rows = jnp.arange(s)[:, None]
        cols = jnp.arange(s)[None, :]
        wmask = (cols <= rows) & (cols > rows - WIN)
        a_win = _masked_softmax(sw, wmask[None, None])
        out_win = jnp.einsum('bhst,bhtd->bhsd', a_win, v4).transpose(0, 2, 1, 3).reshape(b, s, DOUT)
        g = jax.nn.softmax(x @ Wg + bg, axis=-1)
        out = g[..., 0:1] * out_comp + g[..., 1:2] * out_sel + g[..., 2:3] * out_win
        return out @ Wo + bo

    def _L0_ffn_ref(x, base_W, base_b, shared_A, shared_B, routed_A, routed_B, router_W, router_b):
        import jax, jax.numpy as jnp
        import numpy as np
        B, S, D = (8, 2048, 512)
        E, R, K = (6, 16, 2)
        base_out = jax.lax.stop_gradient(jnp.einsum('bsi,oi->bso', x, base_W) + base_b)
        shared_out = jnp.einsum('bsr,or->bso', jnp.einsum('bsi,ri->bsr', x, shared_A), shared_B)
        logits = jnp.einsum('bsi,ei->bse', x, router_W) + router_b
        gate = jax.nn.softmax(logits, axis=-1)
        topk_w, topk_i = jax.lax.top_k(gate, K)
        sparse_w = jnp.sum(jax.nn.one_hot(topk_i, E, dtype=gate.dtype) * topk_w[..., None], axis=-2)
        sparse_w = sparse_w / (jnp.sum(sparse_w, axis=-1, keepdims=True) + 1e-06)
        h = jnp.einsum('bsi,eri->bser', x, routed_A)
        routed_outs = jnp.einsum('bser,eor->bseo', h, routed_B)
        routed_out = jnp.einsum('bseo,bse->bso', routed_outs, sparse_w)
        return base_out + shared_out + routed_out
    x = L0_attn_x
    mod = (_silu(L0_c) @ L0_wmod).reshape(L0_c.shape[0], 6, 1, -1)
    sa, ca, ga, sb, cb, gb = (mod[:, 0], mod[:, 1], mod[:, 2], mod[:, 3], mod[:, 4], mod[:, 5])
    ga = (2 * (ga >= 0) - 1) * jnp.maximum(jnp.abs(ga), 0.25)
    gb = (2 * (gb >= 0) - 1) * jnp.maximum(jnp.abs(gb), 0.25)
    h = _layernorm(x, axis=-1) * (1 + ca) + sa
    x = x + ga * _L0_attn_ref(h, L0_attn_Wq, L0_attn_Wk, L0_attn_Wv, L0_attn_Wo, L0_attn_bo, L0_attn_wk_comp, L0_attn_wv_comp, L0_attn_pe, L0_attn_Wg, L0_attn_bg)
    h = _layernorm(x, axis=-1) * (1 + cb) + sb
    x = x + gb * _L0_ffn_ref(h, L0_ffn_base_W, L0_ffn_base_b, L0_ffn_shared_A, L0_ffn_shared_B, L0_ffn_routed_A, L0_ffn_routed_B, L0_ffn_router_W, L0_ffn_router_b)
    return x

_drawn_inputs = setup_inputs


def setup_inputs(seed=0):
    import zlib

    import numpy as np

    out = dict(_drawn_inputs(seed))
    spreads = {'L0_attn_bo': (0.0, 0.376), 'L0_attn_bg': (0.0, 0.8)}
    factors = {'L0_ffn_base_b': 8.0,
     'L0_ffn_shared_A': 6.975,
     'L0_ffn_shared_B': 7.027,
     'L0_ffn_routed_A': 8.0,
     'L0_ffn_routed_B': 8.0,
     'L0_ffn_router_W': 8.0,
     'L0_ffn_router_b': 8.0}
    for name, (base, spread) in spreads.items():
        noise = np.random.default_rng([zlib.crc32(name.encode()), seed]).standard_normal(out[name].shape)
        drawn = base * np.exp(spread * noise) if base else spread * noise
        out[name] = jnp.asarray(drawn.astype(out[name].dtype))
    for name, factor in factors.items():
        out[name] = (out[name] * factor).astype(out[name].dtype)
    return out
```

```python
from contextlib import ExitStack

import numpy as np
import concourse.bass as bass
from concourse import mybir

F32 = mybir.dt.float32
BF16 = mybir.dt.bfloat16
U32 = mybir.dt.uint32
ALU = mybir.AluOpType
ACT = mybir.ActivationFunctionType
AX = mybir.AxisListType

P = 128
B, S, D = 8, 1024, 512
NT = S // P
NC = D // P
H, HD = 16, 32
CB, NB = 16, 64
SB, TOPK = 8, 2
NSEL = SB * TOPK
CS = NSEL + NB
E, R = 6, 16
NZ = R + E * R
SCALE = 1.0 / np.sqrt(HD)
NEG = -1e30
FLOOR = -1e29
EPS = 1e-5

C_ID, C_WM, C_CM, C_ROT, C_BLK, C_TOK, C_IO, C_END = np.cumsum(
    [0, P, 2 * P, NT * NB, NT * 2 * HD, 2 * (NB - 8) + 8, NT * NSEL, 8]).tolist()


def constants():
    p = np.arange(P)
    out = np.zeros((P, C_END), np.float32)
    out[:, C_ID:C_WM] = np.eye(P)
    k = np.arange(P)
    out[:, C_WM:C_WM + P] = np.where(k[None] > p[:, None], 0, NEG)
    out[:, C_WM + P:C_CM] = np.where(k[None] <= p[:, None], 0, NEG)
    tok = np.arange(NT)[None, :, None] * P + p[:, None, None]
    out[:, C_CM:C_ROT] = np.where((np.arange(NB) + 1) * CB <= tok, 0, NEG).reshape(P, -1)
    half = HD // 2
    inv = (np.float32(1.0) / np.float32(10000.0) ** (np.arange(half, dtype=np.float32) * np.float32(2.0) / np.float32(HD))).astype(np.float32)
    ang = (np.arange(S, dtype=np.float32)[:, None] * inv[None, :]).astype(np.float32)
    cos, sin = np.cos(ang), np.sin(ang)
    rot = np.concatenate([np.repeat(cos, 2, axis=1), -sin, sin], axis=1)
    out[:, C_ROT:C_BLK] = rot.reshape(NT, P, 2 * HD).transpose(1, 0, 2).reshape(P, -1)
    out[:, C_BLK:C_TOK] = np.arange(2 * (NB - 8) + 8)[None] - (NB - 8) == p[:, None] // CB
    out[:, C_TOK:C_IO] = (tok - np.arange(NSEL) % SB).reshape(P, -1)
    out[:, C_IO:C_END] = np.arange(8)
    return out


N_FIRST = 2 + 2 * P // CB + 5
SILU_STEPS = 3
SETUP_V = GUARD_STEPS = 3 + 3 + 6 + 8
SETUP_G = 5
CS_STEPS = 11
G_STEPS = 3
B_STEPS = 4 + 3 * TOPK
R_STEPS = 16

def slot_units(c1, a, c2):
    order = ["HT", "Y", "Q", "K", "H2T", "Z", "G", "QT", "KT", "F", "ZT", "V"]
    stage = dict(HT=a, Q=a, K=a, V=a, QT=a, KT=a, G=a, Y=c2, H2T=c2, Z=c2, ZT=c2, F=c2)
    return [u for u in order if stage[u]]


def segment_units(c, a):
    units = []
    for s in range(NT + 1):
        units += [(u, s - 1) for u in slot_units(c, a and s > 0, c and s > 0)]
    if a:
        units += [(u, 0) for u in ("CKT", "IMP", "POS", "SELV")]
    return units


SETUP_UNITS = [(f"MOD{i}", 0) for i in range(6)] + [("MODT", 0)]
SEGMENTS = {"pro": SETUP_UNITS + segment_units(False, True), "loop": segment_units(True, True),
            "epi": segment_units(True, False)}


def m_unit(seg, b, name, t):
    i = SEGMENTS[seg].index((name, t))
    bank, before = i % 2, i // 2
    per = {s: (len(u) + 1 - bank) // 2 for s, u in SEGMENTS.items()}
    if seg == "pro":
        return bank, before
    return bank, (b if seg == "loop" else B - 1) * per["loop"] + per["pro"] + before


def tile_blocks(t):
    whats = (["prev"] if t else []) + ["own", "cs"]
    return [((half, j, i), w) for half in range(2) for j in range(4) for i in range(2) for w in whats]


ZT_ROUND = 4


def tp_rounds(t):
    return len(tile_blocks(t)) // 4


TP_BATCH = sum(tp_rounds(t) for t in range(NT))


def tp_before(b, t):
    return TP_BATCH * b + sum(tp_rounds(u) for u in range(t))


def program(nc, x, wqkv, wo, wbt, wa, wb, cT, wmod, bo, bg, rb, wcomp, pe, wg, const, gscr, out):
    with ExitStack() as ctx:
        def sb(name, shape, dt=F32):
            return ctx.enter_context(nc.sbuf_tensor(name, shape, dt))

        def sem(name):
            return ctx.enter_context(nc.semaphore(name))

        wqkv_s = sb("wqkv_s", [P, NC, 3 * D])
        wo_s = sb("wo_s", [P, NC, D])
        wbt_s = sb("wbt_s", [P, NC, D])
        wa_s = sb("wa_s", [P, NC, NZ + E])
        wb_s = sb("wb_s", [NZ + 1, D])
        wg_s = sb("wg_s", [P, NC, 3])
        cst = sb("cst", [P, C_END])
        ident = cst[:, C_ID:C_WM]
        rot = cst[:, C_ROT:C_BLK].rearrange("p (t n) -> p t n", t=NT)
        token = cst[:, C_TOK:C_IO].rearrange("p (t n) -> p t n", t=NT)
        ident_b = sb("ident_b", [P, P], BF16)
        wmask = sb("wmask", [P, 2 * P], BF16)
        csmask = sb("csmask", [P, NT, CS], BF16)
        wcol = sb("wcol", [P, 2])
        blkw = sb("blkw", [P, 2, C_TOK - C_BLK])
        pe_s = sb("pe_s", [CB, D])
        pew = sb("pew", [CB, 2, NB])
        bo_s = sb("bo_s", [P, D])
        bg_s = sb("bg_s", [P, 3])
        rb_s = sb("rb_s", [P, E])
        ones = sb("ones", [1, P])
        cT_s = sb("cT_s", [P, NC, B])
        silu = sb("silu", [P, 3, NC, B])
        modT = sb("modT", [P, 4, NC, B])
        mod_a = sb("mod_a", [P, 2, NC])
        mod_c = sb("mod_c", [P, 2, NC])
        gbc = sb("gbc", [P, 2, D])
        boga = sb("boga", [P, D])
        xa = sb("xa", [P, 2, D])
        sta = sb("sta", [P, 6])
        mva = sb("mva", [P, 2])
        vea = sb("vea", [P, 2])
        power = sb("power", [P, 1])
        xn = sb("xn", [P, D])
        hT = sb("hT", [P, NC, P])
        ra = sb("ra", [P, D])
        rbf = sb("rbf", [P, D])
        qr = sb("qr", [P, D])
        kr = sb("kr", [P, D])
        qT = sb("qT", [P, NC, S])
        kT = sb("kT", [P, NC, S])
        v_s = sb("v_s", [P, NT, D])
        qsum = sb("qsum", [P, NC, NT])
        gl = sb("gl", [P, 8])
        gates = sb("gates", [P, NT, 3])
        ckrow = qr[0:NB, :]
        csv = sb("csv", [P, D])
        csk = sb("csk", [P, NC, CS])
        qs = sb("qs", [P, NC])
        imp = sb("imp", [1, NB])
        top = sb("top", [1, 8])
        topi = sb("topi", [1, 8], U32)
        pos = sb("pos", [1, 2])
        posb = sb("posb", [P, 2])
        held = sb("held", [P, 1])
        onehot = sb("onehot", [P, NT, NSEL])
        css = sb("css", [P, H, CS])
        csp = sb("csp", [P, H, P])
        cm = sb("cm", [P, 2, H])
        cden = sb("cden", [P, 4, H])
        pw = sb("pw", [P, H, 2 * P])
        wmax = sb("wmax", [P, H])
        wden = sb("wden", [P, 3, H])
        pT = sb("pT", [P, 4, 4, P])
        aT = sb("aT", [P, NC, P])
        xc = sb("xc", [P, 2, D])
        xb = sb("xb", [P, D])
        t1 = sb("t1", [P, D])
        x1 = sb("x1", [P, D])
        stc = sb("stc", [P, 6])
        mvc = sb("mvc", [P, 2])
        vec = sb("vec", [P, 2])
        x2n = sb("x2n", [P, D])
        h2T = sb("h2T", [P, NC, P])
        zs = sb("zs", [P, NZ + E])
        ro = sb("ro", [P, 48])
        roi = sb("roi", [P, 8], U32)
        zr = sb("zr", [P, NZ + 1])
        zT = sb("zT", [NZ + 1, P])
        o_s = sb("o_s", [P, 2, D])
        modr = pT[0:B].rearrange("p a b n -> p (a b n)").rearrange("p (a n) -> p a n", a=4)
        gr = css[0:B].rearrange("p a n -> p (a n)")[:, 0:2 * D].rearrange("p (a n) -> p a n", a=2)
        gpart = o_s[0:B]
        wm_ring = pw[:, :, :].rearrange("p a b -> p (a b)").rearrange("p (s c n) -> p s c n", s=2, c=NC)

        ps_s = [ctx.enter_context(nc.psum_tensor(f"ps_s{i}", [P, 512], F32)) for i in range(3)]
        ps_m = [ctx.enter_context(nc.psum_tensor(f"ps_m{i}", [P, 512], F32)) for i in range(2)]
        ps_t = ctx.enter_context(nc.psum_tensor("ps_t", [P, 4, P], F32))
        ps_o = ctx.enter_context(nc.psum_tensor("ps_o", [P, NC, P], F32))
        t_banks = [ps_t, ps_s[0][:].rearrange("p (k n) -> p k n", k=4)]
        ps_c = ctx.enter_context(nc.psum_tensor("ps_c", [P, D], F32))

        d_first = sem("d_first")
        d_w = sem("d_w")
        d_mod = [sem("d_mod0"), sem("d_mod1")]
        d_xa = [sem("d_xa0"), sem("d_xa1")]
        d_xc = [sem("d_xc0"), sem("d_xc1")]
        d_scr = sem("d_scr")
        d_gbc = sem("d_gbc")
        d_out = [sem("d_out0"), sem("d_out1")]
        started = sem("started")
        set_v, set_a, set_g = sem("set_v"), sem("set_a"), sem("set_g")
        m_full = [sem("m_full0"), sem("m_full1")]
        m_done = [sem("m_done0"), sem("m_done1")]
        s_full = [sem(f"s_full{i}") for i in range(3)]
        s_done = [sem(f"s_done{i}") for i in range(3)]
        t_full, t_done = sem("t_full"), sem("t_done")
        pv_done = sem("pv_done")
        o_done = sem("o_done")
        wmax_ok = sem("wmax_ok")
        wn_ok = sem("wn_ok")
        cs_ok = sem("cs_ok")
        cs_exp = sem("cs_exp")
        cs_norm = sem("cs_norm")
        lna, lnc = sem("lna"), sem("lnc")
        lnap, lncp = sem("lnap"), sem("lncp")
        rope_ok = sem("rope_ok")
        qsum_ok = sem("qsum_ok")
        g_ok, g_exp = sem("g_ok"), sem("g_exp")
        ckv_full, ckv_done = sem("ckv_full"), sem("ckv_done")
        selv_ok = sem("selv_ok")
        b_ok = sem("b_ok")
        xb_ok = sem("xb_ok")
        y_ok = sem("y_ok")
        r_ok, r_exp = sem("r_ok"), sem("r_exp")
        o_ok = sem("o_ok")
        modc_ok, moda_ok = sem("modc_ok"), sem("moda_ok")
        boga_ok = sem("boga_ok")
        credited = (set_v, set_a, set_g, *m_full, *m_done, *s_full, *s_done, t_full, t_done, pv_done, o_done,
                    wmax_ok, wn_ok, cs_ok, cs_exp, cs_norm, lna, lnc, lnap, lncp, rope_ok, qsum_ok, g_ok, g_exp,
                    ckv_full, ckv_done, selv_ok, b_ok, xb_ok, y_ok, r_ok, r_exp, o_ok, modc_ok, moda_ok, boga_ok)

        def m_bank(seg, b, name, t):
            bank, _ = m_unit(seg, b, name, t)
            return ps_m[bank], m_done[bank]

        def m_free_at(seg, b, name, t):
            bank, before = m_unit(seg, b, name, t)
            return m_done[bank], before + 1

        def m_full_at(seg, b, name, t):
            bank, before = m_unit(seg, b, name, t)
            return m_full[bank], before + 2

        def m_done_at(seg, b, name, t):
            bank, before = m_unit(seg, b, name, t)
            return m_done[bank], before + 2

        block = ctx.enter_context(nc.Block())

        @block.sync
        def _(sp):
            for s in credited:
                sp.sem_inc(s, 1)
            sp.sem_inc(started, 1)
            for s in d_out:
                sp.sem_inc(s, 16)
            sp.dma_start(cT_s[:], cT.rearrange("(c p) b -> p c b", p=P)).then_inc(d_first, 16)
            sp.dma_start(cst[:], const).then_inc(d_first, 16)
            n_first = 2

            def load_mod(i):
                if i >= 2:
                    bank, before = m_unit("pro", 0, f"MOD{i - 2}", 0)
                    sp.wait_ge(m_full[bank], before + 2)
                sp.dma_start(wm_ring[:, i % 2], wmod[:, i * D:(i + 1) * D].rearrange("(c p) n -> p c n", p=P)
                             ).then_inc(d_mod[i % 2], 16)

            load_mod(0)
            load_mod(1)
            for i in range(P // CB):
                for w in range(2):
                    sp.dma_start(wcol[i * CB:(i + 1) * CB, w:w + 1], wcomp[w].rearrange("(p a) -> p a", a=1)
                                 ).then_inc(d_first, 16)
                    n_first += 1
            for dst, src in ((pe_s[:], pe), (bo_s[:], bo.partition_broadcast(P)), (bg_s[:], bg.partition_broadcast(P)),
                             (rb_s[:], rb.partition_broadcast(P)),
                             (wg_s[:], wg.rearrange("(c p) n -> p c n", p=P))):
                sp.dma_start(dst, src).then_inc(d_first, 16)
                n_first += 1
            assert n_first == N_FIRST

            def load_xa(T_former, b, t):
                if T_former is not None:
                    sp.wait_ge(lna, 4 * T_former + 5)
                sp.dma_start(xa[:, t % 2, :], x[b, t * P:(t + 1) * P, :]).then_inc(d_xa[t % 2], 16)

            def load_xc(T, b, t):
                if t > 0:
                    sp.wait_ge(xb_ok, T)
                sp.dma_start(xc[:, t % 2, :], x[b, t * P:(t + 1) * P, :]).then_inc(d_xc[t % 2], 16)

            def store(T, b, t):
                sp.wait_ge(o_ok, 1 + T + 1)
                sp.dma_start(out[b, t * P:(t + 1) * P, :], o_s[:, t % 2, :]).then_inc(d_out[t % 2], 16)

            def load_gates(b):
                sp.wait_ge(o_ok, NT * b + 1)
                sp.wait_ge(d_scr, 16 * (2))
                for i in range(2):
                    sp.dma_start(gbc[:, i, :], gscr[i, b, :].partition_broadcast(P)).then_inc(d_gbc, 16)

            load_xa(None, 0, 0)
            load_xa(None, 0, 1)
            sp.dma_start(wqkv_s[:], wqkv.rearrange("(c p) n -> p c n", p=P)).then_inc(d_w, 16)
            for i in range(2, 6):
                load_mod(i)
            sp.dma_start(wo_s[:], wo.rearrange("(c p) n -> p c n", p=P)).then_inc(d_w, 16)
            sp.dma_start(wbt_s[:], wbt.rearrange("(c p) n -> p c n", p=P)).then_inc(d_w, 16)
            sp.dma_start(wa_s[:], wa.rearrange("(c p) n -> p c n", p=P)).then_inc(d_w, 16)
            sp.dma_start(wb_s[:], wb).then_inc(d_w, 16)
            sp.wait_ge(set_v, GUARD_STEPS + 1)
            for i in range(2):
                sp.dma_start(gscr[i], gr[:, i, :]).then_inc(d_scr, 16)
            for t in range(2, NT):
                load_xa(t - 2, 0, t)

            def batch(b, a):
                load_gates(b)
                for s in range(NT + 1):
                    if s < NT:
                        load_xc(NT * b + s, b, s)
                    if a and s < NT:
                        load_xa(NT * b + NT + s - 2, b + 1, s)
                    if s > 0:
                        store(NT * b + s - 1, b, s - 1)

            with sp.Fori(0, B - 1) as b:
                batch(b, True)
            batch(B - 1, False)
            for i in range(2):
                sp.wait_ge(d_out[i], 16 * (B * NT // 2 + 1))
            sp.wait_ge(d_scr, 32)

        @block.tensor
        def _(pe_):
            def m_target(seg, b, name, t):
                bank, _ = m_unit(seg, b, name, t)
                return ps_m[bank], m_full[bank]

            pe_.wait_ge(d_first, 16 * (N_FIRST))
            pe_.wait_ge(set_v, SILU_STEPS + 1)
            for i in range(6):
                pe_.wait_ge(*m_free_at("pro", 0, f"MOD{i}", 0))
                ps, full = m_target("pro", 0, f"MOD{i}", 0)
                pe_.wait_ge(d_mod[i % 2], 16 * (i // 2 + 1))
                for c in range(NC):
                    mm = pe_.matmul(ps[0:B, :], silu[:, 2, c, :], wm_ring[:, i % 2, c, :], start=(c == 0), stop=(c == NC - 1))
                mm.then_inc(full, 1)
            pe_.wait_ge(*m_free_at("pro", 0, "MODT", 0))
            ps, full = m_target("pro", 0, "MODT", 0)
            pe_.wait_ge(*m_done_at("pro", 0, "MOD4", 0))
            pe_.wait_ge(*m_done_at("pro", 0, "MOD5", 0))
            for i in range(4):
                for c in range(NC):
                    k = (i * NC + c) * B
                    mm = pe_.transpose(ps[:, k:k + B], modr[:, i, c * P:(c + 1) * P], ident[0:B, 0:B])
            mm.then_inc(full, 1)
            pe_.wait_ge(d_w, 16 * 5)
            pe_.wait_ge(set_v, SETUP_V + 1)

            def transpose_h(seg, b, t, T):
                pe_.wait_ge(*m_free_at(seg, b, "HT", t))
                ps, full = m_target(seg, b, "HT", t)
                pe_.wait_ge(lna, 4 * T + 5)
                for c in range(NC):
                    mm = pe_.transpose(ps[:, c * P:(c + 1) * P], xn[:, c * P:(c + 1) * P], ident)
                mm.then_inc(full, 1)

            def project(seg, b, t, name, col, chunks=range(NC)):
                ps, full = m_target(seg, b, name, t)
                if chunks[0] == 0:
                    pe_.wait_ge(*m_free_at(seg, b, name, t))
                if name == "Q" and chunks[0] == 0:
                    pe_.wait_ge(*m_done_at(seg, b, "HT", t))
                for c in chunks:
                    mm = pe_.matmul(ps[:], hT[:, c, :], wqkv_s[:, c, col * D:(col + 1) * D],
                                    start=(c == 0), stop=(c == NC - 1))
                if c == NC - 1:
                    mm.then_inc(full, 1)

            def transpose_rot(seg, b, t, T, name, src, n):
                pe_.wait_ge(*m_free_at(seg, b, name, t))
                ps, full = m_target(seg, b, name, t)
                pe_.wait_ge(rope_ok, 2 * T + n + 1)
                for c in range(NC):
                    mm = pe_.transpose(ps[:, c * P:(c + 1) * P], src[:, c * P:(c + 1) * P], ident)
                mm.then_inc(full, 1)

            def gate_logits(seg, b, t):
                pe_.wait_ge(*m_free_at(seg, b, "G", t))
                ps, full = m_target(seg, b, "G", t)
                for c in range(NC):
                    mm = pe_.matmul(ps[:, 0:3], hT[:, c, :], wg_s[:, c, :], start=(c == 0), stop=(c == NC - 1))
                mm.then_inc(full, 1)

            def compress(seg, b, t, T, batch_a):
                if t == 0:
                    pe_.wait_ge(ckv_done, batch_a + 1)
                    for w in range(2):
                        pe_.matmul(ps_c[w * NB:(w + 1) * NB, :], pew[:, w, :], pe_s[:, :], start=True, stop=False,
                                   skip_group_check=True)
                pe_.wait_ge(*m_done_at(seg, b, "V", t))
                off = NB - 8 - 8 * t
                for w, src in ((0, kr[:, :]), (1, v_s[:, t, :])):
                    mm = pe_.matmul(ps_c[w * NB:(w + 1) * NB, :], blkw[:, w, off:off + NB], src,
                                    start=False, stop=(t == NT - 1), skip_group_check=True)
                if t == NT - 1:
                    mm.then_inc(ckv_full, 1)

            def select(seg, b, batch_a):
                pe_.wait_ge(*m_free_at(seg, b, "CKT", 0))
                ps, full = m_target(seg, b, "CKT", 0)
                pe_.wait_ge(ckv_done, batch_a + 2)
                for c in range(NC):
                    mm = pe_.transpose(ps[:, c * P:(c + 1) * P], qr[:, c * P:(c + 1) * P], ident)
                mm.then_inc(full, 1)
                pe_.wait_ge(*m_free_at(seg, b, "IMP", 0))
                ps, full = m_target(seg, b, "IMP", 0)
                pe_.wait_ge(*m_done_at(seg, b, "CKT", 0))
                pe_.wait_ge(b_ok, B_STEPS * batch_a + 2)
                for c in range(NC):
                    mm = pe_.matmul(ps[0:1, 0:NB], qs[:, c:c + 1], csk[:, c, NSEL:CS], start=(c == 0), stop=(c == NC - 1))
                mm.then_inc(full, 1)
                pe_.wait_ge(*m_free_at(seg, b, "POS", 0))
                ps, full = m_target(seg, b, "POS", 0)
                pe_.wait_ge(b_ok, B_STEPS * batch_a + 5)
                pe_.matmul(ps[:, 0:2], ones[:, :], pos[:, :], start=True, stop=True).then_inc(full, 1)
                pe_.wait_ge(*m_free_at(seg, b, "SELV", 0))
                ps, full = m_target(seg, b, "SELV", 0)
                pe_.wait_ge(b_ok, B_STEPS * batch_a + B_STEPS + 1)
                for t in range(NT):
                    mm = pe_.matmul(ps[0:NSEL, :], onehot[:, t, :], v_s[:, t, :], start=(t == 0), stop=(t == NT - 1))
                mm.then_inc(full, 1)

            def score_round(b, t, r):
                T = NT * b + t
                bank = r % 3
                pe_.wait_ge(s_done[bank], 4 * T + r // 3 + 1)
                if r == 0:
                    pe_.wait_ge(t_done, tp_before(b, t) + 1)
                ps = ps_s[bank]
                if r < 4:
                    rows = slice(HD * r, HD * r + HD)
                    dst = ps[:, 0:4 * CS].rearrange("p (c n) -> p c n", c=4)
                    if t == 0 and r == 0:
                        pe_.wait_ge(selv_ok, b + 2)
                    pe_.matmul(dst, ident_b[:, :], csmask[:, t, :].unsqueeze(1).broadcast_to([P, 4, CS]),
                               start=True, stop=False, skip_group_check=True)
                    for c in range(NC):
                        mm = pe_.matmul(dst[:, c, :], qT[rows, c, t * P:(t + 1) * P], csk[rows, c, :],
                                        start=False, stop=True, skip_group_check=True)
                else:
                    half, j = divmod(r - 4, 4)
                    rows = slice(HD * j, HD * j + HD)
                    k0, n = ((t - 1) * P, 2 * P) if t else (0, P)
                    dst = ps[:, 0:2 * n].rearrange("p (c n) -> p c n", c=2)
                    pe_.matmul(dst, ident_b[:, :], wmask[:, 2 * P - n:].unsqueeze(1).broadcast_to([P, 2, n]),
                               start=True, stop=False, skip_group_check=True)
                    for i in range(2):
                        mm = pe_.matmul(dst[:, i, :], qT[rows, 2 * half + i, t * P:(t + 1) * P],
                                        kT[rows, 2 * half + i, k0:k0 + n], start=False, stop=True, skip_group_check=True)
                mm.then_inc(s_full[bank], 1)

            def head_column(slot):
                half, j, i = slot
                return (half * 4 + j) * 2 + i

            def transpose_round(b, t, i):
                T, n = NT * b + t, tp_before(b, t) + i
                if i >= 2:
                    pe_.wait_ge(t_done, n)
                elif i == 1:
                    pe_.wait_ge(s_done[0], 4 * T + 9 // 3 + 2)
                dst = t_banks[i % 2]
                blocks = tile_blocks(t)
                for k in range(4):
                    (half, j, ii), what = blocks[4 * i + k]
                    hw = head_column((half, j, ii))
                    if what == "cs":
                        src = csp[:, 4 * j + 2 * half + ii, :]
                        if i < 2:
                            pe_.wait_ge(cs_norm, 2 * T + 3)
                    else:
                        src = pw[:, hw, P:2 * P] if what == "own" else pw[:, hw, 0:P]
                        if k == 0 or blocks[4 * i + k - 1][0][0] != half:
                            pe_.wait_ge(wn_ok, 6 * T + 3 * half + 4)
                    mm = pe_.transpose(dst[:, k, :], src, ident)
                mm.then_inc(t_full, 1)

            def value_round(b, t, i):
                T, n = NT * b + t, tp_before(b, t) + i
                if i == 0:
                    pe_.wait_ge(o_done, T + 1)
                pe_.wait_ge(t_done, n + 2)
                blocks = tile_blocks(t)
                for k in range(4):
                    m = 4 * i + k
                    (half, j, ii), what = blocks[m]
                    c = 2 * half + ii
                    cols = slice(P * c + HD * j, P * c + HD * j + HD)
                    src = csv[:, cols] if what == "cs" else v_s[:, t if what == "own" else t - 1, cols]
                    mm = pe_.matmul(ps_o[HD * j:HD * j + HD, c, :], src, pT[:, i % 4, k, :],
                                    start=(m == 0 or blocks[m - 1][0] != blocks[m][0]), stop=(what == "cs"),
                                    skip_group_check=True)
                mm.then_inc(pv_done, 1)

            def output(seg, b, t):
                pe_.wait_ge(*m_free_at(seg, b, "Y", t))
                ps, full = m_target(seg, b, "Y", t)
                pe_.wait_ge(o_done, NT * b + t + 2)
                for c in range(NC):
                    mm = pe_.matmul(ps[:], aT[:, c, :], wo_s[:, c, :], start=(c == 0), stop=(c == NC - 1))
                mm.then_inc(full, 1)

            def transpose_h2(seg, b, t):
                pe_.wait_ge(*m_free_at(seg, b, "H2T", t))
                ps, full = m_target(seg, b, "H2T", t)
                pe_.wait_ge(lnc, 4 * (NT * b + t) + 5)
                for c in range(NC):
                    mm = pe_.transpose(ps[:, c * P:(c + 1) * P], x2n[:, c * P:(c + 1) * P], ident)
                mm.then_inc(full, 1)

            def lora_down(seg, b, t):
                pe_.wait_ge(*m_free_at(seg, b, "Z", t))
                ps, full = m_target(seg, b, "Z", t)
                pe_.wait_ge(*m_done_at(seg, b, "H2T", t))
                for c in range(NC):
                    mm = pe_.matmul(ps[:, 0:NZ + E], h2T[:, c, :], wa_s[:, c, :], start=(c == 0), stop=(c == NC - 1))
                mm.then_inc(full, 1)

            def transpose_z(seg, b, t):
                pe_.wait_ge(*m_free_at(seg, b, "ZT", t))
                ps, full = m_target(seg, b, "ZT", t)
                pe_.wait_ge(r_ok, R_STEPS * (NT * b + t + 1) + 1)
                pe_.transpose(ps[0:NZ + 1, 0:P], zr[:, :], ident).then_inc(full, 1)

            def feed(seg, b, t, chunks=range(NC + 1)):
                ps, full = m_target(seg, b, "F", t)
                if chunks[0] == 0:
                    pe_.wait_ge(*m_free_at(seg, b, "F", t))
                for c in chunks:
                    if c < NC:
                        pe_.matmul(ps[:], h2T[:, c, :], wbt_s[:, c, :], start=(c == 0), stop=False)
                    else:
                        pe_.wait_ge(*m_done_at(seg, b, "ZT", t))
                        pe_.matmul(ps[:], zT[:, :], wb_s[:, :], start=False, stop=True).then_inc(full, 1)

            def slot(seg, b, s, c, a):
                c1, c2, a = c and s < NT, c and s > 0, a and s > 0
                t = s - 1
                ba = b + 1 if seg == "loop" else 0
                Ta = NT * ba + t
                if c1:
                    for r in range(4):
                        score_round(b, s, r)
                if a:
                    transpose_h(seg, b, t, Ta)
                if c1:
                    score_round(b, s, 4)
                if c2:
                    output(seg, b, t)
                if c1:
                    score_round(b, s, 5)
                if a:
                    project(seg, b, t, "Q", 0)
                if c1:
                    score_round(b, s, 6)
                    score_round(b, s, 7)
                if a:
                    project(seg, b, t, "K", 1)
                if c2:
                    transpose_h2(seg, b, t)
                if c1:
                    score_round(b, s, 8)
                    score_round(b, s, 9)
                if c1:
                    score_round(b, s, 10)
                if c2:
                    lora_down(seg, b, t)
                if c1:
                    score_round(b, s, 11)
                if a:
                    gate_logits(seg, b, t)
                    transpose_rot(seg, b, t, Ta, "QT", qr, 1)
                    transpose_rot(seg, b, t, Ta, "KT", kr, 2)
                if c1:
                    n = tp_rounds(s)
                    transpose_round(b, s, 0)
                    transpose_round(b, s, 1)
                    for i in range(n):
                        if c2:
                            if i < NC:
                                feed(seg, b, t, [i])
                            if i == ZT_ROUND:
                                transpose_z(seg, b, t)
                            if i == ZT_ROUND + 2:
                                feed(seg, b, t, [NC])
                        if a and n - 1 - NC <= i < n - 1:
                            project(seg, b, t, "V", 2, [i - (n - 1 - NC)])
                        value_round(b, s, i)
                        if i + 2 < n:
                            transpose_round(b, s, i + 2)
                else:
                    if c2:
                        feed(seg, b, t, range(NC))
                        transpose_z(seg, b, t)
                        feed(seg, b, t, [NC])
                    if a:
                        project(seg, b, t, "V", 2)
                if a:
                    compress(seg, b, t, Ta, ba)

            for s in range(1, NT + 1):
                slot("pro", 0, s, False, True)
            select("pro", 0, 0)
            with pe_.Fori(0, B - 1) as b:
                for s in range(NT + 1):
                    slot("loop", b, s, True, True)
                select("loop", b, b + 1)
            for s in range(NT + 1):
                slot("epi", B - 1, s, True, False)

        @block.scalar
        def _(act):
            act.wait_ge(d_first, 16 * (N_FIRST))
            act.activation(silu[:, 0], cT_s[:], ACT.Exp, scale=-1.0).then_inc(set_a, 1)
            for k, i in enumerate((0, 1, 3, 4)):
                act.wait_ge(*m_full_at("pro", 0, f"MOD{i}", 0))
                ps, done = m_bank("pro", 0, f"MOD{i}", 0)
                act.activation(modr[:, k, :], ps[0:B, :], ACT.Copy).then_inc(done, 1)

            def h_scaled(seg, b, t, name, dst, mod, mod_sem, mod_count):
                act.wait_ge(*m_full_at(seg, b, name, t))
                ps, done = m_bank(seg, b, name, t)
                if t == 0:
                    act.wait_ge(mod_sem, mod_count + 1)
                for c in range(NC):
                    ins = act.activation(dst[:, c, :], ps[:, c * P:(c + 1) * P], ACT.Identity,
                                         scale=mod[:, 1, c:c + 1], bias=mod[:, 0, c:c + 1])
                ins.then_inc(done, 1)

            def copy_v(seg, b, t):
                act.wait_ge(*m_full_at(seg, b, "V", t))
                ps, done = m_bank(seg, b, "V", t)
                act.activation(v_s[:, t, :], ps[:], ACT.Copy).then_inc(done, 1)

            def copy_qT(seg, b, t):
                act.wait_ge(*m_full_at(seg, b, "QT", t))
                ps, done = m_bank(seg, b, "QT", t)
                act.activation(qT[:, :, t * P:(t + 1) * P], ps[:].rearrange("p (c n) -> p c n", c=NC), ACT.Copy,
                               scale=float(SCALE)).then_inc(done, 1)

            def copy_kT(seg, b, t):
                act.wait_ge(*m_full_at(seg, b, "KT", t))
                ps, done = m_bank(seg, b, "KT", t)
                act.activation(kT[:, :, t * P:(t + 1) * P], ps[:].rearrange("p (c n) -> p c n", c=NC), ACT.Copy
                               ).then_inc(done, 1)

            def gate_exp(Ta):
                act.wait_ge(g_ok, G_STEPS * Ta + 2)
                act.activation(gl[:, 3:6], gl[:, 0:3], ACT.Exp, bias=gl[:, 6:7], accum_out=gl[:, 7:8]).then_inc(g_exp, 1)

            def cs_copy(b, t, r):
                T = NT * b + t
                act.wait_ge(s_full[r % 3], 4 * T + r // 3 + 2)
                if r == 0:
                    act.wait_ge(cs_ok, CS_STEPS * T + 1)
                    act.wait_ge(cs_norm, 2 * T + 1)
                act.activation(css[:, 4 * r:4 * r + 4, :], ps_s[r % 3][:, 0:4 * CS].rearrange("p (c n) -> p c n", c=4),
                               ACT.Copy).then_inc(s_done[r % 3], 1)

            def cs_exps(b, t):
                T = NT * b + t
                act.wait_ge(cs_ok, CS_STEPS * T + 6)
                act.wait_ge(t_full, tp_before(b, t) + 1)
                act.activation(csp[:, :, 0:NSEL], css[:, :, 0:NSEL], ACT.Exp).then_inc(cs_exp, 1)
                act.activation(csp[:, :, P - NB:P], css[:, :, NSEL:CS], ACT.Exp).then_inc(cs_exp, 1)

            def window_exp(b, t, r):
                T = NT * b + t
                act.wait_ge(wmax_ok, 8 * T + r - 2)
                if r == 4:
                    act.wait_ge(t_full, tp_before(b, t) + 1)
                    act.wait_ge(wn_ok, 6 * T + 1)
                n = 2 * P if t else P
                for i in range(2):
                    hw = 2 * (r - 4) + i
                    ins = act.activation(pw[:, hw, 2 * P - n:2 * P], ps_s[r % 3][:, i * n:(i + 1) * n], ACT.Exp,
                                         bias=wmax[:, hw:hw + 1], accum_out=wden[:, 0, hw:hw + 1])
                ins.then_inc(s_done[r % 3], 1)

            def copy_z(seg, b, t):
                act.wait_ge(*m_full_at(seg, b, "Z", t))
                ps, done = m_bank(seg, b, "Z", t)
                act.wait_ge(r_ok, R_STEPS * (NT * b + t) + 1)
                act.activation(zs[:, :], ps[:, 0:NZ + E], ACT.Copy).then_inc(done, 1)

            def router_exp(b, t):
                T = NT * b + t
                act.wait_ge(r_ok, R_STEPS * T + 3)
                act.activation(ro[:, 8:14], ro[:, 0:6], ACT.Exp, bias=ro[:, 6:7], accum_out=ro[:, 7:8]).then_inc(r_exp, 1)

            def copy_zT(seg, b, t):
                act.wait_ge(*m_full_at(seg, b, "ZT", t))
                ps, done = m_bank(seg, b, "ZT", t)
                act.activation(zT[:, :], ps[0:NZ + 1, 0:P], ACT.Copy).then_inc(done, 1)

            def probs_copy(b, t, i):
                n = tp_before(b, t) + i
                act.wait_ge(t_full, n + 2)
                if i >= 4:
                    act.wait_ge(pv_done, n - 2)
                act.activation(pT[:, i % 4], t_banks[i % 2][:], ACT.Copy).then_inc(t_done, 1)

            def copy_out(b, t):
                act.wait_ge(pv_done, tp_before(b, t) + tp_rounds(t) + 1)
                act.activation(aT[:], ps_o[:], ACT.Copy).then_inc(o_done, 1)

            def select(seg, b, ba):
                act.wait_ge(ckv_full, ba + 2)
                act.activation(ckrow[:, :], ps_c[0:NB, :], ACT.Copy)
                act.activation(csv[P - NB:P, :], ps_c[NB:P, :], ACT.Copy).then_inc(ckv_done, 1)
                act.wait_ge(*m_full_at(seg, b, "CKT", 0))
                ps, done = m_bank(seg, b, "CKT", 0)
                act.activation(csk[:, :, NSEL:CS], ps[:].rearrange("p (c n) -> p c n", c=NC)[:, :, 0:NB], ACT.Copy
                               ).then_inc(done, 1)
                act.wait_ge(*m_full_at(seg, b, "SELV", 0))
                ps, done = m_bank(seg, b, "SELV", 0)
                act.activation(csv[0:NSEL, :], ps[0:NSEL, :], ACT.Copy).then_inc(done, 1)
                act.wait_ge(*m_done_at(seg, b, "SELV", 0))
                act.sem_inc(selv_ok, 1)

            def slot(seg, b, s, c, a):
                c1, c2, a = c and s < NT, c and s > 0, a and s > 0
                t = s - 1
                ba = b + 1 if seg == "loop" else 0
                Ta = NT * ba + t
                if c1:
                    for r in range(4):
                        cs_copy(b, s, r)
                if a:
                    h_scaled(seg, b, t, "HT", hT, mod_a, moda_ok, ba + 1)
                if c1:
                    window_exp(b, s, 4)
                    window_exp(b, s, 5)
                    window_exp(b, s, 6)
                    window_exp(b, s, 7)
                    cs_exps(b, s)
                if c2:
                    h_scaled(seg, b, t, "H2T", h2T, mod_c, modc_ok, b + 1)
                if c1:
                    window_exp(b, s, 8)
                    window_exp(b, s, 9)
                if c1:
                    window_exp(b, s, 10)
                if c2:
                    copy_z(seg, b, t)
                if c1:
                    window_exp(b, s, 11)
                if c2:
                    router_exp(b, t)
                if a:
                    gate_exp(Ta)
                    copy_qT(seg, b, t)
                    copy_kT(seg, b, t)
                if c1:
                    for i in range(tp_rounds(s)):
                        probs_copy(b, s, i)
                        if c2 and i == ZT_ROUND:
                            copy_zT(seg, b, t)
                    copy_out(b, s)
                elif c2:
                    copy_zT(seg, b, t)
                if a:
                    copy_v(seg, b, t)

            act.wait_ge(*m_full_at("pro", 0, "MODT", 0))
            ps, done = m_bank("pro", 0, "MODT", 0)
            v = ps[:, 0:4 * NC * B].rearrange("p (m c b) -> p m c b", m=4, c=NC)
            for i in range(4):
                ins = act.activation(modT[:, i], v[:, i], ACT.Copy, bias=float(i % 2))
            ins.then_inc(done, 1)
            for s in range(1, NT + 1):
                slot("pro", 0, s, False, True)
            select("pro", 0, 0)
            act.wait_ge(d_scr, 32)
            with act.Fori(0, B - 1) as b:
                for s in range(NT + 1):
                    slot("loop", b, s, True, True)
                select("loop", b, b + 1)
            for s in range(NT + 1):
                slot("epi", B - 1, s, True, False)

        @block.gpsimd
        def _(gp):
            gp.memset(power[:], -0.5).then_inc(set_g, 1)
            gp.memset(csp[:], 0.0).then_inc(set_g, 1)
            gp.memset(csv[:], 0.0).then_inc(set_g, 1)
            gp.memset(ones[:], 1.0).then_inc(set_g, 1)
            gp.memset(zr[:], 1.0).then_inc(set_g, 1)
            gp.wait_ge(set_g, SETUP_G + 1)

            def deviation_a(Ta):
                gp.wait_ge(lna, 4 * Ta + 4)
                gp.tensor_tensor(vea[:, 1:2], vea[:, 0:1], power[:], ALU.pow).then_inc(lnap, 1)

            def deviation_c(T):
                gp.wait_ge(lnc, 4 * T + 4)
                gp.tensor_tensor(vec[:, 1:2], vec[:, 0:1], power[:], ALU.pow).then_inc(lncp, 1)

            def rotate(seg, b, t, Ta, name, dst):
                gp.wait_ge(*m_done_at(seg, b, name, t))
                gp.tensor_tensor(dst[:], ra[:], rbf[:], ALU.add).then_inc(rope_ok, 1)

            def cs_normalise(b, t):
                T = NT * b + t
                gp.wait_ge(cs_ok, CS_STEPS * T + CS_STEPS + 1)
                for lo, n, w in ((0, NSEL, 2), (P - NB, NB, 3)):
                    v = csp[:, :, lo:lo + n]
                    gp.tensor_tensor(v, v, cden[:, w, :].unsqueeze(2).broadcast_to([P, H, n]), ALU.mult
                                     ).then_inc(cs_norm, 1)

            def bias_gate(b):
                gp.wait_ge(d_gbc, 16 * (2 * b + 2))
                gp.tensor_tensor(boga[:], bo_s[:], gbc[:, 0, :], ALU.mult).then_inc(boga_ok, 1)
                gp.wait_ge(boga_ok, b + 2)

            def residual_in(b, t):
                T = NT * b + t
                gp.wait_ge(d_xc[t % 2], 16 * (4 * b + t // 2 + 1))
                gp.wait_ge(y_ok, T + 1)
                gp.tensor_tensor(xb[:], xc[:, t % 2, :], boga[:], ALU.add).then_inc(xb_ok, 1)

            def slot(seg, b, s, c, a, prefetch):
                c1, c2, a = c and s < NT, c and s > 0, a and s > 0
                t = s - 1
                ba = b + 1 if seg == "loop" else 0
                Ta = NT * ba + t
                if c2:
                    deviation_c(NT * b + t)
                if a:
                    rotate(seg, b, t, Ta, "Q", qr)
                    rotate(seg, b, t, Ta, "K", kr)
                if c1:
                    cs_normalise(b, s)
                if prefetch:
                    deviation_a(Ta + 1)
                if c1:
                    residual_in(b, s)

            gp.wait_ge(d_first, 16 * (N_FIRST))
            deviation_a(0)
            for s in range(1, NT + 1):
                slot("pro", 0, s, False, True, s < NT)
            with gp.Fori(0, B - 1) as b:
                bias_gate(b)
                for s in range(NT + 1):
                    slot("loop", b, s, True, True, s < NT)
            bias_gate(B - 1)
            for s in range(NT + 1):
                slot("epi", B - 1, s, True, False, False)

        @block.vector
        def _(dve):
            steps = [0]

            def setup(ins):
                steps[0] += 1
                ins.then_inc(set_v, 1)
                dve.wait_ge(set_v, steps[0] + 1)

            dve.wait_ge(d_first, 16 * (N_FIRST))
            dve.wait_ge(set_a, 2)
            setup(dve.tensor_scalar(silu[:, 0], silu[:, 0], 1.0, None, ALU.add))
            setup(dve.reciprocal(silu[:, 1], silu[:, 0]))
            setup(dve.tensor_tensor(silu[:, 2], cT_s[:], silu[:, 1], ALU.mult))
            assert steps[0] == SILU_STEPS
            setup(dve.tensor_copy(ident_b[:], ident))
            setup(dve.tensor_copy(wmask[:], cst[:, C_WM:C_CM]))
            setup(dve.tensor_copy(csmask[:, :, NSEL:CS], cst[:, C_CM:C_ROT].rearrange("p (t n) -> p t n", t=NT)))
            for w in range(2):
                setup(dve.tensor_scalar(blkw[:, w, :], cst[:, C_BLK:C_TOK], wcol[:, w:w + 1], None, ALU.mult))
                setup(dve.memset(pew[:, w, :], 1.0))
                setup(dve.tensor_scalar(pew[:, w, :], pew[:, w, :], wcol[0:CB, w:w + 1], None, ALU.mult))
            for k, i in enumerate((2, 5)):
                dve.wait_ge(*m_full_at("pro", 0, f"MOD{i}", 0))
                ps, done = m_bank("pro", 0, f"MOD{i}", 0)
                dve.tensor_copy(gpart[:, 0, :], ps[0:B, :]).then_inc(done, 1)
                dve.wait_ge(*m_done_at("pro", 0, f"MOD{i}", 0))
                setup(dve.tensor_scalar(gpart[:, 1, :], gpart[:, 0, :], 0.0, 2.0, ALU.is_ge, ALU.mult))
                setup(dve.tensor_scalar(gpart[:, 1, :], gpart[:, 1, :], -1.0, None, ALU.add))
                setup(dve.scalar_tensor_tensor(out=gpart[:, 0, :], in0=gpart[:, 0, :], scalar=-1.0, in1=gpart[:, 0, :],
                                               op0=ALU.mult, op1=ALU.max))
                setup(dve.scalar_tensor_tensor(out=gr[:, k, :], in0=gpart[:, 0, :], scalar=0.25, in1=gpart[:, 1, :],
                                               op0=ALU.max, op1=ALU.mult))
            assert steps[0] == GUARD_STEPS == SETUP_V

            def hold():
                dve.memset(held[:], 0.0)

            def ln_stats(x_, st, mv, ve, s, T):
                dve.bn_stats(st[:], x_).then_inc(s, 1)
                dve.wait_ge(s, 4 * T + 2)
                hold()
                dve.bn_aggr(mv[:], st[:]).then_inc(s, 1)
                dve.wait_ge(s, 4 * T + 3)
                dve.tensor_scalar(ve[:, 0:1], mv[:, 1:2], EPS, None, ALU.add).then_inc(s, 1)

            def ln_scale(x_, mv, ve, dst, s, sp_, T):
                dve.wait_ge(sp_, T + 2)
                dve.tensor_scalar(dst[:], x_, mv[:, 0:1], ve[:, 1:2], ALU.subtract, ALU.mult).then_inc(s, 1)

            def ln_a(seg, b, t, Ta, tile_a):
                dve.wait_ge(d_xa[tile_a % 2], 16 * (4 * (b + 1 if seg == "loop" else 0) + tile_a // 2 + 1))
                if tile_a > 0:
                    dve.wait_ge(*m_done_at(seg, b, "HT", tile_a - 1))
                ln_stats(xa[:, tile_a % 2, :], sta, mva, vea, lna, Ta)
                ln_scale(xa[:, tile_a % 2, :], mva, vea, xn, lna, lnap, Ta)

            def mod_copy(b, dst, first, ok):
                dve.tensor_copy(dst[:], modT[:, first:first + 2, :, b]).then_inc(ok, 1)

            def rope(seg, b, t, name):
                dve.wait_ge(*m_full_at(seg, b, name, t))
                ps, done = m_bank(seg, b, name, t)
                q3 = ps[:].rearrange("p (h n) -> p h n", h=H)
                q4 = ps[:].rearrange("p (h n e) -> p h n e", h=H, e=2)
                r4 = rbf[:].rearrange("p (h n e) -> p h n e", h=H, e=2)
                dve.tensor_tensor(ra[:].rearrange("p (h n) -> p h n", h=H), q3,
                                  rot[:, t, 0:HD].unsqueeze(1).broadcast_to([P, H, HD]), ALU.mult)
                for e in range(2):
                    half = HD // 2
                    w = rot[:, t, HD + e * half:HD + (e + 1) * half].unsqueeze(1).broadcast_to([P, H, half])
                    ins = dve.tensor_tensor(r4[:, :, :, e], q4[:, :, :, 1 - e], w, ALU.mult)
                ins.then_inc(done, 1)

            def sum_q(seg, b, t, Ta):
                dve.wait_ge(*m_done_at(seg, b, "QT", t))
                dve.tensor_reduce(qsum[:, :, t], qT[:, :, t * P:(t + 1) * P], AX.X, ALU.add).then_inc(qsum_ok, 1)

            def gates_soft(seg, b, t, Ta, part):
                if part == 1:
                    dve.wait_ge(g_exp, Ta + 2)
                    dve.reciprocal(gl[:, 7:8], gl[:, 7:8]).then_inc(g_ok, 1)
                    dve.wait_ge(g_ok, G_STEPS * Ta + 3)
                    dve.tensor_scalar(gates[:, t, :], gl[:, 3:6], gl[:, 7:8], None, ALU.mult).then_inc(g_ok, 1)
                    return
                dve.wait_ge(*m_full_at(seg, b, "G", t))
                ps, done = m_bank(seg, b, "G", t)
                dve.tensor_tensor(gl[:, 0:3], ps[:, 0:3], bg_s[:], ALU.add).then_inc(done, 1)
                dve.wait_ge(*m_done_at(seg, b, "G", t))
                dve.tensor_reduce(gl[:, 6:7], gl[:, 0:3], AX.X, ALU.max, negate=True).then_inc(g_ok, 1)

            def window_max(b, t, r):
                T = NT * b + t
                dve.wait_ge(s_full[r % 3], 4 * T + r // 3 + 2)
                if r == 4:
                    dve.wait_ge(s_done[11 % 3], 4 * T + 1)
                n = 2 * P if t else P
                dve.tensor_reduce(wmax[:, 2 * (r - 4):2 * (r - 3)],
                                  ps_s[r % 3][:, 0:2 * n].rearrange("p (c n) -> p c n", c=2), AX.X, ALU.max,
                                  negate=True).then_inc(wmax_ok, 1)

            def window_norm(b, t, half):
                T = NT * b + t
                h0 = 8 * half
                dve.wait_ge(s_done[(4 + 4 * half + 3) % 3], 4 * T + (4 + 4 * half + 3) // 3 + 2)
                base = 6 * T + 3 * half
                dve.reciprocal(wden[:, 1, h0:h0 + 8], wden[:, 0, h0:h0 + 8]).then_inc(wn_ok, 1)
                dve.wait_ge(wn_ok, base + 2)
                dve.tensor_scalar(wden[:, 2, h0:h0 + 8], wden[:, 1, h0:h0 + 8], gates[:, t, 2:3], None, ALU.mult
                                  ).then_inc(wn_ok, 1)
                dve.wait_ge(wn_ok, base + 3)
                lo = 0 if t else P
                for h in range(h0, h0 + 8):
                    ins = dve.tensor_scalar(pw[:, h, lo:2 * P], pw[:, h, lo:2 * P], wden[:, 2, h:h + 1], None, ALU.mult)
                ins.then_inc(wn_ok, 1)

            parts = ((0, NSEL), (NSEL, CS))

            def cs_shift(b, t):
                T = NT * b + t
                base = CS_STEPS * T
                dve.wait_ge(s_done[3 % 3], 4 * T + 3 // 3 + 2)
                for w, (lo, hi) in enumerate(parts):
                    dve.tensor_reduce(cm[:, w, :], css[:, :, lo:hi], AX.X, ALU.max).then_inc(cs_ok, 1)
                dve.wait_ge(cs_ok, base + 3)
                dve.tensor_scalar(cm[:], cm[:], FLOOR, None, ALU.max).then_inc(cs_ok, 1)
                dve.wait_ge(cs_ok, base + 4)
                for w, (lo, hi) in enumerate(parts):
                    dve.tensor_tensor(css[:, :, lo:hi], css[:, :, lo:hi],
                                      cm[:, w, :].unsqueeze(2).broadcast_to([P, H, hi - lo]), ALU.subtract
                                      ).then_inc(cs_ok, 1)

            def cs_factor(b, t):
                T = NT * b + t
                base = CS_STEPS * T
                dve.wait_ge(cs_exp, 2 * T + 3)
                for w, (lo, n) in enumerate(((0, NSEL), (P - NB, NB))):
                    dve.tensor_reduce(cden[:, w, :], csp[:, :, lo:lo + n], AX.X, ALU.add).then_inc(cs_ok, 1)
                dve.wait_ge(cs_ok, base + 8)
                dve.tensor_scalar(cden[:, 0:2, :], cden[:, 0:2, :], 1e-30, None, ALU.max).then_inc(cs_ok, 1)
                dve.wait_ge(cs_ok, base + 9)
                dve.reciprocal(cden[:, 2:4, :], cden[:, 0:2, :]).then_inc(cs_ok, 1)
                dve.wait_ge(cs_ok, base + 10)
                for w, g in ((2, 1), (3, 0)):
                    dve.tensor_scalar(cden[:, w, :], cden[:, w, :], gates[:, t, g:g + 1], None, ALU.mult).then_inc(cs_ok, 1)

            def residual(seg, b, t):
                T = NT * b + t
                dve.wait_ge(*m_full_at(seg, b, "Y", t))
                ps, done = m_bank(seg, b, "Y", t)
                if t == 0:
                    dve.wait_ge(d_gbc, 16 * (2 * b + 2))
                dve.wait_ge(o_ok, T + 1)
                dve.tensor_tensor(t1[:], ps[:], gbc[:, 0, :], ALU.mult).then_inc(done, 1)
                dve.wait_ge(*m_done_at(seg, b, "Y", t))
                dve.wait_ge(xb_ok, T + 2)
                dve.tensor_tensor(x1[:], t1[:], xb[:], ALU.add).then_inc(y_ok, 1)
                dve.wait_ge(y_ok, T + 2)
                ln_stats(x1[:], stc, mvc, vec, lnc, T)

            def router(seg, b, t, part):
                T = NT * b + t
                base = R_STEPS * T
                n = [0 if part == 0 else 2]

                def step(ins):
                    n[0] += 1
                    ins.then_inc(r_ok, 1)
                    if n[0] != 2:
                        dve.wait_ge(r_ok, base + n[0] + 1)

                if part == 0:
                    dve.wait_ge(*m_done_at(seg, b, "Z", t))
                    step(dve.tensor_tensor(ro[:, 0:E], zs[:, NZ:NZ + E], rb_s[:], ALU.add))
                    step(dve.tensor_reduce(ro[:, 6:7], ro[:, 0:E], AX.X, ALU.max, negate=True))
                    return
                dve.wait_ge(r_exp, T + 2)
                step(dve.reciprocal(ro[:, 15:16], ro[:, 7:8]))
                step(dve.tensor_scalar(ro[:, 16:16 + E], ro[:, 8:8 + E], ro[:, 15:16], None, ALU.mult))
                hold()
                step(dve.max(ro[:, 24:32], ro[:, 16:24]))
                hold()
                step(dve.max_index(roi[:], ro[:, 24:32], ro[:, 16:24]))
                step(dve.tensor_copy(ro[:, 40:42], roi[:, 0:2]))
                step(dve.tensor_scalar(ro[:, 32:32 + E], cst[:, C_IO:C_IO + E], ro[:, 40:41], None, ALU.is_equal))
                step(dve.scalar_tensor_tensor(out=ro[:, 32:32 + E], in0=cst[:, C_IO:C_IO + E], scalar=ro[:, 41:42],
                                              in1=ro[:, 32:32 + E], op0=ALU.is_equal, op1=ALU.add))
                step(dve.tensor_tensor(ro[:, 32:32 + E], ro[:, 32:32 + E], ro[:, 16:16 + E], ALU.mult))
                step(dve.tensor_reduce(ro[:, 42:43], ro[:, 32:32 + E], AX.X, ALU.add))
                step(dve.tensor_scalar(ro[:, 42:43], ro[:, 42:43], 1e-6, None, ALU.add))
                step(dve.reciprocal(ro[:, 43:44], ro[:, 42:43]))
                step(dve.tensor_scalar(ro[:, 32:32 + E], ro[:, 32:32 + E], ro[:, 43:44], None, ALU.mult))
                step(dve.tensor_copy(zr[:, 0:R], zs[:, 0:R]))
                step(dve.tensor_tensor(zr[:, R:NZ].rearrange("p (e r) -> p e r", e=E),
                                       zs[:, R:NZ].rearrange("p (e r) -> p e r", e=E),
                                       ro[:, 32:32 + E].unsqueeze(2).broadcast_to([P, E, R]), ALU.mult))
                assert n[0] == R_STEPS

            def final(seg, b, t):
                T = NT * b + t
                dve.wait_ge(*m_full_at(seg, b, "F", t))
                ps, done = m_bank(seg, b, "F", t)
                dve.tensor_tensor(t1[:], ps[:], gbc[:, 1, :], ALU.mult).then_inc(done, 1)
                dve.wait_ge(*m_done_at(seg, b, "F", t))
                dve.wait_ge(d_out[t % 2], 16 * (4 * b + t // 2 + 1))
                dve.tensor_tensor(o_s[:, t % 2, :], x1[:], t1[:], ALU.add).then_inc(o_ok, 1)

            def select(seg, b, ba):
                base = B_STEPS * ba
                dve.wait_ge(qsum_ok, NT * ba + NT + 1)
                dve.tensor_reduce(qs[:], qsum[:], AX.X, ALU.add).then_inc(b_ok, 1)
                dve.wait_ge(*m_full_at(seg, b, "IMP", 0))
                ps, done = m_bank(seg, b, "IMP", 0)
                dve.tensor_copy(imp[:], ps[0:1, 0:NB]).then_inc(done, 1)
                dve.wait_ge(*m_done_at(seg, b, "IMP", 0))
                hold()
                dve.max(top[:], imp[:]).then_inc(b_ok, 1)
                dve.wait_ge(b_ok, base + 3)
                hold()
                dve.max_index(topi[:], top[:], imp[:]).then_inc(b_ok, 1)
                dve.wait_ge(b_ok, base + 4)
                dve.tensor_scalar(pos[:], topi[:, 0:2], float(CB), None, ALU.mult).then_inc(b_ok, 1)
                dve.wait_ge(*m_full_at(seg, b, "POS", 0))
                ps, done = m_bank(seg, b, "POS", 0)
                dve.tensor_copy(posb[:], ps[:, 0:2]).then_inc(done, 1)
                dve.wait_ge(*m_done_at(seg, b, "POS", 0))
                hold()
                for j in range(TOPK):
                    own = slice(SB * j, SB * j + SB)
                    first = dve.value_load(topi[0:1, j:j + 1], min_val=0, max_val=NB - 1)
                    dve.tensor_copy(csk[:, :, own], kT[:, :, bass.ds(first * CB, SB)]).then_inc(b_ok, 1)
                    dve.tensor_scalar(csmask[:, :, own], token[:, :, own], posb[:, j:j + 1], NEG, ALU.is_lt, ALU.mult
                                      ).then_inc(b_ok, 1)
                    dve.tensor_scalar(onehot[:, :, own], token[:, :, own], posb[:, j:j + 1], None, ALU.is_equal
                                      ).then_inc(b_ok, 1)

            def slot(seg, b, s, c, a, prefetch):
                c1, c2, a = c and s < NT, c and s > 0, a and s > 0
                t = s - 1
                ba = b + 1 if seg == "loop" else 0
                Ta = NT * ba + t
                if c1:
                    window_max(b, s, 4)
                if c2:
                    residual(seg, b, t)
                if c1:
                    window_max(b, s, 5)
                if c2:
                    ln_scale(x1[:], mvc, vec, x2n, lnc, lncp, NT * b + t)
                if c1:
                    cs_shift(b, s)
                if a:
                    rope(seg, b, t, "Q")
                if c1:
                    window_max(b, s, 6)
                    window_max(b, s, 7)
                if a:
                    dve.wait_ge(rope_ok, 2 * Ta + 2)
                    rope(seg, b, t, "K")
                if c1:
                    cs_factor(b, s)
                    window_max(b, s, 8)
                    window_max(b, s, 9)
                    window_norm(b, s, 0)
                    window_max(b, s, 10)
                    window_max(b, s, 11)
                if c2:
                    router(seg, b, t, 0)
                if a:
                    gates_soft(seg, b, t, Ta, 0)
                if c1:
                    window_norm(b, s, 1)
                if c2:
                    router(seg, b, t, 1)
                if a:
                    gates_soft(seg, b, t, Ta, 1)
                    sum_q(seg, b, t, Ta)
                if prefetch:
                    ln_a(seg, b, s - 1, Ta + 1, s)
                if c2:
                    final(seg, b, t)

            dve.wait_ge(set_g, SETUP_G + 1)
            dve.memset(ro[:, 16 + E:24], -1.0)
            dve.wait_ge(*m_done_at("pro", 0, "MODT", 0))
            mod_copy(0, mod_a, 0, moda_ok)
            ln_a("pro", 0, -1, 0, 0)
            for s in range(1, NT + 1):
                slot("pro", 0, s, False, True, s < NT)
            select("pro", 0, 0)
            with dve.Fori(0, B - 1) as b:
                mod_copy(b, mod_c, 2, modc_ok)
                mod_copy(b + 1, mod_a, 0, moda_ok)
                for s in range(NT + 1):
                    slot("loop", b, s, True, True, s < NT)
                select("loop", b, b + 1)
            mod_copy(B - 1, mod_c, 2, modc_ok)
            for s in range(NT + 1):
                slot("epi", B - 1, s, True, False, False)



def kernel(L0_attn_x, L0_attn_Wq, L0_attn_Wk, L0_attn_Wv, L0_attn_Wo, L0_attn_bo, L0_attn_wk_comp, L0_attn_wv_comp,
           L0_attn_pe, L0_attn_Wg, L0_attn_bg, L0_ffn_base_W, L0_ffn_base_b, L0_ffn_shared_A, L0_ffn_shared_B,
           L0_ffn_routed_A, L0_ffn_routed_B, L0_ffn_router_W, L0_ffn_router_b, L0_c, L0_wmod):
    import concourse.bacc as bacc
    from concourse.bass_utils import run_bass_kernel_spmd

    f = np.asarray
    arrays = {
        "x": f(L0_attn_x),
        "wqkv": np.concatenate([f(L0_attn_Wq), f(L0_attn_Wk), f(L0_attn_Wv)], axis=1),
        "wo": f(L0_attn_Wo),
        "wbt": f(L0_ffn_base_W).T,
        "wa": np.concatenate([f(L0_ffn_shared_A), f(L0_ffn_routed_A).reshape(E * R, D), f(L0_ffn_router_W)]).T,
        "wb": np.concatenate([f(L0_ffn_shared_B).T, f(L0_ffn_routed_B).transpose(0, 2, 1).reshape(E * R, D),
                              f(L0_ffn_base_b)[None]]),
        "cT": f(L0_c).T,
        "wmod": f(L0_wmod),
        "bo": f(L0_attn_bo),
        "bg": f(L0_attn_bg),
        "rb": f(L0_ffn_router_b),
        "wcomp": np.stack([f(L0_attn_wk_comp), f(L0_attn_wv_comp)]),
        "pe": f(L0_attn_pe),
        "wg": f(L0_attn_Wg),
        "const": constants(),
    }
    arrays = {k: np.ascontiguousarray(a) for k, a in arrays.items()}
    nc = bacc.Bacc("TRN2", target_bir_lowering=False, num_devices=1)
    ins = {k: nc.dram_tensor(f"{k}_in", a.shape, mybir.dt.from_np(a.dtype), kind="ExternalInput").ap()
           for k, a in arrays.items()}
    gscr = nc.dram_tensor("gate_rows", [2, B, D], F32, kind="Internal").ap()
    out = nc.dram_tensor("out", [B, S, D], F32, kind="ExternalOutput").ap()
    program(nc, **ins, gscr=gscr, out=out)
    r = run_bass_kernel_spmd(nc, [{f"{k}_in": a for k, a in arrays.items()}], core_ids=[0])
    return r.results[0]["out"]
```

```python
from contextlib import ExitStack

import numpy as np
import concourse.bass as bass
from concourse import mybir

F32 = mybir.dt.float32
BF16 = mybir.dt.bfloat16
U32 = mybir.dt.uint32
ALU = mybir.AluOpType
ACT = mybir.ActivationFunctionType
AX = mybir.AxisListType

P = 128
B, S, D = 8, 1024, 512
NT = S // P
NC = D // P
H, HD = 16, 32
CB, NB = 16, 64
SB, TOPK = 8, 2
NSEL = SB * TOPK
CS = NSEL + NB
E, R = 6, 16
NZ = R + E * R
SCALE = 1.0 / np.sqrt(HD)
NEG = -1e30
FLOOR = -1e29
EPS = 1e-5

C_ID, C_ROT, C_BLK, C_TOK, C_IO, C_WM, C_CM, C_END = np.cumsum(
    [0, P, NT * 2 * HD, 2 * (NB - 8) + 8, NT * NSEL, 8, 2 * P, NT * NB]).tolist()



def constants():
    p = np.arange(P)
    out = np.zeros((P, C_END), np.float32)
    out[:, C_ID:C_ROT] = np.eye(P)
    k = np.arange(P)
    out[:, C_WM:C_WM + P] = np.where(k[None] > p[:, None], 0, NEG)
    out[:, C_WM + P:C_CM] = np.where(k[None] <= p[:, None], 0, NEG)
    tok = np.arange(NT)[None, :, None] * P + p[:, None, None]
    out[:, C_CM:C_END] = np.where((np.arange(NB) + 1) * CB <= tok, 0, NEG).reshape(P, -1)
    half = HD // 2
    inv = (np.float32(1.0) / np.float32(10000.0) ** (np.arange(half, dtype=np.float32) * np.float32(2.0) / np.float32(HD))).astype(np.float32)
    ang = (np.arange(S, dtype=np.float32)[:, None] * inv[None, :]).astype(np.float32)
    cos, sin = np.cos(ang), np.sin(ang)
    rot = np.concatenate([np.repeat(cos, 2, axis=1), -sin, sin], axis=1)
    out[:, C_ROT:C_BLK] = rot.reshape(NT, P, 2 * HD).transpose(1, 0, 2).reshape(P, -1)
    out[:, C_BLK:C_TOK] = np.arange(2 * (NB - 8) + 8)[None] - (NB - 8) == p[:, None] // CB
    out[:, C_TOK:C_IO] = (tok - np.arange(NSEL) % SB).reshape(P, -1)
    out[:, C_IO:C_WM] = np.arange(8)
    return out


N_FIRST = 3 + P // CB + 7
C_UNITS = 4
SILU_STEPS = 3
GUARD_STEPS = 3 + 3 + 5 + 8
SETUP_V = GUARD_STEPS + 1
SETUP_G = 7
CS_STEPS = 9
G_STEPS = 3
B_STEPS = 5 + 8 * TOPK
R_STEPS = 16

SLOT_ORDER = [("HT", 1), ("Y", 0), ("Q", 1), ("H2T", 0), ("K", 1), ("Z", 0), ("G", 1), ("QT", 0), ("F", 1), ("KT", 0),
              ("ZT", 0), ("V", 0)]
TURN_ORDER = [("HT", 1), ("Y", 0), ("Q", 1), ("H2T", 0), ("K", 1), ("V", 0), ("QT", 1), ("KT", 0), ("G", 1), ("Z", 0),
              ("F", 1), ("ZT", 0)]
C2_UNITS = ("Y", "H2T", "Z", "F", "ZT")


def segment_units(c2, a):
    return [(u, s - 1, bank) for s in range(1, NT + 1) for u, bank in (SLOT_ORDER if s < NT else TURN_ORDER)
            if (c2 if u in C2_UNITS else a)]


SETUP_UNITS = [(f"MOD{i}", 0, i % 2) for i in range(6)] + [("MODT", 0, 0)]
SEGMENTS = {"pro": SETUP_UNITS + segment_units(c2=False, a=True), "loop": segment_units(c2=True, a=True),
            "epi": segment_units(c2=True, a=False)}


def m_unit(seg, b, name, t):
    i, bank = next((i, u[2]) for i, u in enumerate(SEGMENTS[seg]) if u[:2] == (name, t))
    before = sum(u[2] == bank for u in SEGMENTS[seg][:i])
    per = {s: sum(u[2] == bank for u in units) for s, units in SEGMENTS.items()}
    if seg == "pro":
        return bank, before
    return bank, (b if seg == "loop" else B - 1) * per["loop"] + per["pro"] + before


def place(t, r):
    return r if t else (r - 4) % 12


def s_bank(t, r):
    return place(t, r) % 3


def s_before(T, t, r):
    return 4 * T + place(t, r) // 3


def tile_blocks(t):
    slots = [(half, j, i) for half in range(2) for j in range(4) for i in range(2)]
    if t == 0:
        return [(h, w) for w in ("own", "cs") for h in slots]
    return [(h, w) for h in slots for w in ("prev", "own", "cs")]


def t_bank(t, i):
    return i % 3 if t else (0 if i >= 4 else i % 2)


def wn_count(T, slot):
    half, j, i = slot
    return WN_STEPS * T + WN_STEPS // 2 * half + 2 + 2 * j + i + 1


WN_STEPS = 20
ZT_ROUND = 4


def tp_rounds(t):
    return len(tile_blocks(t)) // 4


TP_BATCH = sum(tp_rounds(t) for t in range(NT))


def tp_before(b, t):
    return TP_BATCH * b + sum(tp_rounds(u) for u in range(t))


def program(nc, x, wqkv, wo, wbt, wa, wb, cT, wmod, bo, bg, rb, wcomp, pe, pet, wg, const, gscr, out):
    with ExitStack() as ctx:
        def sb(name, shape, dt=F32):
            return ctx.enter_context(nc.sbuf_tensor(name, shape, dt))

        def sem(name):
            return ctx.enter_context(nc.semaphore(name))

        wqkv_s = sb("wqkv_s", [P, NC, 3 * D])
        wo_s = sb("wo_s", [P, NC, D])
        wbt_s = sb("wbt_s", [P, NC, D])
        wa_s = sb("wa_s", [P, NC, NZ + E])
        wb_s = sb("wb_s", [NZ + 1, D])
        wg_s = sb("wg_s", [P, NC, 3])
        cst = sb("cst", [P, C_WM])
        ident = cst[:, C_ID:C_ROT]
        rot = cst[:, C_ROT:C_BLK].rearrange("p (t n) -> p t n", t=NT)
        token = cst[:, C_TOK:C_IO].rearrange("p (t n) -> p t n", t=NT)
        ident_b = sb("ident_b", [P, P], BF16)
        zero_b = sb("zero_b", [P, 1], BF16)
        wmask = sb("wmask", [P, 2 * P], BF16)
        csmask = sb("csmask", [P, NT, CS], BF16)
        wcol = sb("wcol", [P, 1])
        blkw = sb("blkw", [P, C_TOK - C_BLK])
        wrow = sb("wrow", [P, CB])
        peT = sb("peT", [P, NC, CB])
        pewT = sb("pewT", [P, NC])
        ckn = sb("ckn", [P, NC, NB])
        pe_s = sb("pe_s", [CB, D])
        pew = sb("pew", [CB, NB])
        bo_s = sb("bo_s", [P, D])
        bg_s = sb("bg_s", [P, 3])
        rb_s = sb("rb_s", [P, E])
        ones = sb("ones", [1, P])
        cT_s = sb("cT_s", [P, NC, B])
        silu = sb("silu", [P, 3, NC, B])
        modT = sb("modT", [P, 4, NC, B])
        mod_a = sb("mod_a", [P, 2, NC])
        mod_c = sb("mod_c", [P, 2, NC])
        gbc = sb("gbc", [P, 2, D])
        boga = sb("boga", [P, D])
        xa = sb("xa", [P, 2, D])
        sta = sb("sta", [P, 6])
        mva = sb("mva", [P, 2])
        vea = sb("vea", [P, 2])
        power = sb("power", [P, 1])
        xn = sb("xn", [P, D])
        hT = sb("hT", [P, NC, P])
        ra = sb("ra", [P, D])
        rbf = sb("rbf", [P, D])
        qr = sb("qr", [P, D])
        kr = sb("kr", [P, D])
        qT = sb("qT", [P, NC, S])
        kT = sb("kT", [P, NC, S])
        v_s = sb("v_s", [P, NT, D])
        qsum = sb("qsum", [P, NC, NT])
        gl = sb("gl", [P, 8])
        gates = sb("gates", [P, NT, 3])
        csv = sb("csv", [P, D])
        csk = sb("csk", [P, NC, 4 * CS])
        qs = sb("qs", [P, NC])
        imp = sb("imp", [1, NB])
        top = sb("top", [1, 8])
        topi = sb("topi", [1, 8], U32)
        pos = sb("pos", [1, 2])
        posb = sb("posb", [P, 2])
        held = sb("held", [P, 1])
        onehot = sb("onehot", [P, TOPK, NSEL])
        v_tiles = [ra, rbf]
        tokj = sb("tokj", [P, TOPK, SB])
        css = sb("css", [P, H, CS])
        csp = sb("csp", [P, H, P])
        cm = sb("cm", [P, 2, H])
        cden = sb("cden", [P, 4, H])
        pw = sb("pw", [P, H, 2 * P])
        wmax = sb("wmax", [P, H])
        wden = sb("wden", [P, 3, H])
        pT = sb("pT", [P, 4, 4, P])
        aT = sb("aT", [P, NC, P])
        xc = sb("xc", [P, 2, D])
        t1 = sb("t1", [P, D])
        x1 = sb("x1", [P, D])
        stc = sb("stc", [P, 6])
        mvc = sb("mvc", [P, 2])
        vec = sb("vec", [P, 2])
        x2n = sb("x2n", [P, D])
        h2T = sb("h2T", [P, NC, P])
        zs = sb("zs", [P, NZ + E])
        ro = sb("ro", [P, 48])
        roi = sb("roi", [P, 8], U32)
        zr = sb("zr", [P, NZ + 1])
        zT = sb("zT", [NZ + 1, P])
        o_s = sb("o_s", [P, 2, D])
        modr = pT[0:B].rearrange("p a b n -> p (a b n)").rearrange("p (a n) -> p a n", a=4)
        gr = css[0:B].rearrange("p a n -> p (a n)")[:, 0:2 * D].rearrange("p (a n) -> p a n", a=2)
        gpart = o_s[0:B]
        masks = o_s[:, :, :].rearrange("p a n -> p (a n)")[:, 0:C_END - C_WM]
        wm_ring = pw[:, :, :].rearrange("p a b -> p (a b)").rearrange("p (s c n) -> p s c n", s=2, c=NC)

        ps_s = [ctx.enter_context(nc.psum_tensor(f"ps_s{i}", [P, 512], F32)) for i in range(3)]
        ps_m = [ctx.enter_context(nc.psum_tensor(f"ps_m{i}", [P, 512], F32)) for i in range(2)]
        ps_t = ctx.enter_context(nc.psum_tensor("ps_t", [P, 4, P], F32))
        ps_o = ctx.enter_context(nc.psum_tensor("ps_o", [P, NC, P], F32))
        t_banks = [ps_t] + [ps_s[i][:].rearrange("p (k n) -> p k n", k=4) for i in range(2)]
        ps_c = ctx.enter_context(nc.psum_tensor("ps_c", [P, D], F32))

        d_first = sem("d_first")
        d_w = sem("d_w")
        d_mod = [sem("d_mod0"), sem("d_mod1")]
        d_xa = [sem("d_xa0"), sem("d_xa1")]
        d_xc = [sem("d_xc0"), sem("d_xc1")]
        d_scr = sem("d_scr")
        d_gbc = sem("d_gbc")
        d_out = [sem("d_out0"), sem("d_out1")]
        started = sem("started")
        set_v, set_a, set_g = sem("set_v"), sem("set_a"), sem("set_g")
        m_full = [sem("m_full0"), sem("m_full1")]
        m_done = [sem("m_done0"), sem("m_done1")]
        s_full = [sem(f"s_full{i}") for i in range(3)]
        s_done = [sem(f"s_done{i}") for i in range(3)]
        t_full, t_done = sem("t_full"), sem("t_done")
        pv_done = sem("pv_done")
        o_done = sem("o_done")
        wmax_ok = sem("wmax_ok")
        wn_ok = sem("wn_ok")
        cs_ok = sem("cs_ok")
        cs_exp = sem("cs_exp")
        cs_shift = sem("cs_shift")
        cs_norm = sem("cs_norm")
        lna, lnc = sem("lna"), sem("lnc")
        lnap, lncp = sem("lnap"), sem("lncp")
        rope_ok = sem("rope_ok")
        qsum_ok = sem("qsum_ok")
        g_ok, g_exp = sem("g_ok"), sem("g_exp")
        c_full, c_done = sem("c_full"), sem("c_done")
        ckp_ok = sem("ckp_ok")
        ckr_ok = sem("ckr_ok")
        ck_spread = sem("ck_spread")
        b_ok = sem("b_ok")
        xb_ok = sem("xb_ok")
        y_ok = sem("y_ok")
        r_ok, r_exp = sem("r_ok"), sem("r_exp")
        o_ok = sem("o_ok")
        modc_ok, moda_ok = sem("modc_ok"), sem("moda_ok")
        boga_ok = sem("boga_ok")
        credited = (set_v, set_a, set_g, *m_full, *m_done, *s_full, *s_done, t_full, t_done, pv_done, o_done,
                    wmax_ok, wn_ok, cs_ok, cs_exp, cs_shift, cs_norm, lna, lnc, lnap, lncp, rope_ok, qsum_ok, g_ok, g_exp,
                    c_full, c_done, ckp_ok, ckr_ok, ck_spread, b_ok, xb_ok, y_ok, r_ok, r_exp, o_ok, modc_ok, moda_ok, boga_ok)

        def m_bank(seg, b, name, t):
            bank, _ = m_unit(seg, b, name, t)
            return ps_m[bank], m_done[bank]

        def m_free_at(seg, b, name, t):
            bank, before = m_unit(seg, b, name, t)
            return m_done[bank], before + 1

        def m_full_at(seg, b, name, t):
            bank, before = m_unit(seg, b, name, t)
            return m_full[bank], before + 2

        def m_done_at(seg, b, name, t):
            bank, before = m_unit(seg, b, name, t)
            return m_done[bank], before + 2

        parts = ((0, NSEL), (NSEL, CS))
        block = ctx.enter_context(nc.Block())

        @block.sync
        def _(sp):
            for s in credited:
                sp.sem_inc(s, 1)
            sp.sem_inc(started, 1)
            for s in d_out:
                sp.sem_inc(s, 16)
            sp.dma_start(cT_s[:], cT.rearrange("(c p) b -> p c b", p=P)).then_inc(d_first, 16)
            sp.dma_start(cst[:], const[:, 0:C_WM]).then_inc(d_first, 16)
            sp.dma_start(masks, const[:, C_WM:C_END]).then_inc(d_first, 16)
            n_first = 3

            def load_mod(i):
                if i >= 2:
                    bank, before = m_unit("pro", 0, f"MOD{i - 2}", 0)
                    sp.wait_ge(m_full[bank], before + 2)
                sp.dma_start(wm_ring[:, i % 2], wmod[:, i * D:(i + 1) * D].rearrange("(c p) n -> p c n", p=P)
                             ).then_inc(d_mod[i % 2], 16)

            load_mod(0)
            load_mod(1)
            for i in range(P // CB):
                sp.dma_start(wcol[i * CB:(i + 1) * CB, :], wcomp[1].rearrange("(p a) -> p a", a=1)).then_inc(d_first, 16)
                n_first += 1
            for dst, src in ((pe_s[:], pe), (bo_s[:], bo.partition_broadcast(P)), (bg_s[:], bg.partition_broadcast(P)),
                             (rb_s[:], rb.partition_broadcast(P)),
                             (wg_s[:], wg.rearrange("(c p) n -> p c n", p=P)),
                             (wrow[:], wcomp[0].partition_broadcast(P)),
                             (peT[:], pet.rearrange("(c p) k -> p c k", p=P))):
                sp.dma_start(dst, src).then_inc(d_first, 16)
                n_first += 1
            assert n_first == N_FIRST

            def load_xa(T_former, b, t):
                if T_former is not None:
                    sp.wait_ge(lna, 4 * T_former + 5)
                sp.dma_start(xa[:, t % 2, :], x[b, t * P:(t + 1) * P, :]).then_inc(d_xa[t % 2], 16)

            def load_xc(T, b, t):
                if t > 0:
                    sp.wait_ge(y_ok, T)
                sp.dma_start(xc[:, t % 2, :], x[b, t * P:(t + 1) * P, :]).then_inc(d_xc[t % 2], 16)

            def load_gates(b):
                sp.wait_ge(o_ok, NT * b + 1)
                sp.wait_ge(d_scr, 16 * (2))
                for i in range(2):
                    sp.dma_start(gbc[:, i, :], gscr[i, b, :].partition_broadcast(P)).then_inc(d_gbc, 16)

            load_xa(None, 0, 0)
            load_xa(None, 0, 1)
            sp.dma_start(wqkv_s[:], wqkv.rearrange("(c p) n -> p c n", p=P)).then_inc(d_w, 16)
            for i in range(2, 6):
                load_mod(i)
            sp.dma_start(wo_s[:], wo.rearrange("(c p) n -> p c n", p=P)).then_inc(d_w, 16)
            sp.dma_start(wbt_s[:], wbt.rearrange("(c p) n -> p c n", p=P)).then_inc(d_w, 16)
            sp.dma_start(wa_s[:], wa.rearrange("(c p) n -> p c n", p=P)).then_inc(d_w, 16)
            sp.dma_start(wb_s[:], wb).then_inc(d_w, 16)
            sp.wait_ge(set_v, GUARD_STEPS + 1)
            for i in range(2):
                sp.dma_start(gscr[i], gr[:, i, :]).then_inc(d_scr, 16)
            for t in range(2, NT):
                load_xa(t - 2, 0, t)

            def batch(b, a):
                if a:
                    load_xa(NT * b + NT - 2, b + 1, 0)
                load_gates(b)
                load_xc(NT * b, b, 0)
                for s in range(1, NT + 1):
                    if s < NT:
                        load_xc(NT * b + s, b, s)
                    if a and s < NT:
                        load_xa(NT * b + NT + s - 2, b + 1, s)

            with sp.Fori(0, B - 1) as b:
                batch(b, True)
            batch(B - 1, False)
            for i in range(2):
                sp.wait_ge(d_out[i], 16 * (B * NT // 2 + 1))
            sp.wait_ge(d_scr, 32)

        @block.tensor
        def _(pe_):
            def m_target(seg, b, name, t):
                bank, _ = m_unit(seg, b, name, t)
                return ps_m[bank], m_full[bank]

            pe_.wait_ge(d_first, 16 * (N_FIRST))
            pe_.wait_ge(set_v, SILU_STEPS + 1)
            for i in range(6):
                pe_.wait_ge(*m_free_at("pro", 0, f"MOD{i}", 0))
                ps, full = m_target("pro", 0, f"MOD{i}", 0)
                pe_.wait_ge(d_mod[i % 2], 16 * (i // 2 + 1))
                for c in range(NC):
                    mm = pe_.matmul(ps[0:B, :], silu[:, 2, c, :], wm_ring[:, i % 2, c, :], start=(c == 0), stop=(c == NC - 1))
                mm.then_inc(full, 1)
            pe_.wait_ge(*m_free_at("pro", 0, "MODT", 0))
            ps, full = m_target("pro", 0, "MODT", 0)
            pe_.wait_ge(*m_done_at("pro", 0, "MOD4", 0))
            pe_.wait_ge(*m_done_at("pro", 0, "MOD5", 0))
            for i in range(4):
                for c in range(NC):
                    k = (i * NC + c) * B
                    mm = pe_.transpose(ps[:, k:k + B], modr[:, i, c * P:(c + 1) * P], ident[0:B, 0:B])
            mm.then_inc(full, 1)
            pe_.wait_ge(d_w, 16 * 5)
            pe_.wait_ge(set_v, SETUP_V + 1)

            def transpose_h(seg, b, t, T):
                pe_.wait_ge(*m_free_at(seg, b, "HT", t))
                ps, full = m_target(seg, b, "HT", t)
                pe_.wait_ge(lna, 4 * T + 5)
                for c in range(NC):
                    mm = pe_.transpose(ps[:, c * P:(c + 1) * P], xn[:, c * P:(c + 1) * P], ident)
                mm.then_inc(full, 1)

            def project(seg, b, t, name, col, chunks=range(NC)):
                ps, full = m_target(seg, b, name, t)
                if chunks[0] == 0:
                    pe_.wait_ge(*m_free_at(seg, b, name, t))
                if name == "Q" and chunks[0] == 0:
                    pe_.wait_ge(*m_done_at(seg, b, "HT", t))
                for c in chunks:
                    mm = pe_.matmul(ps[:], hT[:, c, :], wqkv_s[:, c, col * D:(col + 1) * D],
                                    start=(c == 0), stop=(c == NC - 1))
                if c == NC - 1:
                    mm.then_inc(full, 1)

            def transpose_rot(seg, b, t, T, name, src, n):
                pe_.wait_ge(*m_free_at(seg, b, name, t))
                ps, full = m_target(seg, b, name, t)
                pe_.wait_ge(rope_ok, 2 * T + n + 1)
                for c in range(NC):
                    mm = pe_.transpose(ps[:, c * P:(c + 1) * P], src[:, c * P:(c + 1) * P], ident)
                mm.then_inc(full, 1)

            def gate_logits(seg, b, t):
                pe_.wait_ge(*m_free_at(seg, b, "G", t))
                ps, full = m_target(seg, b, "G", t)
                for c in range(NC):
                    mm = pe_.matmul(ps[:, 0:3], hT[:, c, :], wg_s[:, c, :], start=(c == 0), stop=(c == NC - 1))
                mm.then_inc(full, 1)

            def compress(seg, b, t, T, batch_a):
                dst = ps_c[NB:P, :]
                if t == 0:
                    pe_.wait_ge(c_done, C_UNITS * batch_a + 1)
                    pe_.matmul(dst, pew[:, :], pe_s[:, :], start=True, stop=False, skip_group_check=True)
                pe_.wait_ge(*m_done_at(seg, b, "V", t))
                off = NB - 8 - 8 * t
                mm = pe_.matmul(dst, blkw[:, off:off + NB], v_s[:, t, :], start=False, stop=(t == NT - 1),
                                skip_group_check=True)
                if t == NT - 1:
                    mm.then_inc(c_full, 1)

            def importance(ba):
                pe_.wait_ge(c_done, C_UNITS * ba + 2)
                pe_.wait_ge(b_ok, B_STEPS * ba + 3)
                for c in range(NC):
                    mm = pe_.matmul(ps_c[0:1, 0:NB], qs[:, c:c + 1], ckn[:, c, :], start=(c == 0), stop=(c == NC - 1))
                mm.then_inc(c_full, 1)

            def spread_positions(ba):
                pe_.wait_ge(c_done, C_UNITS * ba + 3)
                pe_.wait_ge(b_ok, B_STEPS * ba + 6)
                pe_.matmul(ps_c[:, 0:2], ones[:, :], pos[:, :], start=True, stop=True).then_inc(c_full, 1)

            def select_values(ba):
                pe_.wait_ge(c_done, C_UNITS * ba + 4)
                pe_.wait_ge(b_ok, B_STEPS * ba + B_STEPS + 1)
                for j, v_tile in enumerate(v_tiles):
                    mm = pe_.matmul(ps_c[0:NSEL, :], onehot[:, j, :], v_tile[:, :], start=(j == 0), stop=(j == TOPK - 1))
                mm.then_inc(c_full, 1)

            def score_round(b, t, r):
                T = NT * b + t
                bank = s_bank(t, r)
                pe_.wait_ge(s_done[bank], s_before(T, t, r) + 1)
                if place(t, r) == 0:
                    pe_.wait_ge(t_done, tp_before(b, t) + 1 - (4 if t == 1 else 0))
                if place(t, r) == 9 and t == 0:
                    pe_.wait_ge(t_done, tp_before(b, t) + 5)
                ps = ps_s[bank]
                if r < 4:
                    dst = ps[:, 0:4 * CS]
                    if t == 0 and r == 0:
                        pe_.wait_ge(c_done, C_UNITS * b + 5)
                        pe_.wait_ge(ck_spread, 4 * b + 5)
                    pe_.matmul(dst.rearrange("p (c n) -> p c n", c=4), ident_b[:, :],
                               csmask[:, t, :].unsqueeze(1).broadcast_to([P, 4, CS]),
                               start=True, stop=False, skip_group_check=True)
                    mm = pe_.matmul(dst, qT[:, r, t * P:(t + 1) * P], csk[:, r, :], start=False, stop=True,
                                    skip_group_check=True)
                else:
                    half, j = divmod(r - 4, 4)
                    rows = slice(HD * j, HD * j + HD)
                    k0, n = ((t - 1) * P, 2 * P) if t else (0, P)
                    dst = ps[:, 0:2 * n].rearrange("p (c n) -> p c n", c=2)
                    pe_.matmul(dst, ident_b[:, :], wmask[:, 2 * P - n:].unsqueeze(1).broadcast_to([P, 2, n]),
                               start=True, stop=False, skip_group_check=True)
                    for i in range(2):
                        mm = pe_.matmul(dst[:, i, :], qT[rows, 2 * half + i, t * P:(t + 1) * P],
                                        kT[rows, 2 * half + i, k0:k0 + n], start=False, stop=True, skip_group_check=True)
                mm.then_inc(s_full[bank], 1)

            def head_column(slot):
                half, j, i = slot
                return (half * 4 + j) * 2 + i

            def transpose_round(b, t, i):
                T, n = NT * b + t, tp_before(b, t) + i
                bank = t_bank(t, i)
                former = [k for k in range(i) if t_bank(t, k) == bank]
                if former:
                    pe_.wait_ge(t_done, tp_before(b, t) + former[-1] + 2)
                elif t > 0 and bank > 0:
                    pe_.wait_ge(s_done[bank - 1], s_before(T, t, 8 + bank) + 2)
                elif bank > 0:
                    pe_.wait_ge(s_done[0], s_before(T, t, 10) + 2)
                dst = t_banks[t_bank(t, i)]
                blocks = tile_blocks(t)
                for k in range(4):
                    (half, j, ii), what = blocks[4 * i + k]
                    hw = head_column((half, j, ii))
                    if what == "cs":
                        src = csp[:, 4 * (2 * half + ii) + j, :]
                        if k == 0 or not t or i < 1:
                            pe_.wait_ge(cs_norm, 2 * T + 3)
                    else:
                        src = pw[:, hw, P:2 * P] if what == "own" else pw[:, hw, 0:P]
                        pe_.wait_ge(wn_ok, wn_count(T, (half, j, ii)) + 1)
                    mm = pe_.transpose(dst[:, k, :], src, ident)
                mm.then_inc(t_full, 1)

            def value_round(b, t, i):
                T, n = NT * b + t, tp_before(b, t) + i
                if i == 0:
                    pe_.wait_ge(o_done, T + 1)
                    if t == 0:
                        pe_.matmul(ps_o[:], ident_b[:, :], zero_b[:].unsqueeze(1).broadcast_to([P, NC, P]),
                                   start=True, stop=False, skip_group_check=True)
                pe_.wait_ge(t_done, n + 2)
                blocks = tile_blocks(t)
                for k in range(4):
                    m = 4 * i + k
                    (half, j, ii), what = blocks[m]
                    c = 2 * half + ii
                    cols = slice(P * c + HD * j, P * c + HD * j + HD)
                    src = csv[:, cols] if what == "cs" else v_s[:, t if what == "own" else t - 1, cols]
                    mm = pe_.matmul(ps_o[HD * j:HD * j + HD, c, :], src, pT[:, i % 4, k, :],
                                    start=(what == "prev"), stop=(what == "cs"),
                                    skip_group_check=True)
                mm.then_inc(pv_done, 1)

            def output(seg, b, t, chunks=range(NC)):
                ps, full = m_target(seg, b, "Y", t)
                if chunks[0] == 0:
                    pe_.wait_ge(*m_free_at(seg, b, "Y", t))
                    pe_.wait_ge(o_done, NT * b + t + 2)
                for c in chunks:
                    mm = pe_.matmul(ps[:], aT[:, c, :], wo_s[:, c, :], start=(c == 0), stop=(c == NC - 1))
                if c == NC - 1:
                    mm.then_inc(full, 1)

            def transpose_h2(seg, b, t):
                pe_.wait_ge(*m_free_at(seg, b, "H2T", t))
                ps, full = m_target(seg, b, "H2T", t)
                pe_.wait_ge(lnc, 4 * (NT * b + t) + 5)
                for c in range(NC):
                    mm = pe_.transpose(ps[:, c * P:(c + 1) * P], x2n[:, c * P:(c + 1) * P], ident)
                mm.then_inc(full, 1)

            def lora_down(seg, b, t):
                pe_.wait_ge(*m_free_at(seg, b, "Z", t))
                ps, full = m_target(seg, b, "Z", t)
                pe_.wait_ge(*m_done_at(seg, b, "H2T", t))
                for c in range(NC):
                    mm = pe_.matmul(ps[:, 0:NZ + E], h2T[:, c, :], wa_s[:, c, :], start=(c == 0), stop=(c == NC - 1))
                mm.then_inc(full, 1)

            def transpose_z(seg, b, t):
                pe_.wait_ge(*m_free_at(seg, b, "ZT", t))
                ps, full = m_target(seg, b, "ZT", t)
                pe_.wait_ge(r_ok, R_STEPS * (NT * b + t + 1) + 1)
                pe_.transpose(ps[0:NZ + 1, 0:P], zr[:, :], ident).then_inc(full, 1)

            def feed(seg, b, t, chunks=range(NC + 1)):
                ps, full = m_target(seg, b, "F", t)
                if chunks[0] == 0:
                    pe_.wait_ge(*m_free_at(seg, b, "F", t))
                for c in chunks:
                    if c < NC:
                        pe_.matmul(ps[:], h2T[:, c, :], wbt_s[:, c, :], start=(c == 0), stop=False)
                    else:
                        pe_.wait_ge(*m_done_at(seg, b, "ZT", t))
                        pe_.matmul(ps[:], zT[:, :], wb_s[:, :], start=False, stop=True).then_inc(full, 1)

            def slot(seg, b, s):
                c, a, t = seg != "pro", seg != "epi", s - 1
                ba = b + 1 if seg == "loop" else 0
                Ta = NT * ba + t
                if c:
                    score_round(b, s, 0)
                if c and s == 1:
                    score_round(b, s, 1)
                    score_round(b, s, 2)
                if a:
                    transpose_h(seg, b, t, Ta)
                if c and s == 1:
                    score_round(b, s, 3)
                    score_round(b, s, 4)
                if c and s > 1:
                    score_round(b, s, 1)
                    output(seg, b, t, [0])
                    score_round(b, s, 2)
                    output(seg, b, t, [1])
                    score_round(b, s, 3)
                    score_round(b, s, 4)
                    output(seg, b, t, [2, 3])
                if a and s > 1:
                    compress(seg, b, t - 1, Ta - 1, ba)
                if c:
                    score_round(b, s, 5)
                if c and s == 1:
                    if a:
                        project(seg, b, t, "Q", 0, [0, 1])
                    for i in range(4, 8):
                        transpose_round(b, 0, i)
                        if a and i < 6:
                            project(seg, b, t, "Q", 0, [i - 2])
                        if i == 6:
                            score_round(b, s, 6)
                        if a and i == 7:
                            project(seg, b, t, "K", 1, [0])
                        value_round(b, 0, i)
                    if a:
                        project(seg, b, t, "K", 1, [1])
                    output(seg, b, t)
                if a and not (c and s == 1):
                    project(seg, b, t, "Q", 0)
                if c:
                    if s > 1:
                        score_round(b, s, 6)
                    score_round(b, s, 7)
                if c and s > 1:
                    transpose_h2(seg, b, t)
                if a:
                    project(seg, b, t, "K", 1, range(2 if s == 1 and c else 0, NC))
                if c and s == 1:
                    transpose_h2(seg, b, t)
                if c:
                    score_round(b, s, 8)
                    score_round(b, s, 9)
                    lora_down(seg, b, t)
                    score_round(b, s, 10)
                if a:
                    gate_logits(seg, b, t)
                    transpose_rot(seg, b, t, Ta, "QT", qr, 1)
                if c:
                    score_round(b, s, 11)
                    feed(seg, b, t, [0])
                if a:
                    transpose_rot(seg, b, t, Ta, "KT", kr, 2)
                if c:
                    n = tp_rounds(s)
                    feed(seg, b, t, [1, 2])
                    transpose_round(b, s, 0)
                    transpose_round(b, s, 1)
                    transpose_round(b, s, 2)
                    for i in range(n):
                        if i == 1:
                            feed(seg, b, t, [3])
                        if i == ZT_ROUND:
                            transpose_z(seg, b, t)
                        if i == ZT_ROUND + 2:
                            feed(seg, b, t, [NC])
                        if a and n - 1 - NC <= i < n - 1:
                            project(seg, b, t, "V", 2, [i - (n - 1 - NC)])
                        value_round(b, s, i)
                        if i + 3 < n:
                            transpose_round(b, s, i + 3)
                elif a:
                    project(seg, b, t, "V", 2)

            def turn(seg, b):
                c2, t = seg != "pro", NT - 1
                ba = b + 1 if seg == "loop" else 0
                Ta = NT * ba + t
                score_round(ba, 0, 4)
                transpose_h(seg, b, t, Ta)
                score_round(ba, 0, 5)
                compress(seg, b, t - 1, Ta - 1, ba)
                if c2:
                    output(seg, b, t)
                project(seg, b, t, "Q", 0)
                score_round(ba, 0, 6)
                project(seg, b, t, "K", 1, [0])
                if c2:
                    transpose_h2(seg, b, t)
                project(seg, b, t, "K", 1, [1, 2, 3])
                score_round(ba, 0, 7)
                project(seg, b, t, "V", 2)
                score_round(ba, 0, 8)
                transpose_rot(seg, b, t, Ta, "QT", qr, 1)
                score_round(ba, 0, 9)
                transpose_rot(seg, b, t, Ta, "KT", kr, 2)
                compress(seg, b, t, Ta, ba)
                gate_logits(seg, b, t)
                score_round(ba, 0, 10)
                score_round(ba, 0, 11)
                if c2:
                    lora_down(seg, b, t)
                importance(ba)
                transpose_round(ba, 0, 0)
                if c2:
                    feed(seg, b, t, [0])
                transpose_round(ba, 0, 1)
                value_round(ba, 0, 0)
                spread_positions(ba)
                if c2:
                    feed(seg, b, t, [1])
                transpose_round(ba, 0, 2)
                value_round(ba, 0, 1)
                transpose_round(ba, 0, 3)
                value_round(ba, 0, 2)
                value_round(ba, 0, 3)
                select_values(ba)
                if c2:
                    feed(seg, b, t, [2])
                score_round(ba, 0, 0)
                score_round(ba, 0, 1)
                if c2:
                    feed(seg, b, t, [3])
                    transpose_z(seg, b, t)
                score_round(ba, 0, 2)
                score_round(ba, 0, 3)
                if c2:
                    feed(seg, b, t, [NC])

            def last(seg, b):
                t = NT - 1
                output(seg, b, t)
                transpose_h2(seg, b, t)
                lora_down(seg, b, t)
                feed(seg, b, t, range(NC))
                transpose_z(seg, b, t)
                feed(seg, b, t, [NC])

            for s in range(1, NT):
                slot("pro", 0, s)
            turn("pro", 0)
            with pe_.Fori(0, B - 1) as b:
                for s in range(1, NT):
                    slot("loop", b, s)
                turn("loop", b)
            for s in range(1, NT):
                slot("epi", B - 1, s)
            last("epi", B - 1)

        @block.scalar
        def _(act):
            act.wait_ge(d_first, 16 * (N_FIRST))
            act.activation(silu[:, 0], cT_s[:], ACT.Exp, scale=-1.0).then_inc(set_a, 1)
            for k, i in enumerate((0, 1, 3, 4)):
                act.wait_ge(*m_full_at("pro", 0, f"MOD{i}", 0))
                ps, done = m_bank("pro", 0, f"MOD{i}", 0)
                act.activation(modr[:, k, :], ps[0:B, :], ACT.Copy).then_inc(done, 1)

            def h_scaled(seg, b, t, name, dst, mod, mod_sem, mod_count):
                act.wait_ge(*m_full_at(seg, b, name, t))
                ps, done = m_bank(seg, b, name, t)
                if t == 0:
                    act.wait_ge(mod_sem, mod_count + 1)
                for c in range(NC):
                    ins = act.activation(dst[:, c, :], ps[:, c * P:(c + 1) * P], ACT.Identity,
                                         scale=mod[:, 1, c:c + 1], bias=mod[:, 0, c:c + 1])
                ins.then_inc(done, 1)

            def copy_v(seg, b, t):
                act.wait_ge(*m_full_at(seg, b, "V", t))
                ps, done = m_bank(seg, b, "V", t)
                act.activation(v_s[:, t, :], ps[:], ACT.Copy).then_inc(done, 1)

            def copy_qT(seg, b, t):
                act.wait_ge(*m_full_at(seg, b, "QT", t))
                ps, done = m_bank(seg, b, "QT", t)
                act.activation(qT[:, :, t * P:(t + 1) * P], ps[:].rearrange("p (c n) -> p c n", c=NC), ACT.Copy,
                               scale=float(SCALE)).then_inc(done, 1)

            def copy_kT(seg, b, t):
                act.wait_ge(*m_full_at(seg, b, "KT", t))
                ps, done = m_bank(seg, b, "KT", t)
                act.activation(kT[:, :, t * P:(t + 1) * P], ps[:].rearrange("p (c n) -> p c n", c=NC), ACT.Copy
                               ).then_inc(done, 1)

            def gate_exp(Ta):
                act.wait_ge(g_ok, G_STEPS * Ta + 2)
                act.activation(gl[:, 3:6], gl[:, 0:3], ACT.Exp, bias=gl[:, 6:7], accum_out=gl[:, 7:8]).then_inc(g_exp, 1)

            def cs_copy(b, t, r):
                T = NT * b + t
                bank = s_bank(t, r)
                act.wait_ge(s_full[bank], s_before(T, t, r) + 2)
                if r == 0:
                    act.wait_ge(cs_exp, 2 * T + 1)
                act.activation(css[:, 4 * r:4 * r + 4, :], ps_s[bank][:, 0:4 * CS].rearrange("p (c n) -> p c n", c=4),
                               ACT.Copy).then_inc(s_done[bank], 1)

            def cs_exps(b, t):
                T = NT * b + t
                act.wait_ge(cs_shift, 2 * T + 3)
                act.wait_ge(t_full, tp_before(b, t) + 1)
                act.activation(csp[:, :, 0:NSEL], css[:, :, 0:NSEL], ACT.Exp).then_inc(cs_exp, 1)
                act.activation(csp[:, :, P - NB:P], css[:, :, NSEL:CS], ACT.Exp).then_inc(cs_exp, 1)

            def window_exp(b, t, r):
                T = NT * b + t
                act.wait_ge(wmax_ok, 8 * T + r - 2)
                if r == 4:
                    act.wait_ge(t_full, tp_before(b, t) + 1 - (4 if t == 1 else 0))
                    act.wait_ge(wn_ok, WN_STEPS * T + 1)
                n = 2 * P if t else P
                for i in range(2):
                    hw = 2 * (r - 4) + i
                    ins = act.activation(pw[:, hw, 2 * P - n:2 * P], ps_s[s_bank(t, r)][:, i * n:(i + 1) * n], ACT.Exp,
                                         bias=wmax[:, hw:hw + 1], accum_out=wden[:, 0, hw:hw + 1])
                ins.then_inc(s_done[s_bank(t, r)], 1)

            def copy_z(seg, b, t):
                act.wait_ge(*m_full_at(seg, b, "Z", t))
                ps, done = m_bank(seg, b, "Z", t)
                act.wait_ge(r_ok, R_STEPS * (NT * b + t) + 1)
                act.activation(zs[:, :], ps[:, 0:NZ + E], ACT.Copy).then_inc(done, 1)

            def router_exp(b, t):
                T = NT * b + t
                act.wait_ge(r_ok, R_STEPS * T + 3)
                act.activation(ro[:, 8:14], ro[:, 0:6], ACT.Exp, bias=ro[:, 6:7], accum_out=ro[:, 7:8]).then_inc(r_exp, 1)

            def copy_zT(seg, b, t):
                act.wait_ge(*m_full_at(seg, b, "ZT", t))
                ps, done = m_bank(seg, b, "ZT", t)
                act.activation(zT[:, :], ps[0:NZ + 1, 0:P], ACT.Copy).then_inc(done, 1)

            def probs_copy(b, t, i):
                n = tp_before(b, t) + i
                act.wait_ge(t_full, n + 2)
                if i >= 4:
                    act.wait_ge(pv_done, n - 2)
                act.activation(pT[:, i % 4], t_banks[t_bank(t, i)][:], ACT.Copy).then_inc(t_done, 1)

            def copy_out(b, t):
                act.wait_ge(pv_done, tp_before(b, t) + tp_rounds(t) + 1)
                act.activation(aT[:], ps_o[:], ACT.Copy).then_inc(o_done, 1)

            def copy_cv(ba):
                act.wait_ge(c_full, C_UNITS * ba + 2)
                act.activation(csv[P - NB:P, :], ps_c[NB:P, :], ACT.Copy).then_inc(c_done, 1)

            def spread_ck(ba):
                act.wait_ge(b_ok, B_STEPS * ba + 3)
                for j in range(4):
                    rows = slice(HD * j, HD * j + HD)
                    act.activation(csk[rows, :, CS * j + NSEL:CS * j + CS], ckn[rows, :, :], ACT.Copy).then_inc(ck_spread, 1)

            def copy_selv(ba):
                act.wait_ge(c_full, C_UNITS * ba + 5)
                act.activation(csv[0:NSEL, :], ps_c[0:NSEL, :], ACT.Copy).then_inc(c_done, 1)

            def store(b, t):
                act.wait_ge(o_ok, NT * b + t + 2)
                act.dma_start(out[b, t * P:(t + 1) * P, :], o_s[:, t % 2, :]).then_inc(d_out[t % 2], 16)

            def slot(seg, b, s):
                c, a, t = seg != "pro", seg != "epi", s - 1
                ba = b + 1 if seg == "loop" else 0
                Ta = NT * ba + t
                if c:
                    for r in range(4):
                        cs_copy(b, s, r)
                if a:
                    h_scaled(seg, b, t, "HT", hT, mod_a, moda_ok, ba + 1)
                if c:
                    window_exp(b, s, 4)
                    if s == 1:
                        for i in range(4, 8):
                            probs_copy(b, 0, i)
                        copy_out(b, 0)
                        window_exp(b, s, 5)
                        cs_exps(b, s)
                        window_exp(b, s, 6)
                        h_scaled(seg, b, t, "H2T", h2T, mod_c, modc_ok, b + 1)
                    else:
                        cs_exps(b, s)
                        window_exp(b, s, 5)
                        h_scaled(seg, b, t, "H2T", h2T, mod_c, modc_ok, b + 1)
                        window_exp(b, s, 6)
                    window_exp(b, s, 7)
                    window_exp(b, s, 8)
                    window_exp(b, s, 9)
                    copy_z(seg, b, t)
                    window_exp(b, s, 10)
                if a:
                    copy_qT(seg, b, t)
                if c:
                    window_exp(b, s, 11)
                    router_exp(b, t)
                if a:
                    copy_kT(seg, b, t)
                    gate_exp(Ta)
                if c:
                    for i in range(tp_rounds(s)):
                        probs_copy(b, s, i)
                        if i == ZT_ROUND:
                            copy_zT(seg, b, t)
                    copy_out(b, s)
                if a:
                    copy_v(seg, b, t)
                if c:
                    store(b, t)

            def turn(seg, b):
                c2, t = seg != "pro", NT - 1
                ba = b + 1 if seg == "loop" else 0
                Ta = NT * ba + t
                h_scaled(seg, b, t, "HT", hT, mod_a, moda_ok, ba + 1)
                for r in range(4, 7):
                    window_exp(ba, 0, r)
                if c2:
                    h_scaled(seg, b, t, "H2T", h2T, mod_c, modc_ok, b + 1)
                window_exp(ba, 0, 7)
                copy_v(seg, b, t)
                window_exp(ba, 0, 8)
                copy_qT(seg, b, t)
                window_exp(ba, 0, 9)
                copy_kT(seg, b, t)
                copy_cv(ba)
                window_exp(ba, 0, 10)
                window_exp(ba, 0, 11)
                if c2:
                    copy_z(seg, b, t)
                    router_exp(b, t)
                gate_exp(Ta)
                for i in range(4):
                    probs_copy(ba, 0, i)
                spread_ck(ba)
                copy_selv(ba)
                for r in range(4):
                    cs_copy(ba, 0, r)
                if c2:
                    copy_zT(seg, b, t)
                cs_exps(ba, 0)
                if c2:
                    store(b, t)

            def last(seg, b):
                t = NT - 1
                h_scaled(seg, b, t, "H2T", h2T, mod_c, modc_ok, b + 1)
                copy_z(seg, b, t)
                router_exp(b, t)
                copy_zT(seg, b, t)
                store(b, t)

            act.wait_ge(*m_full_at("pro", 0, "MODT", 0))
            ps, done = m_bank("pro", 0, "MODT", 0)
            v = ps[:, 0:4 * NC * B].rearrange("p (m c b) -> p m c b", m=4, c=NC)
            for i in range(4):
                ins = act.activation(modT[:, i], v[:, i], ACT.Copy, bias=float(i % 2))
            ins.then_inc(done, 1)
            act.wait_ge(d_scr, 32)
            for s in range(1, NT):
                slot("pro", 0, s)
            turn("pro", 0)
            with act.Fori(0, B - 1) as b:
                for s in range(1, NT):
                    slot("loop", b, s)
                turn("loop", b)
            for s in range(1, NT):
                slot("epi", B - 1, s)
            last("epi", B - 1)

        @block.gpsimd
        def _(gp):
            gp.memset(power[:], -0.5).then_inc(set_g, 1)
            gp.memset(csp[:], 0.0).then_inc(set_g, 1)
            gp.memset(csv[:], 0.0).then_inc(set_g, 1)
            gp.memset(onehot[:], 0.0).then_inc(set_g, 1)
            gp.memset(csk[:], 0.0).then_inc(set_g, 1)
            gp.memset(ones[:], 1.0).then_inc(set_g, 1)
            gp.memset(zr[:], 1.0).then_inc(set_g, 1)
            gp.wait_ge(set_g, SETUP_G + 1)

            def deviation_a(Ta):
                gp.wait_ge(lna, 4 * Ta + 4)
                gp.tensor_tensor(vea[:, 1:2], vea[:, 0:1], power[:], ALU.pow).then_inc(lnap, 1)

            def deviation_c(T):
                gp.wait_ge(lnc, 4 * T + 4)
                gp.tensor_tensor(vec[:, 1:2], vec[:, 0:1], power[:], ALU.pow).then_inc(lncp, 1)

            def rotate(seg, b, t, Ta, name, dst):
                gp.wait_ge(*m_done_at(seg, b, name, t))
                gp.tensor_tensor(dst[:], ra[:], rbf[:], ALU.add).then_inc(rope_ok, 1)

            def cs_subtract(b, t):
                T = NT * b + t
                gp.wait_ge(cs_ok, CS_STEPS * T + 4)
                for w, (lo, hi) in enumerate(parts):
                    v = css[:, :, lo:hi]
                    gp.tensor_tensor(v, v, cm[:, w, :].unsqueeze(2).broadcast_to([P, H, hi - lo]), ALU.subtract
                                     ).then_inc(cs_shift, 1)

            def cs_normalise(b, t):
                T = NT * b + t
                gp.wait_ge(cs_ok, CS_STEPS * T + CS_STEPS + 1)
                for lo, n, w in ((0, NSEL, 2), (P - NB, NB, 3)):
                    v = csp[:, :, lo:lo + n]
                    gp.tensor_tensor(v, v, cden[:, w, :].unsqueeze(2).broadcast_to([P, H, n]), ALU.mult
                                     ).then_inc(cs_norm, 1)

            def bias_gate(b):
                gp.wait_ge(d_gbc, 16 * (2 * b + 2))
                gp.tensor_tensor(boga[:], bo_s[:], gbc[:, 0, :], ALU.mult).then_inc(boga_ok, 1)
                gp.wait_ge(boga_ok, b + 2)

            def residual_in(b, t):
                gp.wait_ge(d_xc[t % 2], 16 * (4 * b + t // 2 + 1))
                gp.tensor_tensor(xc[:, t % 2, :], xc[:, t % 2, :], boga[:], ALU.add).then_inc(xb_ok, 1)

            def weigh_keys(seg, b, t, Ta):
                gp.wait_ge(*m_done_at(seg, b, "KT", t))
                gp.tensor_tensor(ra[:].rearrange("p (c m k) -> p c m k", c=NC, k=CB),
                                 kT[:, :, t * P:(t + 1) * P].rearrange("p c (m k) -> p c m k", k=CB),
                                 wrow[:].unsqueeze(1).unsqueeze(1).broadcast_to([P, NC, P // CB, CB]), ALU.mult
                                 ).then_inc(ckp_ok, 1)

            def slot(seg, b, s, c1, prefetch):
                c2, a, t = seg != "pro", seg != "epi", s - 1
                ba = b + 1 if seg == "loop" else 0
                Ta = NT * ba + t
                if s == 1 and seg == "loop":
                    deviation_a(Ta)
                if s == 1 and seg != "pro":
                    cs_normalise(b, 0)
                    bias_gate(b)
                if c2:
                    residual_in(b, t)
                if c1 and s < NT:
                    cs_subtract(b, s)
                if a and s == 1:
                    rotate(seg, b, t, Ta, "Q", qr)
                if c2:
                    deviation_c(NT * b + t)
                if a:
                    if s > 1:
                        rotate(seg, b, t, Ta, "Q", qr)
                    rotate(seg, b, t, Ta, "K", kr)
                if c1 and s < NT:
                    cs_normalise(b, s)
                if a:
                    weigh_keys(seg, b, t, Ta)
                if c1 and s == NT:
                    cs_subtract(ba, 0)
                if prefetch:
                    deviation_a(Ta + 1)

            gp.wait_ge(d_first, 16 * (N_FIRST))
            deviation_a(0)
            for s in range(1, NT + 1):
                slot("pro", 0, s, s == NT, s < NT)
            with gp.Fori(0, B - 1) as b:
                for s in range(1, NT + 1):
                    slot("loop", b, s, True, s < NT)
            for s in range(1, NT + 1):
                slot("epi", B - 1, s, s < NT, False)

        @block.vector
        def _(dve):
            steps = [0]

            def setup(ins):
                steps[0] += 1
                ins.then_inc(set_v, 1)
                dve.wait_ge(set_v, steps[0] + 1)

            dve.wait_ge(d_first, 16 * (N_FIRST))
            dve.wait_ge(set_a, 2)
            setup(dve.tensor_scalar(silu[:, 0], silu[:, 0], 1.0, None, ALU.add))
            setup(dve.reciprocal(silu[:, 1], silu[:, 0]))
            setup(dve.tensor_tensor(silu[:, 2], cT_s[:], silu[:, 1], ALU.mult))
            assert steps[0] == SILU_STEPS
            setup(dve.tensor_copy(ident_b[:], ident))
            setup(dve.tensor_copy(wmask[:], masks[:, 0:2 * P]))
            setup(dve.tensor_copy(csmask[:, :, NSEL:CS], masks[:, 2 * P:].rearrange("p (t n) -> p t n", t=NT)))
            setup(dve.tensor_scalar(blkw[:], cst[:, C_BLK:C_TOK], wcol[:], None, ALU.mult))
            setup(dve.memset(pew[:], 1.0))
            setup(dve.tensor_scalar(pew[:], pew[:], wcol[0:CB, :], None, ALU.mult))
            setup(dve.tensor_tensor(peT[:], peT[:], wrow[:].unsqueeze(1).broadcast_to([P, NC, CB]), ALU.mult))
            setup(dve.tensor_reduce(pewT[:], peT[:], AX.X, ALU.add))
            for k, i in enumerate((2, 5)):
                dve.wait_ge(*m_full_at("pro", 0, f"MOD{i}", 0))
                ps, done = m_bank("pro", 0, f"MOD{i}", 0)
                dve.tensor_copy(gpart[:, 0, :], ps[0:B, :]).then_inc(done, 1)
                dve.wait_ge(*m_done_at("pro", 0, f"MOD{i}", 0))
                setup(dve.tensor_scalar(gpart[:, 1, :], gpart[:, 0, :], 0.0, 2.0, ALU.is_ge, ALU.mult))
                setup(dve.tensor_scalar(gpart[:, 1, :], gpart[:, 1, :], -1.0, None, ALU.add))
                setup(dve.scalar_tensor_tensor(out=gpart[:, 0, :], in0=gpart[:, 0, :], scalar=-1.0, in1=gpart[:, 0, :],
                                               op0=ALU.mult, op1=ALU.max))
                setup(dve.scalar_tensor_tensor(out=gr[:, k, :], in0=gpart[:, 0, :], scalar=0.25, in1=gpart[:, 1, :],
                                               op0=ALU.max, op1=ALU.mult))
            setup(dve.memset(zero_b[:], 0.0))
            assert steps[0] == SETUP_V

            def hold():
                dve.memset(held[:], 0.0)

            def ln_stats(x_, st, mv, ve, s, T):
                dve.bn_stats(st[:], x_).then_inc(s, 1)
                dve.wait_ge(s, 4 * T + 2)
                hold()
                dve.bn_aggr(mv[:], st[:]).then_inc(s, 1)
                dve.wait_ge(s, 4 * T + 3)
                dve.tensor_scalar(ve[:, 0:1], mv[:, 1:2], EPS, None, ALU.add).then_inc(s, 1)

            def ln_scale(x_, mv, ve, dst, s, sp_, T):
                dve.wait_ge(sp_, T + 2)
                dve.tensor_scalar(dst[:], x_, mv[:, 0:1], ve[:, 1:2], ALU.subtract, ALU.mult).then_inc(s, 1)

            def ln_a(seg, b, t, Ta, tile_a):
                dve.wait_ge(d_xa[tile_a % 2], 16 * (4 * (b + 1 if seg == "loop" else 0) + tile_a // 2 + 1))
                if tile_a > 0:
                    dve.wait_ge(*m_done_at(seg, b, "HT", tile_a - 1))
                ln_stats(xa[:, tile_a % 2, :], sta, mva, vea, lna, Ta)
                ln_scale(xa[:, tile_a % 2, :], mva, vea, xn, lna, lnap, Ta)

            def mod_copy(b, dst, first, ok):
                dve.tensor_copy(dst[:], modT[:, first:first + 2, :, b]).then_inc(ok, 1)

            def rope(seg, b, t, name):
                dve.wait_ge(*m_full_at(seg, b, name, t))
                ps, done = m_bank(seg, b, name, t)
                q3 = ps[:].rearrange("p (h n) -> p h n", h=H)
                q4 = ps[:].rearrange("p (h n e) -> p h n e", h=H, e=2)
                r4 = rbf[:].rearrange("p (h n e) -> p h n e", h=H, e=2)
                dve.tensor_tensor(ra[:].rearrange("p (h n) -> p h n", h=H), q3,
                                  rot[:, t, 0:HD].unsqueeze(1).broadcast_to([P, H, HD]), ALU.mult)
                for e in range(2):
                    half = HD // 2
                    w = rot[:, t, HD + e * half:HD + (e + 1) * half].unsqueeze(1).broadcast_to([P, H, half])
                    ins = dve.tensor_tensor(r4[:, :, :, e], q4[:, :, :, 1 - e], w, ALU.mult)
                ins.then_inc(done, 1)

            def sum_q(seg, b, t, Ta):
                dve.wait_ge(*m_done_at(seg, b, "QT", t))
                dve.tensor_reduce(qsum[:, :, t], qT[:, :, t * P:(t + 1) * P], AX.X, ALU.add).then_inc(qsum_ok, 1)

            def gates_soft(seg, b, t, Ta, part):
                if part == 1:
                    dve.wait_ge(g_exp, Ta + 2)
                    dve.reciprocal(gl[:, 7:8], gl[:, 7:8]).then_inc(g_ok, 1)
                    dve.wait_ge(g_ok, G_STEPS * Ta + 3)
                    dve.tensor_scalar(gates[:, t, :], gl[:, 3:6], gl[:, 7:8], None, ALU.mult).then_inc(g_ok, 1)
                    return
                dve.wait_ge(*m_full_at(seg, b, "G", t))
                ps, done = m_bank(seg, b, "G", t)
                dve.tensor_tensor(gl[:, 0:3], ps[:, 0:3], bg_s[:], ALU.add).then_inc(done, 1)
                dve.wait_ge(*m_done_at(seg, b, "G", t))
                dve.tensor_reduce(gl[:, 6:7], gl[:, 0:3], AX.X, ALU.max, negate=True).then_inc(g_ok, 1)

            def window_max(b, t, r):
                T = NT * b + t
                dve.wait_ge(s_full[s_bank(t, r)], s_before(T, t, r) + 2)
                if r == 4:
                    dve.wait_ge(s_done[11 % 3], 4 * T + 1)
                n = 2 * P if t else P
                dve.tensor_reduce(wmax[:, 2 * (r - 4):2 * (r - 3)],
                                  ps_s[s_bank(t, r)][:, 0:2 * n].rearrange("p (c n) -> p c n", c=2), AX.X, ALU.max,
                                  negate=True).then_inc(wmax_ok, 1)

            def window_norm(b, t, half):
                T = NT * b + t
                h0 = 8 * half
                r = 4 + 4 * half + 3
                dve.wait_ge(s_done[s_bank(t, r)], s_before(T, t, r) + 2)
                base = WN_STEPS * T + WN_STEPS // 2 * half
                dve.reciprocal(wden[:, 1, h0:h0 + 8], wden[:, 0, h0:h0 + 8]).then_inc(wn_ok, 1)
                dve.wait_ge(wn_ok, base + 2)
                dve.tensor_scalar(wden[:, 2, h0:h0 + 8], wden[:, 1, h0:h0 + 8], gates[:, t, 2:3], None, ALU.mult
                                  ).then_inc(wn_ok, 1)
                dve.wait_ge(wn_ok, base + 3)
                lo = 0 if t else P
                for h in range(h0, h0 + 8):
                    dve.tensor_scalar(pw[:, h, lo:2 * P], pw[:, h, lo:2 * P], wden[:, 2, h:h + 1], None, ALU.mult
                                      ).then_inc(wn_ok, 1)

            def cs_max(b, t):
                T = NT * b + t
                base = CS_STEPS * T
                dve.wait_ge(s_done[s_bank(t, 3)], s_before(T, t, 3) + 2)
                for w, (lo, hi) in enumerate(parts):
                    dve.tensor_reduce(cm[:, w, :], css[:, :, lo:hi], AX.X, ALU.max).then_inc(cs_ok, 1)
                dve.wait_ge(cs_ok, base + 3)
                dve.tensor_scalar(cm[:], cm[:], FLOOR, None, ALU.max).then_inc(cs_ok, 1)

            def cs_factor(b, t):
                T = NT * b + t
                base = CS_STEPS * T
                dve.wait_ge(cs_exp, 2 * T + 3)
                for w, (lo, n) in enumerate(((0, NSEL), (P - NB, NB))):
                    dve.tensor_reduce(cden[:, w, :], csp[:, :, lo:lo + n], AX.X, ALU.add).then_inc(cs_ok, 1)
                dve.wait_ge(cs_ok, base + 6)
                dve.tensor_scalar(cden[:, 0:2, :], cden[:, 0:2, :], 1e-30, None, ALU.max).then_inc(cs_ok, 1)
                dve.wait_ge(cs_ok, base + 7)
                dve.reciprocal(cden[:, 2:4, :], cden[:, 0:2, :]).then_inc(cs_ok, 1)
                dve.wait_ge(cs_ok, base + 8)
                for w, g in ((2, 1), (3, 0)):
                    dve.tensor_scalar(cden[:, w, :], cden[:, w, :], gates[:, t, g:g + 1], None, ALU.mult).then_inc(cs_ok, 1)

            def residual(seg, b, t):
                T = NT * b + t
                dve.wait_ge(*m_full_at(seg, b, "Y", t))
                ps, done = m_bank(seg, b, "Y", t)
                if t == 0:
                    dve.wait_ge(d_gbc, 16 * (2 * b + 2))
                dve.wait_ge(o_ok, T + 1)
                dve.tensor_tensor(t1[:], ps[:], gbc[:, 0, :], ALU.mult).then_inc(done, 1)
                dve.wait_ge(*m_done_at(seg, b, "Y", t))
                dve.wait_ge(xb_ok, T + 2)
                dve.tensor_tensor(x1[:], t1[:], xc[:, t % 2, :], ALU.add).then_inc(y_ok, 1)
                dve.wait_ge(y_ok, T + 2)
                ln_stats(x1[:], stc, mvc, vec, lnc, T)

            def router(seg, b, t, part):
                T = NT * b + t
                base = R_STEPS * T
                n = [0 if part == 0 else 2]

                def step(ins):
                    n[0] += 1
                    ins.then_inc(r_ok, 1)
                    if n[0] != 2:
                        dve.wait_ge(r_ok, base + n[0] + 1)

                if part == 0:
                    dve.wait_ge(*m_done_at(seg, b, "Z", t))
                    step(dve.tensor_tensor(ro[:, 0:E], zs[:, NZ:NZ + E], rb_s[:], ALU.add))
                    step(dve.tensor_reduce(ro[:, 6:7], ro[:, 0:E], AX.X, ALU.max, negate=True))
                    return
                dve.wait_ge(r_exp, T + 2)
                step(dve.reciprocal(ro[:, 15:16], ro[:, 7:8]))
                step(dve.tensor_scalar(ro[:, 16:16 + E], ro[:, 8:8 + E], ro[:, 15:16], None, ALU.mult))
                hold()
                step(dve.max(ro[:, 24:32], ro[:, 16:24]))
                hold()
                step(dve.max_index(roi[:], ro[:, 24:32], ro[:, 16:24]))
                step(dve.tensor_copy(ro[:, 40:42], roi[:, 0:2]))
                step(dve.tensor_scalar(ro[:, 32:32 + E], cst[:, C_IO:C_IO + E], ro[:, 40:41], None, ALU.is_equal))
                step(dve.scalar_tensor_tensor(out=ro[:, 32:32 + E], in0=cst[:, C_IO:C_IO + E], scalar=ro[:, 41:42],
                                              in1=ro[:, 32:32 + E], op0=ALU.is_equal, op1=ALU.add))
                step(dve.tensor_tensor(ro[:, 32:32 + E], ro[:, 32:32 + E], ro[:, 16:16 + E], ALU.mult))
                step(dve.tensor_reduce(ro[:, 42:43], ro[:, 32:32 + E], AX.X, ALU.add))
                step(dve.tensor_scalar(ro[:, 42:43], ro[:, 42:43], 1e-6, None, ALU.add))
                step(dve.reciprocal(ro[:, 43:44], ro[:, 42:43]))
                step(dve.tensor_scalar(ro[:, 32:32 + E], ro[:, 32:32 + E], ro[:, 43:44], None, ALU.mult))
                step(dve.tensor_copy(zr[:, 0:R], zs[:, 0:R]))
                step(dve.tensor_tensor(zr[:, R:NZ].rearrange("p (e r) -> p e r", e=E),
                                       zs[:, R:NZ].rearrange("p (e r) -> p e r", e=E),
                                       ro[:, 32:32 + E].unsqueeze(2).broadcast_to([P, E, R]), ALU.mult))
                assert n[0] == R_STEPS

            def final(seg, b, t):
                T = NT * b + t
                dve.wait_ge(*m_full_at(seg, b, "F", t))
                ps, done = m_bank(seg, b, "F", t)
                dve.tensor_tensor(t1[:], ps[:], gbc[:, 1, :], ALU.mult).then_inc(done, 1)
                dve.wait_ge(*m_done_at(seg, b, "F", t))
                dve.wait_ge(d_out[t % 2], 16 * (4 * b + t // 2 + 1))
                dve.tensor_tensor(o_s[:, t % 2, :], x1[:], t1[:], ALU.add).then_inc(o_ok, 1)

            def sum_keys(Ta, t):
                dve.wait_ge(ckp_ok, Ta + 2)
                nb = P // CB
                dve.tensor_reduce(ckn[:, :, nb * t:nb * t + nb], ra[:].rearrange("p (c m k) -> p c m k", c=NC, k=CB),
                                  AX.X, ALU.add).then_inc(ckr_ok, 1)

            def finish_keys(ba):
                dve.wait_ge(ckr_ok, NT * ba + NT + 1)
                dve.tensor_tensor(ckn[:], ckn[:], pewT[:].unsqueeze(2).broadcast_to([P, NC, NB]), ALU.add).then_inc(b_ok, 1)

            def sum_queries(ba):
                dve.wait_ge(qsum_ok, NT * ba + NT + 1)
                dve.tensor_reduce(qs[:], qsum[:], AX.X, ALU.add).then_inc(b_ok, 1)

            def choose(ba):
                base = B_STEPS * ba
                dve.wait_ge(c_full, C_UNITS * ba + 3)
                dve.tensor_copy(imp[:], ps_c[0:1, 0:NB]).then_inc(c_done, 1)
                dve.wait_ge(c_done, C_UNITS * ba + 3)
                hold()
                dve.max(top[:], imp[:]).then_inc(b_ok, 1)
                dve.wait_ge(b_ok, base + 4)
                hold()
                dve.max_index(topi[:], top[:], imp[:]).then_inc(b_ok, 1)
                dve.wait_ge(b_ok, base + 5)
                dve.tensor_scalar(pos[:], topi[:, 0:2], float(CB), None, ALU.mult).then_inc(b_ok, 1)

            def gather(ba):
                base = B_STEPS * ba
                dve.wait_ge(c_full, C_UNITS * ba + 4)
                dve.tensor_copy(posb[:], ps_c[:, 0:2]).then_inc(c_done, 1)
                dve.wait_ge(c_done, C_UNITS * ba + 4)
                hold()
                for j in range(TOPK):
                    own = slice(SB * j, SB * j + SB)
                    first = dve.value_load(topi[0:1, j:j + 1], min_val=0, max_val=NB - 1)
                    for i in range(4):
                        rows = slice(HD * i, HD * i + HD)
                        dve.tensor_copy(csk[rows, :, CS * i + SB * j:CS * i + SB * j + SB],
                                        kT[rows, :, bass.ds(first * CB, SB)]).then_inc(b_ok, 1)
                    dve.tensor_scalar(csmask[:, :, own], token[:, :, own], posb[:, j:j + 1], NEG, ALU.is_lt, ALU.mult
                                      ).then_inc(b_ok, 1)
                    dve.tensor_copy(v_tiles[j][:], v_s[:, bass.ds(first // (P // CB), 1), :].squeeze(1)).then_inc(b_ok, 1)
                    dve.tensor_copy(tokj[:, j, :], token[:, bass.ds(first // (P // CB), 1), own].squeeze(1)).then_inc(b_ok, 1)
                    dve.wait_ge(b_ok, base + 13 + 8 * j)
                    dve.tensor_scalar(onehot[:, j, own], tokj[:, j, :], posb[:, j:j + 1], None, ALU.is_equal
                                      ).then_inc(b_ok, 1)

            def slot(seg, b, s):
                c, a, t = seg != "pro", seg != "epi", s - 1
                ba = b + 1 if seg == "loop" else 0
                Ta = NT * ba + t
                if s == 1 and seg == "loop":
                    ln_a(seg, b, -1, Ta, 0)
                if c and s == 1:
                    cs_factor(b, 0)
                if c:
                    window_max(b, s, 4)
                    cs_max(b, s)
                if c and s == 1:
                    window_max(b, s, 5)
                    if a:
                        rope(seg, b, t, "Q")
                    window_max(b, s, 6)
                    residual(seg, b, t)
                    ln_scale(x1[:], mvc, vec, x2n, lnc, lncp, NT * b + t)
                if c and s > 1:
                    residual(seg, b, t)
                    window_max(b, s, 5)
                    ln_scale(x1[:], mvc, vec, x2n, lnc, lncp, NT * b + t)
                if a and not (c and s == 1):
                    rope(seg, b, t, "Q")
                if c:
                    if s > 1:
                        window_max(b, s, 6)
                    window_max(b, s, 7)
                    cs_factor(b, s)
                if a:
                    dve.wait_ge(rope_ok, 2 * Ta + 2)
                    rope(seg, b, t, "K")
                if c:
                    window_max(b, s, 8)
                    window_max(b, s, 9)
                    window_max(b, s, 10)
                    router(seg, b, t, 0)
                if a:
                    gates_soft(seg, b, t, Ta, 0)
                if c:
                    window_max(b, s, 11)
                    window_norm(b, s, 0)
                    window_norm(b, s, 1)
                    router(seg, b, t, 1)
                if a:
                    gates_soft(seg, b, t, Ta, 1)
                    sum_q(seg, b, t, Ta)
                    sum_keys(Ta, t)
                    ln_a(seg, b, s - 1, Ta + 1, s)
                if c:
                    final(seg, b, t)

            def turn(seg, b):
                c2, t = seg != "pro", NT - 1
                ba = b + 1 if seg == "loop" else 0
                Ta = NT * ba + t
                window_max(ba, 0, 4)
                window_max(ba, 0, 5)
                if c2:
                    residual(seg, b, t)
                rope(seg, b, t, "Q")
                if c2:
                    ln_scale(x1[:], mvc, vec, x2n, lnc, lncp, NT * b + t)
                window_max(ba, 0, 6)
                dve.wait_ge(rope_ok, 2 * Ta + 2)
                rope(seg, b, t, "K")
                window_max(ba, 0, 7)
                window_max(ba, 0, 8)
                window_norm(ba, 0, 0)
                window_max(ba, 0, 9)
                sum_q(seg, b, t, Ta)
                sum_queries(ba)
                gates_soft(seg, b, t, Ta, 0)
                window_max(ba, 0, 10)
                sum_keys(Ta, t)
                finish_keys(ba)
                window_max(ba, 0, 11)
                if c2:
                    router(seg, b, t, 0)
                choose(ba)
                window_norm(ba, 0, 1)
                gather(ba)
                if c2:
                    router(seg, b, t, 1)
                gates_soft(seg, b, t, Ta, 1)
                cs_max(ba, 0)
                if c2:
                    final(seg, b, t)

            def last(seg, b):
                t = NT - 1
                residual(seg, b, t)
                ln_scale(x1[:], mvc, vec, x2n, lnc, lncp, NT * b + t)
                router(seg, b, t, 0)
                router(seg, b, t, 1)
                final(seg, b, t)

            dve.wait_ge(set_g, SETUP_G + 1)
            dve.memset(ro[:, 16 + E:24], -1.0)
            dve.wait_ge(*m_done_at("pro", 0, "MODT", 0))
            mod_copy(0, mod_a, 0, moda_ok)
            ln_a("pro", 0, -1, 0, 0)
            for s in range(1, NT):
                slot("pro", 0, s)
            turn("pro", 0)
            with dve.Fori(0, B - 1) as b:
                mod_copy(b, mod_c, 2, modc_ok)
                mod_copy(b + 1, mod_a, 0, moda_ok)
                for s in range(1, NT):
                    slot("loop", b, s)
                turn("loop", b)
            mod_copy(B - 1, mod_c, 2, modc_ok)
            for s in range(1, NT):
                slot("epi", B - 1, s)
            last("epi", B - 1)


def kernel(L0_attn_x, L0_attn_Wq, L0_attn_Wk, L0_attn_Wv, L0_attn_Wo, L0_attn_bo, L0_attn_wk_comp, L0_attn_wv_comp,
           L0_attn_pe, L0_attn_Wg, L0_attn_bg, L0_ffn_base_W, L0_ffn_base_b, L0_ffn_shared_A, L0_ffn_shared_B,
           L0_ffn_routed_A, L0_ffn_routed_B, L0_ffn_router_W, L0_ffn_router_b, L0_c, L0_wmod):
    import concourse.bacc as bacc
    from concourse.bass_utils import run_bass_kernel_spmd

    f = np.asarray
    arrays = {
        "x": f(L0_attn_x),
        "wqkv": np.concatenate([f(L0_attn_Wq), f(L0_attn_Wk), f(L0_attn_Wv)], axis=1),
        "wo": f(L0_attn_Wo),
        "wbt": f(L0_ffn_base_W).T,
        "wa": np.concatenate([f(L0_ffn_shared_A), f(L0_ffn_routed_A).reshape(E * R, D), f(L0_ffn_router_W)]).T,
        "wb": np.concatenate([f(L0_ffn_shared_B).T, f(L0_ffn_routed_B).transpose(0, 2, 1).reshape(E * R, D),
                              f(L0_ffn_base_b)[None]]),
        "cT": f(L0_c).T,
        "wmod": f(L0_wmod),
        "bo": f(L0_attn_bo),
        "bg": f(L0_attn_bg),
        "rb": f(L0_ffn_router_b),
        "wcomp": np.stack([f(L0_attn_wk_comp), f(L0_attn_wv_comp)]),
        "pe": f(L0_attn_pe),
        "pet": f(L0_attn_pe).T,
        "wg": f(L0_attn_Wg),
        "const": constants(),
    }
    arrays = {k: np.ascontiguousarray(a) for k, a in arrays.items()}
    nc = bacc.Bacc("TRN2", target_bir_lowering=False, num_devices=1)
    ins = {k: nc.dram_tensor(f"{k}_in", a.shape, mybir.dt.from_np(a.dtype), kind="ExternalInput").ap()
           for k, a in arrays.items()}
    gscr = nc.dram_tensor("gate_rows", [2, B, D], F32, kind="Internal").ap()
    out = nc.dram_tensor("out", [B, S, D], F32, kind="ExternalOutput").ap()
    program(nc, **ins, gscr=gscr, out=out)
    r = run_bass_kernel_spmd(nc, [{f"{k}_in": a for k, a in arrays.items()}], core_ids=[0])
    return r.results[0]["out"]
```

```python
from contextlib import ExitStack

import numpy as np
import concourse.bass as bass
from concourse import mybir

F32 = mybir.dt.float32
F32R = mybir.dt.float32r
BF16 = mybir.dt.bfloat16
U32 = mybir.dt.uint32
ALU = mybir.AluOpType
ACT = mybir.ActivationFunctionType
AX = mybir.AxisListType

P = 128
B, S, D = 8, 1024, 512
NT = S // P
NC = D // P
H, HD = 16, 32
CB, NB = 16, 64
SB, TOPK = 8, 2
NSEL = SB * TOPK
CS = NSEL + NB
E, R = 6, 16
NZ = R + E * R
SCALE = 1.0 / np.sqrt(HD)
NEG = -1e30
FLOOR = -1e29
EPS = 1e-5

C_ID, C_ROT, C_BLK, C_TOK, C_IO, C_WM, C_CM, C_END = np.cumsum(
    [0, P, NT * 2 * HD, 2 * (NB - 8) + 8, NT * NSEL, 8, 2 * P, NT * NB]).tolist()



def constants():
    p = np.arange(P)
    out = np.zeros((P, C_END), np.float32)
    out[:, C_ID:C_ROT] = np.eye(P)
    k = np.arange(P)
    out[:, C_WM:C_WM + P] = np.where(k[None] > p[:, None], 0, NEG)
    out[:, C_WM + P:C_CM] = np.where(k[None] <= p[:, None], 0, NEG)
    tok = np.arange(NT)[None, :, None] * P + p[:, None, None]
    out[:, C_CM:C_END] = np.where((np.arange(NB) + 1) * CB <= tok, 0, NEG).reshape(P, -1)
    half = HD // 2
    inv = (np.float32(1.0) / np.float32(10000.0) ** (np.arange(half, dtype=np.float32) * np.float32(2.0) / np.float32(HD))).astype(np.float32)
    ang = (np.arange(S, dtype=np.float32)[:, None] * inv[None, :]).astype(np.float32)
    cos, sin = np.cos(ang), np.sin(ang)
    rot = np.concatenate([np.repeat(cos, 2, axis=1), -sin, sin], axis=1)
    out[:, C_ROT:C_BLK] = rot.reshape(NT, P, 2 * HD).transpose(1, 0, 2).reshape(P, -1)
    out[:, C_BLK:C_TOK] = np.arange(2 * (NB - 8) + 8)[None] - (NB - 8) == p[:, None] // CB
    out[:, C_TOK:C_IO] = (tok - np.arange(NSEL) % SB).reshape(P, -1)
    out[:, C_IO:C_WM] = np.arange(8)
    return out


N_FIRST = 3 + P // CB + 7
C_UNITS = 4
SILU_STEPS = 3
GUARD_STEPS = 3 + 3 + 5 + 8 + 1
SETUP_V = GUARD_STEPS + 1
SETUP_G = 7
CS_STEPS = 9
G_STEPS = 3
B_STEPS = 5 + 8 * TOPK
R_STEPS = 16

SLOT_ORDER = [("HT", 1), ("Y", 0), ("Q", 1), ("H2T", 0), ("K", 1), ("Z", 0), ("G", 1), ("QT", 0), ("F", 1), ("KT", 0),
              ("ZT", 0), ("V", 0)]
TURN_ORDER = [("HT", 1), ("Y", 0), ("Q", 1), ("V", 0), ("K", 1), ("H2T", 0), ("QT", 1), ("KT", 0), ("G", 1), ("Z", 0),
              ("F", 1), ("ZT", 0)]
C2_UNITS = ("Y", "H2T", "Z", "F", "ZT")


def segment_units(c2, a):
    return [(u, s - 1, bank) for s in range(1, NT + 1) for u, bank in (SLOT_ORDER if s < NT else TURN_ORDER)
            if (c2 if u in C2_UNITS else a)]


SETUP_UNITS = [(f"MOD{i}", 0, i % 2) for i in range(6)] + [("MODT", 0, 0)]
HEAD_UNITS = [("HT", 0, 2)] + [(u, t + (u == "HT"), bank) for t in range(NT - 1)
                               for u, bank in (("Q", 0), ("K", 1), ("G", 3), ("HT", 2), ("V", 0), ("QT", 1), ("KT", 2))]
TURN_UNITS = [u for u in segment_units(c2=False, a=True) if u[1] == NT - 1 and u[0] != "HT"]
SEGMENTS = {"pro": SETUP_UNITS + HEAD_UNITS + TURN_UNITS, "loop": segment_units(c2=True, a=True),
            "epi": segment_units(c2=True, a=False)}


def m_unit(seg, b, name, t):
    i, bank = next((i, u[2]) for i, u in enumerate(SEGMENTS[seg]) if u[:2] == (name, t))
    before = sum(u[2] == bank for u in SEGMENTS[seg][:i])
    per = {s: sum(u[2] == bank for u in units) for s, units in SEGMENTS.items()}
    if seg == "pro":
        return bank, before
    return bank, (b if seg == "loop" else B - 1) * per["loop"] + per["pro"] + before


def place(t, r):
    return r if t else (r - 4) % 12


def s_bank(t, r):
    return place(t, r) % 3


def s_before(T, t, r):
    return 4 * T + place(t, r) // 3


def tile_blocks(t):
    slots = [(half, j, i) for half in range(2) for j in range(4) for i in range(2)]
    if t == 0:
        return [(h, w) for w in ("own", "cs") for h in slots]
    return [(h, w) for h in slots for w in ("prev", "own", "cs")]


def t_bank(t, i):
    return i % 3 if t else (0 if i >= 4 else i % 2)


def wn_count(T, slot):
    half, j, i = slot
    return WN_STEPS * T + WN_STEPS // 2 * half + 2 + 2 * j + i + 1


WN_STEPS = 20
ZT_ROUND = 5


def tp_rounds(t):
    return len(tile_blocks(t)) // 4


TP_BATCH = sum(tp_rounds(t) for t in range(NT))


def tp_before(b, t):
    return TP_BATCH * b + sum(tp_rounds(u) for u in range(t))


def program(nc, x, wqkv, wo, wbt, wa, wb, cT, wmod, bo, bg, rb, wcomp, pe, pet, wg, const, gscr, out):
    with ExitStack() as ctx:
        def sb(name, shape, dt=F32):
            return ctx.enter_context(nc.sbuf_tensor(name, shape, dt))

        def sem(name):
            return ctx.enter_context(nc.semaphore(name))

        w_hi = sb("w_hi", [P, 3, NC, D], F32R)
        w_lo = sb("w_lo", [P, 3, NC, D], F32R)
        wo_s = sb("wo_s", [P, NC, D])
        wbt_s = sb("wbt_s", [P, NC, D])
        wa_s = sb("wa_s", [P, NC, NZ + E])
        wb_s = sb("wb_s", [NZ + 1, D])
        wg_s = sb("wg_s", [P, NC, 3])
        cst = sb("cst", [P, C_WM])
        ident = cst[:, C_ID:C_ROT]
        rot = cst[:, C_ROT:C_BLK].rearrange("p (t n) -> p t n", t=NT)
        token = cst[:, C_TOK:C_IO].rearrange("p (t n) -> p t n", t=NT)
        ident_b = sb("ident_b", [P, P], BF16)
        zero_b = sb("zero_b", [P, 1], BF16)
        wmask = sb("wmask", [P, 2 * P], BF16)
        csmask = sb("csmask", [P, NT, CS], BF16)
        wcol = sb("wcol", [P, 1])
        blkw = sb("blkw", [P, C_TOK - C_BLK])
        wrow = sb("wrow", [P, CB])
        peT = sb("peT", [P, NC, CB])
        pewT = sb("pewT", [P, NC])
        ckn = sb("ckn", [P, NC, NB])
        pe_s = sb("pe_s", [CB, D])
        pew = sb("pew", [CB, NB])
        bg_s = sb("bg_s", [P, 3])
        rb_s = sb("rb_s", [P, E])
        ones = sb("ones", [1, P])
        cT_s = sb("cT_s", [P, NC, B])
        silu = sb("silu", [P, 3, NC, B])
        modT = sb("modT", [P, 4, NC, B])
        mod_a = sb("mod_a", [P, 2, NC])
        mod_c = sb("mod_c", [P, 2, NC])
        gbc = sb("gbc", [P, 3, D])
        xa = sb("xa", [P, 2, D])
        sta = sb("sta", [P, 6])
        mva = sb("mva", [P, 2])
        vea = sb("vea", [P, 2])
        power = sb("power", [P, 1])
        hT = sb("hT", [P, NC, P])
        h_hi = sb("h_hi", [P, NC, P], F32R)
        h_lo = sb("h_lo", [P, NC, P], F32R)
        ra = sb("ra", [P, D])
        rbf = sb("rbf", [P, D])
        kr = sb("kr", [P, D])
        qT = sb("qT", [P, NC, S])
        kT = sb("kT", [P, NC, S])
        v_s = sb("v_s", [P, NT, D])
        qsum = sb("qsum", [P, NC, NT])
        gl = sb("gl", [P, 8])
        gates = sb("gates", [P, NT, 3])
        csv = sb("csv", [P, D])
        csk = sb("csk", [P, NC, 4 * CS])
        qs = sb("qs", [P, NC])
        imp = sb("imp", [1, NB])
        top = sb("top", [1, 8])
        topi = sb("topi", [1, 8], U32)
        pos = sb("pos", [1, 2])
        posb = sb("posb", [P, 2])
        held = sb("held", [P, 1])
        onehot = sb("onehot", [P, TOPK, NSEL])
        v_tiles = [ra, rbf]
        tokj = sb("tokj", [P, TOPK, SB])
        css = sb("css", [P, H, CS])
        csp = sb("csp", [P, H, P])
        cm = sb("cm", [P, 2, H])
        cden = sb("cden", [P, 4, H])
        pw = sb("pw", [P, H, 2 * P])
        wmax = sb("wmax", [P, H])
        wden = sb("wden", [P, 3, H])
        pT = sb("pT", [P, 3, 4, P])
        aT = sb("aT", [P, NC, P])
        xc = sb("xc", [P, 2, D])
        t1 = sb("t1", [P, D])
        x1 = sb("x1", [P, D])
        stc = sb("stc", [P, 6])
        mvc = sb("mvc", [P, 2])
        vec = sb("vec", [P, 2])
        h2T = sb("h2T", [P, NC, P])
        zs = sb("zs", [P, NZ + E])
        ro = sb("ro", [P, 48])
        roi = sb("roi", [P, 8], U32)
        zr = sb("zr", [P, NZ + 1])
        zT = sb("zT", [NZ + 1, P])
        w_stage = [qT[:, :, :].rearrange("p c n -> p (c n)")[:, i * NC * D:(i + 1) * NC * D] for i in range(2)]
        w_stage += [v_s[:, 0:NC, :].rearrange("p c n -> p (c n)")]
        w_stage = [w.rearrange("p (c n) -> p c n", c=NC) for w in w_stage]
        modr = v_s[0:B, NC:2 * NC, :]
        spare = kT[:, :, :].rearrange("p c n -> p (c n)")
        masks = spare[:, 0:C_END - C_WM]
        gpart = spare[0:B, 2 * D:4 * D].rearrange("p (a n) -> p a n", a=2)
        gr = spare[0:B, 4 * D:7 * D].rearrange("p (a n) -> p a n", a=3)
        bo_s = spare[0:B, 7 * D:8 * D]
        wm_ring = pw[:, :, :].rearrange("p a b -> p (a b)").rearrange("p (s c n) -> p s c n", s=2, c=NC)

        ps_s = [ctx.enter_context(nc.psum_tensor(f"ps_s{i}", [P, 512], F32)) for i in range(3)]
        ps_m = [ctx.enter_context(nc.psum_tensor(f"ps_m{i}", [P, 512], F32)) for i in range(2)]
        ps_m += ps_s[1:]
        ps_t = ctx.enter_context(nc.psum_tensor("ps_t", [P, 4, P], F32))
        ps_o = ctx.enter_context(nc.psum_tensor("ps_o", [P, NC, P], F32))
        t_banks = [ps_t] + [ps_s[i][:].rearrange("p (k n) -> p k n", k=4) for i in range(2)]
        ps_c = ctx.enter_context(nc.psum_tensor("ps_c", [P, D], F32))

        d_first = sem("d_first")
        d_w = sem("d_w")
        d_mod = [sem("d_mod0"), sem("d_mod1")]
        d_xa = [sem("d_xa0"), sem("d_xa1")]
        d_xc = [sem("d_xc0"), sem("d_xc1")]
        d_scr = sem("d_scr")
        d_gbc = sem("d_gbc")
        d_out = sem("d_out")
        d_wqkv = sem("d_wqkv")
        started = sem("started")
        set_v, set_a, set_g = sem("set_v"), sem("set_a"), sem("set_g")
        m_full = [sem(f"m_full{i}") for i in range(4)]
        m_done = [sem(f"m_done{i}") for i in range(4)]
        s_full = [sem(f"s_full{i}") for i in range(3)]
        s_done = [sem(f"s_done{i}") for i in range(3)]
        t_full, t_done = sem("t_full"), sem("t_done")
        pv_done = sem("pv_done")
        o_done = sem("o_done")
        wmax_ok = sem("wmax_ok")
        wn_ok = sem("wn_ok")
        cs_ok = sem("cs_ok")
        cs_exp = sem("cs_exp")
        cs_shift = sem("cs_shift")
        cs_norm = sem("cs_norm")
        lna, lnc = sem("lna"), sem("lnc")
        lnap, lncp = sem("lnap"), sem("lncp")
        rope_ok = sem("rope_ok")
        qsum_ok = sem("qsum_ok")
        g_ok, g_exp = sem("g_ok"), sem("g_exp")
        c_full, c_done = sem("c_full"), sem("c_done")
        ckp_ok = sem("ckp_ok")
        ckr_ok = sem("ckr_ok")
        ck_spread = sem("ck_spread")
        b_ok = sem("b_ok")
        xb_ok = sem("xb_ok")
        y_ok = sem("y_ok")
        r_ok, r_exp = sem("r_ok"), sem("r_exp")
        o_ok = sem("o_ok")
        modc_ok, moda_ok = sem("modc_ok"), sem("moda_ok")
        whi_ok, wlo_ok = sem("whi_ok"), sem("wlo_ok")
        hhi_ok, hlo_ok = sem("hhi_ok"), sem("hlo_ok")
        credited = (set_v, set_a, set_g, *m_full, *m_done, *s_full, *s_done, t_full, t_done, pv_done, o_done,
                    wmax_ok, wn_ok, cs_ok, cs_exp, cs_shift, cs_norm, lna, lnc, lnap, lncp, rope_ok, qsum_ok, g_ok, g_exp,
                    c_full, c_done, ckp_ok, ckr_ok, ck_spread, b_ok, xb_ok, y_ok, r_ok, r_exp, o_ok, modc_ok, moda_ok,
                    whi_ok, wlo_ok, hhi_ok, hlo_ok)

        def m_bank(seg, b, name, t):
            bank, _ = m_unit(seg, b, name, t)
            return ps_m[bank], m_done[bank]

        def m_free_at(seg, b, name, t):
            bank, before = m_unit(seg, b, name, t)
            return m_done[bank], before + 1

        def m_full_at(seg, b, name, t):
            bank, before = m_unit(seg, b, name, t)
            return m_full[bank], before + 2

        def m_done_at(seg, b, name, t):
            bank, before = m_unit(seg, b, name, t)
            return m_done[bank], before + 2

        parts = ((0, NSEL), (NSEL, CS))
        block = ctx.enter_context(nc.Block())

        @block.sync
        def _(sp):
            for s in credited:
                sp.sem_inc(s, 1)
            sp.sem_inc(started, 1)
            sp.sem_inc(d_out, 16)
            sp.dma_start(cT_s[:], cT.rearrange("(c p) b -> p c b", p=P)).then_inc(d_first, 16)
            sp.dma_start(cst[:], const[:, 0:C_WM]).then_inc(d_first, 16)
            sp.dma_start(masks, const[:, C_WM:C_END]).then_inc(d_first, 16)
            n_first = 3

            def load_mod(i):
                if i >= 2:
                    bank, before = m_unit("pro", 0, f"MOD{i - 2}", 0)
                    sp.wait_ge(m_full[bank], before + 2)
                sp.dma_start(wm_ring[:, i % 2], wmod[:, i * D:(i + 1) * D].rearrange("(c p) n -> p c n", p=P)
                             ).then_inc(d_mod[i % 2], 16)

            load_mod(0)
            load_mod(1)
            for i in range(P // CB):
                sp.dma_start(wcol[i * CB:(i + 1) * CB, :], wcomp[1].rearrange("(p a) -> p a", a=1)).then_inc(d_first, 16)
                n_first += 1
            for dst, src in ((pe_s[:], pe), (bo_s, bo.partition_broadcast(B)), (bg_s[:], bg.partition_broadcast(P)),
                             (rb_s[:], rb.partition_broadcast(P)),
                             (wg_s[:], wg.rearrange("(c p) n -> p c n", p=P)),
                             (wrow[:], wcomp[0].partition_broadcast(P)),
                             (peT[:], pet.rearrange("(c p) k -> p c k", p=P))):
                sp.dma_start(dst, src).then_inc(d_first, 16)
                n_first += 1
            assert n_first == N_FIRST

            def load_xa(T_former, b, t):
                if T_former is not None:
                    sp.wait_ge(rope_ok, 2 * T_former + 2)
                sp.dma_start(xa[:, t % 2, :], x[b, t * P:(t + 1) * P, :]).then_inc(d_xa[t % 2], 16)

            def load_xc(T, b, t):
                if t > 1:
                    sp.wait_ge(r_ok, R_STEPS * (T - 2) + 2)
                sp.dma_start(xc[:, t % 2, :], x[b, t * P:(t + 1) * P, :]).then_inc(d_xc[t % 2], 16)

            def load_gates(b):
                sp.wait_ge(o_ok, NT * b + 1)
                sp.wait_ge(d_scr, 16 * 3)
                for i in range(3):
                    sp.dma_start(gbc[:, i, :], gscr[i, b, :].partition_broadcast(P)).then_inc(d_gbc, 16)

            load_xa(None, 0, 0)
            load_xa(None, 0, 1)
            for i in range(3):
                sp.dma_start(w_stage[i], wqkv[:, i * D:(i + 1) * D].rearrange("(c p) n -> p c n", p=P)).then_inc(d_wqkv, 16)
            for i in range(2, 6):
                load_mod(i)
            sp.dma_start(wo_s[:], wo.rearrange("(c p) n -> p c n", p=P)).then_inc(d_w, 16)
            sp.dma_start(wbt_s[:], wbt.rearrange("(c p) n -> p c n", p=P)).then_inc(d_w, 16)
            sp.dma_start(wa_s[:], wa.rearrange("(c p) n -> p c n", p=P)).then_inc(d_w, 16)
            sp.dma_start(wb_s[:], wb).then_inc(d_w, 16)
            sp.wait_ge(set_v, GUARD_STEPS + 1)
            for i in range(3):
                sp.dma_start(gscr[i], gr[:, i, :]).then_inc(d_scr, 16)
            for t in range(2, NT):
                load_xa(t - 2, 0, t)
            load_xa(NT - 2, 1, 0)

            def batch(b, a):
                load_gates(b)
                load_xc(NT * b, b, 0)
                for s in range(1, NT + 1):
                    if s < NT:
                        load_xc(NT * b + s, b, s)
                    if a and s < NT:
                        load_xa(NT * b + NT + s - 2, b + 1, s)
                if a:
                    load_xa(NT * (b + 1) + NT - 2, (b + 2) % B, 0)

            with sp.Fori(0, B - 1) as b:
                batch(b, True)
            batch(B - 1, False)
            sp.wait_ge(d_out, 16 * (B * NT + 1))
            sp.wait_ge(d_scr, 48)

        @block.tensor
        def _(pe_):
            def m_target(seg, b, name, t):
                bank, _ = m_unit(seg, b, name, t)
                return ps_m[bank], m_full[bank]

            pe_.wait_ge(d_first, 16 * (N_FIRST))
            pe_.wait_ge(set_v, SILU_STEPS + 1)
            for i in range(6):
                pe_.wait_ge(*m_free_at("pro", 0, f"MOD{i}", 0))
                ps, full = m_target("pro", 0, f"MOD{i}", 0)
                pe_.wait_ge(d_mod[i % 2], 16 * (i // 2 + 1))
                for c in range(NC):
                    mm = pe_.matmul(ps[0:B, :], silu[:, 2, c, :], wm_ring[:, i % 2, c, :], start=(c == 0), stop=(c == NC - 1))
                mm.then_inc(full, 1)
            pe_.wait_ge(*m_free_at("pro", 0, "MODT", 0))
            ps, full = m_target("pro", 0, "MODT", 0)
            pe_.wait_ge(*m_done_at("pro", 0, "MOD4", 0))
            pe_.wait_ge(*m_done_at("pro", 0, "MOD5", 0))
            for i in range(4):
                for c in range(NC):
                    k = (i * NC + c) * B
                    mm = pe_.transpose(ps[:, k:k + B], modr[:, i, c * P:(c + 1) * P], ident[0:B, 0:B])
            mm.then_inc(full, 1)
            pe_.wait_ge(d_w, 16 * 4)
            pe_.wait_ge(whi_ok, 4)
            pe_.wait_ge(wlo_ok, 4)
            pe_.wait_ge(set_v, SETUP_V + 1)

            def transpose_h(seg, b, t, T):
                pe_.wait_ge(*m_free_at(seg, b, "HT", t))
                ps, full = m_target(seg, b, "HT", t)
                pe_.wait_ge(lna, 4 * T + 5)
                for c in range(NC):
                    mm = pe_.transpose(ps[:, c * P:(c + 1) * P], xa[:, t % 2, c * P:(c + 1) * P], ident)
                mm.then_inc(full, 1)

            def project(seg, b, t, name, col, chunks=range(NC)):
                ps, full = m_target(seg, b, name, t)
                if chunks[0] == 0:
                    pe_.wait_ge(*m_free_at(seg, b, name, t))
                if name == "Q" and chunks[0] == 0:
                    Ta = NT * (b + 1 if seg == "loop" else 0) + t
                    pe_.wait_ge(hhi_ok, Ta + 2)
                    pe_.wait_ge(hlo_ok, Ta + 2)
                for c in chunks:
                    pe_.matmul(ps[:], h_hi[:, c, :], w_hi[:, col, c, :], start=(c == 0), stop=False)
                    pe_.matmul(ps[:], h_hi[:, c, :], w_lo[:, col, c, :], start=False, stop=False)
                    mm = pe_.matmul(ps[:], h_lo[:, c, :], w_hi[:, col, c, :], start=False, stop=(c == NC - 1))
                if c == NC - 1:
                    mm.then_inc(full, 1)

            def transpose_rot(seg, b, t, T, name, src, n):
                pe_.wait_ge(*m_free_at(seg, b, name, t))
                ps, full = m_target(seg, b, name, t)
                pe_.wait_ge(rope_ok, 2 * T + n + 1)
                for c in range(NC):
                    mm = pe_.transpose(ps[:, c * P:(c + 1) * P], src[:, c * P:(c + 1) * P], ident)
                mm.then_inc(full, 1)

            def gate_logits(seg, b, t, chunks=range(NC)):
                ps, full = m_target(seg, b, "G", t)
                if chunks[0] == 0:
                    pe_.wait_ge(*m_free_at(seg, b, "G", t))
                for c in chunks:
                    mm = pe_.matmul(ps[:, 0:3], hT[:, c, :], wg_s[:, c, :], start=(c == 0), stop=(c == NC - 1))
                if c == NC - 1:
                    mm.then_inc(full, 1)

            def compress(seg, b, t, T, batch_a):
                dst = ps_c[NB:P, :]
                if t == 0:
                    pe_.wait_ge(c_done, C_UNITS * batch_a + 1)
                    pe_.matmul(dst, pew[:, :], pe_s[:, :], start=True, stop=False, skip_group_check=True)
                pe_.wait_ge(*m_done_at(seg, b, "V", t))
                off = NB - 8 - 8 * t
                mm = pe_.matmul(dst, blkw[:, off:off + NB], v_s[:, t, :], start=False, stop=(t == NT - 1),
                                skip_group_check=True)
                if t == NT - 1:
                    mm.then_inc(c_full, 1)

            def importance(ba):
                pe_.wait_ge(c_done, C_UNITS * ba + 2)
                pe_.wait_ge(b_ok, B_STEPS * ba + 3)
                for c in range(NC):
                    mm = pe_.matmul(ps_c[0:1, 0:NB], qs[:, c:c + 1], ckn[:, c, :], start=(c == 0), stop=(c == NC - 1))
                mm.then_inc(c_full, 1)

            def spread_positions(ba):
                pe_.wait_ge(c_done, C_UNITS * ba + 3)
                pe_.wait_ge(b_ok, B_STEPS * ba + 6)
                pe_.matmul(ps_c[:, 0:2], ones[:, :], pos[:, :], start=True, stop=True).then_inc(c_full, 1)

            def select_values(ba):
                pe_.wait_ge(c_done, C_UNITS * ba + 4)
                pe_.wait_ge(b_ok, B_STEPS * ba + 5 + 3 * TOPK + 1)
                for j, v_tile in enumerate(v_tiles):
                    mm = pe_.matmul(ps_c[0:NSEL, :], onehot[:, j, :], v_tile[:, :], start=(j == 0), stop=(j == TOPK - 1))
                mm.then_inc(c_full, 1)

            def score_round(b, t, r):
                T = NT * b + t
                bank = s_bank(t, r)
                pe_.wait_ge(s_done[bank], s_before(T, t, r) + 1)
                if place(t, r) == 0:
                    pe_.wait_ge(t_done, tp_before(b, t) + 1 - (4 if t == 1 else 0))
                if place(t, r) == 9 and t == 0:
                    pe_.wait_ge(t_done, tp_before(b, t) + 5)
                ps = ps_s[bank]
                if r < 4:
                    dst = ps[:, 0:4 * CS]
                    if t == 0 and r == 0:
                        pe_.wait_ge(c_done, C_UNITS * b + 5)
                        pe_.wait_ge(ck_spread, 4 * b + 5)
                        pe_.wait_ge(b_ok, B_STEPS * (b + 1) + 1)
                    pe_.matmul(dst.rearrange("p (c n) -> p c n", c=4), ident_b[:, :],
                               csmask[:, t, :].unsqueeze(1).broadcast_to([P, 4, CS]),
                               start=True, stop=False, skip_group_check=True)
                    mm = pe_.matmul(dst, qT[:, r, t * P:(t + 1) * P], csk[:, r, :], start=False, stop=True,
                                    skip_group_check=True)
                else:
                    half, j = divmod(r - 4, 4)
                    rows = slice(HD * j, HD * j + HD)
                    k0, n = ((t - 1) * P, 2 * P) if t else (0, P)
                    dst = ps[:, 0:2 * n].rearrange("p (c n) -> p c n", c=2)
                    pe_.matmul(dst, ident_b[:, :], wmask[:, 2 * P - n:].unsqueeze(1).broadcast_to([P, 2, n]),
                               start=True, stop=False, skip_group_check=True)
                    for i in range(2):
                        mm = pe_.matmul(dst[:, i, :], qT[rows, 2 * half + i, t * P:(t + 1) * P],
                                        kT[rows, 2 * half + i, k0:k0 + n], start=False, stop=True, skip_group_check=True)
                mm.then_inc(s_full[bank], 1)

            def head_column(slot):
                half, j, i = slot
                return (half * 4 + j) * 2 + i

            def transpose_round(b, t, i):
                T, n = NT * b + t, tp_before(b, t) + i
                bank = t_bank(t, i)
                former = [k for k in range(i) if t_bank(t, k) == bank]
                if former:
                    pe_.wait_ge(t_done, tp_before(b, t) + former[-1] + 2)
                elif t > 0 and bank > 0:
                    pe_.wait_ge(s_done[bank - 1], s_before(T, t, 8 + bank) + 2)
                elif bank > 0:
                    pe_.wait_ge(s_done[0], s_before(T, t, 10) + 2)
                dst = t_banks[t_bank(t, i)]
                blocks = tile_blocks(t)
                for k in range(4):
                    (half, j, ii), what = blocks[4 * i + k]
                    hw = head_column((half, j, ii))
                    if what == "cs":
                        src = csp[:, 4 * (2 * half + ii) + j, :]
                        if k == 0 or not t or i < 1:
                            pe_.wait_ge(cs_norm, 2 * T + 3)
                    else:
                        src = pw[:, hw, P:2 * P] if what == "own" else pw[:, hw, 0:P]
                        pe_.wait_ge(wn_ok, wn_count(T, (half, j, ii)) + 1)
                    mm = pe_.transpose(dst[:, k, :], src, ident)
                mm.then_inc(t_full, 1)

            def value_round(b, t, i):
                T, n = NT * b + t, tp_before(b, t) + i
                if i == 0:
                    pe_.wait_ge(o_done, T + 1)
                    if t == 0:
                        pe_.matmul(ps_o[:], ident_b[:, :], zero_b[:].unsqueeze(1).broadcast_to([P, NC, P]),
                                   start=True, stop=False, skip_group_check=True)
                pe_.wait_ge(t_done, n + 2)
                blocks = tile_blocks(t)
                for k in range(4):
                    m = 4 * i + k
                    (half, j, ii), what = blocks[m]
                    c = 2 * half + ii
                    cols = slice(P * c + HD * j, P * c + HD * j + HD)
                    src = csv[:, cols] if what == "cs" else v_s[:, t if what == "own" else t - 1, cols]
                    mm = pe_.matmul(ps_o[HD * j:HD * j + HD, c, :], src, pT[:, i % 3, k, :],
                                    start=(what == "prev"), stop=(what == "cs"),
                                    skip_group_check=True)
                mm.then_inc(pv_done, 1)

            def output(seg, b, t, chunks=range(NC)):
                ps, full = m_target(seg, b, "Y", t)
                if chunks[0] == 0:
                    pe_.wait_ge(*m_free_at(seg, b, "Y", t))
                    pe_.wait_ge(o_done, NT * b + t + 2)
                for c in chunks:
                    mm = pe_.matmul(ps[:], aT[:, c, :], wo_s[:, c, :], start=(c == 0), stop=(c == NC - 1))
                if c == NC - 1:
                    mm.then_inc(full, 1)

            def transpose_h2(seg, b, t):
                pe_.wait_ge(*m_free_at(seg, b, "H2T", t))
                ps, full = m_target(seg, b, "H2T", t)
                pe_.wait_ge(lnc, 4 * (NT * b + t) + 5)
                for c in range(NC):
                    mm = pe_.transpose(ps[:, c * P:(c + 1) * P], xc[:, t % 2, c * P:(c + 1) * P], ident)
                mm.then_inc(full, 1)

            def lora_down(seg, b, t):
                pe_.wait_ge(*m_free_at(seg, b, "Z", t))
                ps, full = m_target(seg, b, "Z", t)
                pe_.wait_ge(*m_done_at(seg, b, "H2T", t))
                for c in range(NC):
                    mm = pe_.matmul(ps[:, 0:NZ + E], h2T[:, c, :], wa_s[:, c, :], start=(c == 0), stop=(c == NC - 1))
                mm.then_inc(full, 1)

            def transpose_z(seg, b, t):
                pe_.wait_ge(*m_free_at(seg, b, "ZT", t))
                ps, full = m_target(seg, b, "ZT", t)
                pe_.wait_ge(r_ok, R_STEPS * (NT * b + t + 1) + 1)
                pe_.transpose(ps[0:NZ + 1, 0:P], zr[:, :], ident).then_inc(full, 1)

            def feed(seg, b, t, chunks=range(NC + 1)):
                ps, full = m_target(seg, b, "F", t)
                if chunks[0] == 0:
                    pe_.wait_ge(*m_free_at(seg, b, "F", t))
                for c in chunks:
                    if c < NC:
                        pe_.matmul(ps[:], h2T[:, c, :], wbt_s[:, c, :], start=(c == 0), stop=False)
                    else:
                        pe_.wait_ge(*m_done_at(seg, b, "ZT", t))
                        pe_.matmul(ps[:], zT[:, :], wb_s[:, :], start=False, stop=True).then_inc(full, 1)

            def slot(seg, b, s):
                c, a, t = seg != "pro", seg != "epi", s - 1
                ba = b + 1 if seg == "loop" else 0
                Ta = NT * ba + t
                if c and s > 1:
                    score_round(b, s, 0)
                if a:
                    transpose_h(seg, b, t, Ta)
                if c and s == 1:
                    for r in range(3):
                        score_round(b, s, r)
                    if a:
                        project(seg, b, t, "Q", 0)
                    score_round(b, s, 3)
                    score_round(b, s, 4)
                if c and s > 1:
                    score_round(b, s, 1)
                    output(seg, b, t, [0])
                    score_round(b, s, 2)
                    output(seg, b, t, [1])
                    score_round(b, s, 3)
                    score_round(b, s, 4)
                    output(seg, b, t, [2, 3])
                if a and s > 1:
                    compress(seg, b, t - 1, Ta - 1, ba)
                if c:
                    score_round(b, s, 5)
                if c and s == 1:
                    for i in range(4, 8):
                        transpose_round(b, 0, i)
                        if i == 6:
                            score_round(b, s, 6)
                        elif a:
                            project(seg, b, t, "K", 1, [{4: 0, 5: 1, 7: 2}[i]])
                        value_round(b, 0, i)
                    if a:
                        project(seg, b, t, "K", 1, [3])
                    output(seg, b, t)
                if a and not (c and s == 1):
                    project(seg, b, t, "Q", 0)
                if c:
                    if s > 1:
                        score_round(b, s, 6)
                    score_round(b, s, 7)
                if c and s > 1:
                    transpose_h2(seg, b, t)
                if a and not (c and s == 1):
                    project(seg, b, t, "K", 1)
                if c:
                    score_round(b, s, 8)
                    if s == 1:
                        if a:
                            gate_logits(seg, b, t)
                        transpose_h2(seg, b, t)
                    score_round(b, s, 9)
                    lora_down(seg, b, t)
                if c and a and s > 1:
                    gate_logits(seg, b, t, [0])
                    score_round(b, s, 10)
                    gate_logits(seg, b, t, [1, 2])
                elif c:
                    score_round(b, s, 10)
                if a:
                    transpose_rot(seg, b, t, Ta, "QT", ra, 1)
                if c and a and s > 1:
                    gate_logits(seg, b, t, [3])
                if c:
                    score_round(b, s, 11)
                    feed(seg, b, t, [0])
                if a:
                    transpose_rot(seg, b, t, Ta, "KT", kr, 2)
                if c:
                    n = tp_rounds(s)
                    feed(seg, b, t, [1, 2])
                    transpose_round(b, s, 0)
                    transpose_round(b, s, 1)
                    transpose_round(b, s, 2)
                    for i in range(n):
                        if i == 1:
                            feed(seg, b, t, [3])
                        if i == ZT_ROUND:
                            transpose_z(seg, b, t)
                        if i == ZT_ROUND + 2:
                            feed(seg, b, t, [NC])
                        if a and n - 1 - NC <= i < n - 1:
                            project(seg, b, t, "V", 2, [i - (n - 1 - NC)])
                        value_round(b, s, i)
                        if i + 3 < n:
                            transpose_round(b, s, i + 3)

            def turn(seg, b):
                c2, t = seg != "pro", NT - 1
                ba = b + 1 if seg == "loop" else 0
                Ta = NT * ba + t
                score_round(ba, 0, 4)
                if c2:
                    transpose_h(seg, b, t, Ta)
                else:
                    pe_.wait_ge(*m_done_at(seg, b, "KT", t - 1))
                    pe_.wait_ge(*m_done_at(seg, b, "G", t - 1))
                score_round(ba, 0, 5)
                compress(seg, b, t - 1, Ta - 1, ba)
                if c2:
                    output(seg, b, t)
                project(seg, b, t, "Q", 0)
                score_round(ba, 0, 6)
                project(seg, b, t, "V", 2)
                project(seg, b, t, "K", 1)
                if c2:
                    transpose_h2(seg, b, t)
                score_round(ba, 0, 7)
                compress(seg, b, t, Ta, ba)
                transpose_rot(seg, b, t, Ta, "QT", ra, 1)
                score_round(ba, 0, 8)
                transpose_rot(seg, b, t, Ta, "KT", kr, 2)
                score_round(ba, 0, 9)
                score_round(ba, 0, 10)
                gate_logits(seg, b, t)
                score_round(ba, 0, 11)
                if c2:
                    lora_down(seg, b, t)
                importance(ba)
                if c2:
                    feed(seg, b, t, [0])
                transpose_round(ba, 0, 0)
                transpose_round(ba, 0, 1)
                if c2:
                    feed(seg, b, t, [1])
                value_round(ba, 0, 0)
                transpose_round(ba, 0, 2)
                spread_positions(ba)
                value_round(ba, 0, 1)
                transpose_round(ba, 0, 3)
                value_round(ba, 0, 2)
                value_round(ba, 0, 3)
                if c2:
                    feed(seg, b, t, [2])
                select_values(ba)
                score_round(ba, 0, 0)
                if c2:
                    feed(seg, b, t, [3])
                score_round(ba, 0, 1)
                if c2:
                    transpose_z(seg, b, t)
                score_round(ba, 0, 2)
                if c2:
                    feed(seg, b, t, [NC])
                score_round(ba, 0, 3)

            def last(seg, b):
                t = NT - 1
                output(seg, b, t)
                transpose_h2(seg, b, t)
                lora_down(seg, b, t)
                feed(seg, b, t, range(NC))
                transpose_z(seg, b, t)
                feed(seg, b, t, [NC])

            def head(t):
                project("pro", 0, t, "Q", 0)
                if t > 0:
                    compress("pro", 0, t - 1, t - 1, 0)
                project("pro", 0, t, "K", 1)
                gate_logits("pro", 0, t)
                transpose_h("pro", 0, t + 1, t + 1)
                project("pro", 0, t, "V", 2)
                transpose_rot("pro", 0, t, t, "QT", ra, 1)
                transpose_rot("pro", 0, t, t, "KT", kr, 2)

            transpose_h("pro", 0, 0, 0)
            for t in range(NT - 1):
                head(t)
            turn("pro", 0)
            with pe_.Fori(0, B - 1) as b:
                for s in range(1, NT):
                    slot("loop", b, s)
                turn("loop", b)
            for s in range(1, NT):
                slot("epi", B - 1, s)
            last("epi", B - 1)

        @block.scalar
        def _(act):
            act.wait_ge(d_first, 16 * (N_FIRST))
            act.activation(silu[:, 0], cT_s[:], ACT.Exp, scale=-1.0).then_inc(set_a, 1)
            for k, i in enumerate((0, 1, 3, 4)):
                if k == 2:
                    act.wait_ge(d_wqkv, 48)
                    for j in range(3):
                        act.activation(w_hi[:, j], w_stage[j], ACT.Copy).then_inc(whi_ok, 1)
                act.wait_ge(*m_full_at("pro", 0, f"MOD{i}", 0))
                ps, done = m_bank("pro", 0, f"MOD{i}", 0)
                act.activation(modr[:, k, :], ps[0:B, :], ACT.Copy).then_inc(done, 1)

            def h_scaled(seg, b, t, name, dst, mod, mod_sem, mod_count):
                act.wait_ge(*m_full_at(seg, b, name, t))
                ps, done = m_bank(seg, b, name, t)
                if t == 0:
                    act.wait_ge(mod_sem, mod_count + 1)
                for c in range(NC):
                    ins = act.activation(dst[:, c, :], ps[:, c * P:(c + 1) * P], ACT.Identity,
                                         scale=mod[:, 1, c:c + 1], bias=mod[:, 0, c:c + 1])
                ins.then_inc(done, 1)

            def split_h(Ta):
                act.activation(h_hi[:], hT[:], ACT.Copy).then_inc(hhi_ok, 1)

            def copy_v(seg, b, t):
                act.wait_ge(*m_full_at(seg, b, "V", t))
                ps, done = m_bank(seg, b, "V", t)
                act.activation(v_s[:, t, :], ps[:], ACT.Copy).then_inc(done, 1)

            def copy_qT(seg, b, t):
                act.wait_ge(*m_full_at(seg, b, "QT", t))
                ps, done = m_bank(seg, b, "QT", t)
                act.activation(qT[:, :, t * P:(t + 1) * P], ps[:].rearrange("p (c n) -> p c n", c=NC), ACT.Copy,
                               scale=float(SCALE)).then_inc(done, 1)

            def copy_kT(seg, b, t):
                act.wait_ge(*m_full_at(seg, b, "KT", t))
                ps, done = m_bank(seg, b, "KT", t)
                act.activation(kT[:, :, t * P:(t + 1) * P], ps[:].rearrange("p (c n) -> p c n", c=NC), ACT.Copy
                               ).then_inc(done, 1)

            def gate_exp(Ta):
                act.wait_ge(g_ok, G_STEPS * Ta + 2)
                act.activation(gl[:, 3:6], gl[:, 0:3], ACT.Exp, bias=gl[:, 6:7], accum_out=gl[:, 7:8]).then_inc(g_exp, 1)

            def cs_copy(b, t, r):
                T = NT * b + t
                bank = s_bank(t, r)
                act.wait_ge(s_full[bank], s_before(T, t, r) + 2)
                if r == 0:
                    act.wait_ge(cs_exp, 2 * T + 1)
                act.activation(css[:, 4 * r:4 * r + 4, :], ps_s[bank][:, 0:4 * CS].rearrange("p (c n) -> p c n", c=4),
                               ACT.Copy).then_inc(s_done[bank], 1)

            def cs_exps(b, t):
                T = NT * b + t
                act.wait_ge(cs_shift, 2 * T + 3)
                act.wait_ge(t_full, tp_before(b, t) + 1)
                act.activation(csp[:, :, 0:NSEL], css[:, :, 0:NSEL], ACT.Exp).then_inc(cs_exp, 1)
                act.activation(csp[:, :, P - NB:P], css[:, :, NSEL:CS], ACT.Exp).then_inc(cs_exp, 1)

            def window_exp(b, t, r):
                T = NT * b + t
                act.wait_ge(wmax_ok, 8 * T + r - 2)
                if r == 4:
                    act.wait_ge(t_full, tp_before(b, t) + 1 - (4 if t == 1 else 0))
                    act.wait_ge(wn_ok, WN_STEPS * T + 1)
                n = 2 * P if t else P
                for i in range(2):
                    hw = 2 * (r - 4) + i
                    ins = act.activation(pw[:, hw, 2 * P - n:2 * P], ps_s[s_bank(t, r)][:, i * n:(i + 1) * n], ACT.Exp,
                                         bias=wmax[:, hw:hw + 1], accum_out=wden[:, 0, hw:hw + 1])
                ins.then_inc(s_done[s_bank(t, r)], 1)

            def copy_z(seg, b, t):
                act.wait_ge(*m_full_at(seg, b, "Z", t))
                ps, done = m_bank(seg, b, "Z", t)
                act.wait_ge(r_ok, R_STEPS * (NT * b + t) + 1)
                act.activation(zs[:, :], ps[:, 0:NZ + E], ACT.Copy).then_inc(done, 1)

            def router_exp(b, t):
                T = NT * b + t
                act.wait_ge(r_ok, R_STEPS * T + 3)
                act.activation(ro[:, 8:14], ro[:, 0:6], ACT.Exp, bias=ro[:, 6:7], accum_out=ro[:, 7:8]).then_inc(r_exp, 1)

            def copy_zT(seg, b, t):
                act.wait_ge(*m_full_at(seg, b, "ZT", t))
                ps, done = m_bank(seg, b, "ZT", t)
                act.activation(zT[:, :], ps[0:NZ + 1, 0:P], ACT.Copy).then_inc(done, 1)

            def probs_copy(b, t, i):
                n = tp_before(b, t) + i
                act.wait_ge(t_full, n + 2)
                if i >= 3:
                    act.wait_ge(pv_done, n - 1)
                act.activation(pT[:, i % 3], t_banks[t_bank(t, i)][:], ACT.Copy).then_inc(t_done, 1)

            def copy_out(b, t):
                act.wait_ge(pv_done, tp_before(b, t) + tp_rounds(t) + 1)
                act.activation(aT[:], ps_o[:], ACT.Copy).then_inc(o_done, 1)

            def copy_cv(ba):
                act.wait_ge(c_full, C_UNITS * ba + 2)
                act.activation(csv[P - NB:P, :], ps_c[NB:P, :], ACT.Copy).then_inc(c_done, 1)

            def spread_ck(ba):
                act.wait_ge(b_ok, B_STEPS * ba + 3)
                for j in range(4):
                    rows = slice(HD * j, HD * j + HD)
                    act.activation(csk[rows, :, CS * j + NSEL:CS * j + CS], ckn[rows, :, :], ACT.Copy).then_inc(ck_spread, 1)

            def copy_selv(ba):
                act.wait_ge(c_full, C_UNITS * ba + 5)
                act.activation(csv[0:NSEL, :], ps_c[0:NSEL, :], ACT.Copy).then_inc(c_done, 1)

            def store(b, t):
                act.wait_ge(o_ok, NT * b + t + 2)
                act.dma_start(out[b, t * P:(t + 1) * P, :], t1[:]).then_inc(d_out, 16)

            def slot(seg, b, s):
                c, a, t = seg != "pro", seg != "epi", s - 1
                ba = b + 1 if seg == "loop" else 0
                Ta = NT * ba + t
                if c and s > 1:
                    cs_copy(b, s, 0)
                if a:
                    h_scaled(seg, b, t, "HT", hT, mod_a, moda_ok, ba + 1)
                    act.wait_ge(*m_done_at(seg, b, "HT", t))
                    split_h(Ta)
                if c and s == 1:
                    cs_exps(b, 0)
                if c:
                    for r in range(0 if s == 1 else 1, 4):
                        cs_copy(b, s, r)
                if c:
                    window_exp(b, s, 4)
                    if s == 1:
                        for i in range(4, 8):
                            probs_copy(b, 0, i)
                        copy_out(b, 0)
                        cs_exps(b, s)
                        window_exp(b, s, 5)
                        window_exp(b, s, 6)
                        h_scaled(seg, b, t, "H2T", h2T, mod_c, modc_ok, b + 1)
                    else:
                        cs_exps(b, s)
                        window_exp(b, s, 5)
                        h_scaled(seg, b, t, "H2T", h2T, mod_c, modc_ok, b + 1)
                        window_exp(b, s, 6)
                    window_exp(b, s, 7)
                    window_exp(b, s, 8)
                    window_exp(b, s, 9)
                    copy_z(seg, b, t)
                    window_exp(b, s, 10)
                if a:
                    copy_qT(seg, b, t)
                if c:
                    window_exp(b, s, 11)
                    router_exp(b, t)
                if a:
                    copy_kT(seg, b, t)
                    gate_exp(Ta)
                if c:
                    for i in range(tp_rounds(s)):
                        probs_copy(b, s, i)
                        if i == ZT_ROUND + 1:
                            copy_zT(seg, b, t)
                    copy_out(b, s)
                if a:
                    copy_v(seg, b, t)
                if c:
                    store(b, t)

            def turn(seg, b):
                c2, t = seg != "pro", NT - 1
                ba = b + 1 if seg == "loop" else 0
                Ta = NT * ba + t
                if c2:
                    h_scaled(seg, b, t, "HT", hT, mod_a, moda_ok, ba + 1)
                    act.wait_ge(*m_done_at(seg, b, "HT", t))
                    split_h(Ta)
                for r in range(4, 7):
                    window_exp(ba, 0, r)
                copy_v(seg, b, t)
                if c2:
                    h_scaled(seg, b, t, "H2T", h2T, mod_c, modc_ok, b + 1)
                window_exp(ba, 0, 7)
                window_exp(ba, 0, 8)
                copy_kT(seg, b, t)
                copy_qT(seg, b, t)
                copy_cv(ba)
                window_exp(ba, 0, 9)
                window_exp(ba, 0, 10)
                window_exp(ba, 0, 11)
                if c2:
                    copy_z(seg, b, t)
                    router_exp(b, t)
                gate_exp(Ta)
                for i in range(4):
                    probs_copy(ba, 0, i)
                spread_ck(ba)
                copy_selv(ba)
                cs_copy(ba, 0, 0)
                cs_copy(ba, 0, 1)
                if c2:
                    copy_zT(seg, b, t)
                cs_copy(ba, 0, 2)
                cs_copy(ba, 0, 3)
                if c2:
                    store(b, t)

            def last(seg, b):
                t = NT - 1
                h_scaled(seg, b, t, "H2T", h2T, mod_c, modc_ok, b + 1)
                copy_z(seg, b, t)
                router_exp(b, t)
                copy_zT(seg, b, t)
                store(b, t)

            act.wait_ge(*m_full_at("pro", 0, "MODT", 0))
            ps, done = m_bank("pro", 0, "MODT", 0)
            v = ps[:, 0:4 * NC * B].rearrange("p (m c b) -> p m c b", m=4, c=NC)
            for i in range(4):
                ins = act.activation(modT[:, i], v[:, i], ACT.Copy, bias=float(i % 2))
            ins.then_inc(done, 1)
            act.wait_ge(d_scr, 48)
            def head(t):
                h_scaled("pro", 0, t + 1, "HT", hT, mod_a, moda_ok, 1)
                copy_v("pro", 0, t)
                act.wait_ge(*m_done_at("pro", 0, "HT", t + 1))
                split_h(t + 1)
                gate_exp(t)
                copy_qT("pro", 0, t)
                copy_kT("pro", 0, t)

            h_scaled("pro", 0, 0, "HT", hT, mod_a, moda_ok, 1)
            act.wait_ge(*m_done_at("pro", 0, "HT", 0))
            split_h(0)
            for t in range(NT - 1):
                head(t)
            turn("pro", 0)
            with act.Fori(0, B - 1) as b:
                for s in range(1, NT):
                    slot("loop", b, s)
                turn("loop", b)
            for s in range(1, NT):
                slot("epi", B - 1, s)
            last("epi", B - 1)

        @block.gpsimd
        def _(gp):
            gp.memset(power[:], -0.5).then_inc(set_g, 1)
            gp.memset(csp[:], 0.0).then_inc(set_g, 1)
            gp.memset(csv[:], 0.0).then_inc(set_g, 1)
            gp.memset(onehot[:], 0.0).then_inc(set_g, 1)
            gp.memset(csk[:], 0.0).then_inc(set_g, 1)
            gp.memset(ones[:], 1.0).then_inc(set_g, 1)
            gp.memset(zr[:], 1.0).then_inc(set_g, 1)
            gp.wait_ge(set_g, SETUP_G + 1)

            def deviation_a(Ta):
                gp.wait_ge(lna, 4 * Ta + 4)
                gp.tensor_tensor(vea[:, 1:2], vea[:, 0:1], power[:], ALU.pow).then_inc(lnap, 1)

            def deviation_c(T):
                gp.wait_ge(lnc, 4 * T + 4)
                gp.tensor_tensor(vec[:, 1:2], vec[:, 0:1], power[:], ALU.pow).then_inc(lncp, 1)

            def rotate(seg, b, t, Ta, name, dst):
                gp.wait_ge(*m_done_at(seg, b, name, t))
                gp.tensor_tensor(dst[:], dst[:], rbf[:], ALU.add).then_inc(rope_ok, 1)

            def cs_subtract(b, t):
                T = NT * b + t
                gp.wait_ge(cs_ok, CS_STEPS * T + 4)
                for w, (lo, hi) in enumerate(parts):
                    v = css[:, :, lo:hi]
                    gp.tensor_tensor(v, v, cm[:, w, :].unsqueeze(2).broadcast_to([P, H, hi - lo]), ALU.subtract
                                     ).then_inc(cs_shift, 1)

            def cs_normalise(b, t):
                T = NT * b + t
                gp.wait_ge(cs_ok, CS_STEPS * T + CS_STEPS + 1)
                for lo, n, w in ((0, NSEL, 2), (P - NB, NB, 3)):
                    v = csp[:, :, lo:lo + n]
                    gp.tensor_tensor(v, v, cden[:, w, :].unsqueeze(2).broadcast_to([P, H, n]), ALU.mult
                                     ).then_inc(cs_norm, 1)

            def split_h(Ta):
                gp.wait_ge(hhi_ok, Ta + 2)
                gp.tensor_tensor(h_lo[:], hT[:], h_hi[:], ALU.subtract).then_inc(hlo_ok, 1)

            def residual_in(b, t):
                gp.wait_ge(d_xc[t % 2], 16 * (4 * b + t // 2 + 1))
                if t == 0:
                    gp.wait_ge(d_gbc, 16 * (3 * b + 3))
                gp.tensor_tensor(xc[:, t % 2, :], xc[:, t % 2, :], gbc[:, 2, :], ALU.add).then_inc(xb_ok, 1)

            def weigh_keys(seg, b, t, Ta):
                gp.wait_ge(*m_done_at(seg, b, "KT", t))
                gp.tensor_tensor(ra[:].rearrange("p (c m k) -> p c m k", c=NC, k=CB),
                                 kT[:, :, t * P:(t + 1) * P].rearrange("p c (m k) -> p c m k", k=CB),
                                 wrow[:].unsqueeze(1).unsqueeze(1).broadcast_to([P, NC, P // CB, CB]), ALU.mult
                                 ).then_inc(ckp_ok, 1)

            def slot(seg, b, s, c1, prefetch):
                c2, a, t = seg != "pro", seg != "epi", s - 1
                ba = b + 1 if seg == "loop" else 0
                Ta = NT * ba + t
                if a and c2 and s > 1:
                    split_h(Ta)
                if s == 1:
                    cs_normalise(b, 0)
                if s == 1 and a:
                    rotate(seg, b, t, Ta, "Q", ra)
                if c2:
                    residual_in(b, t)
                if c1 and s < NT:
                    cs_subtract(b, s)
                if a and s == 1:
                    rotate(seg, b, t, Ta, "K", kr)
                if c2:
                    deviation_c(NT * b + t)
                if a and s > 1:
                    rotate(seg, b, t, Ta, "Q", ra)
                    rotate(seg, b, t, Ta, "K", kr)
                if c1 and s < NT:
                    cs_normalise(b, s)
                if a:
                    weigh_keys(seg, b, t, Ta)
                if c1 and s == NT:
                    deviation_a(Ta + 1)
                    cs_subtract(ba, 0)
                if prefetch:
                    deviation_a(Ta + 1)

            gp.wait_ge(d_first, 16 * (N_FIRST))
            deviation_a(0)
            deviation_a(1)
            split_h(0)
            for t in range(NT - 1):
                rotate("pro", 0, t, t, "Q", ra)
                rotate("pro", 0, t, t, "K", kr)
                split_h(t + 1)
                weigh_keys("pro", 0, t, t)
                if t + 2 < NT:
                    deviation_a(t + 2)
            slot("pro", 0, NT, True, False)
            with gp.Fori(0, B - 1) as b:
                for s in range(1, NT + 1):
                    slot("loop", b, s, True, s < NT)
            for s in range(1, NT + 1):
                slot("epi", B - 1, s, s < NT, False)

        @block.vector
        def _(dve):
            steps = [0]

            def setup(ins):
                steps[0] += 1
                ins.then_inc(set_v, 1)
                dve.wait_ge(set_v, steps[0] + 1)

            dve.wait_ge(d_first, 16 * (N_FIRST))
            dve.wait_ge(set_a, 2)
            setup(dve.tensor_scalar(silu[:, 0], silu[:, 0], 1.0, None, ALU.add))
            setup(dve.reciprocal(silu[:, 1], silu[:, 0]))
            setup(dve.tensor_tensor(silu[:, 2], cT_s[:], silu[:, 1], ALU.mult))
            assert steps[0] == SILU_STEPS
            setup(dve.tensor_copy(ident_b[:], ident))
            setup(dve.tensor_copy(wmask[:], masks[:, 0:2 * P]))
            setup(dve.tensor_copy(csmask[:, :, NSEL:CS], masks[:, 2 * P:].rearrange("p (t n) -> p t n", t=NT)))
            setup(dve.tensor_scalar(blkw[:], cst[:, C_BLK:C_TOK], wcol[:], None, ALU.mult))
            setup(dve.memset(pew[:], 1.0))
            setup(dve.tensor_scalar(pew[:], pew[:], wcol[0:CB, :], None, ALU.mult))
            setup(dve.tensor_tensor(peT[:], peT[:], wrow[:].unsqueeze(1).broadcast_to([P, NC, CB]), ALU.mult))
            setup(dve.tensor_reduce(pewT[:], peT[:], AX.X, ALU.add))
            for k, i in enumerate((2, 5)):
                if k == 1:
                    for j in range(3):
                        dve.wait_ge(whi_ok, j + 2)
                        dve.tensor_tensor(w_lo[:, j], w_stage[j], w_hi[:, j], ALU.subtract).then_inc(wlo_ok, 1)
                dve.wait_ge(*m_full_at("pro", 0, f"MOD{i}", 0))
                ps, done = m_bank("pro", 0, f"MOD{i}", 0)
                dve.tensor_copy(gpart[:, 0, :], ps[0:B, :]).then_inc(done, 1)
                dve.wait_ge(*m_done_at("pro", 0, f"MOD{i}", 0))
                setup(dve.tensor_scalar(gpart[:, 1, :], gpart[:, 0, :], 0.0, 2.0, ALU.is_ge, ALU.mult))
                setup(dve.tensor_scalar(gpart[:, 1, :], gpart[:, 1, :], -1.0, None, ALU.add))
                setup(dve.scalar_tensor_tensor(out=gpart[:, 0, :], in0=gpart[:, 0, :], scalar=-1.0, in1=gpart[:, 0, :],
                                               op0=ALU.mult, op1=ALU.max))
                setup(dve.scalar_tensor_tensor(out=gr[:, k, :], in0=gpart[:, 0, :], scalar=0.25, in1=gpart[:, 1, :],
                                               op0=ALU.max, op1=ALU.mult))
            setup(dve.tensor_tensor(gr[:, 2, :], gr[:, 0, :], bo_s, ALU.mult))
            setup(dve.memset(zero_b[:], 0.0))
            assert steps[0] == SETUP_V

            def hold():
                dve.memset(held[:], 0.0)

            def ln_stats(x_, st, mv, ve, s, T):
                dve.bn_stats(st[:], x_).then_inc(s, 1)
                dve.wait_ge(s, 4 * T + 2)
                hold()
                dve.bn_aggr(mv[:], st[:]).then_inc(s, 1)
                dve.wait_ge(s, 4 * T + 3)
                dve.tensor_scalar(ve[:, 0:1], mv[:, 1:2], EPS, None, ALU.add).then_inc(s, 1)

            def ln_scale(x_, mv, ve, dst, s, sp_, T):
                dve.wait_ge(sp_, T + 2)
                dve.tensor_scalar(dst, x_, mv[:, 0:1], ve[:, 1:2], ALU.subtract, ALU.mult).then_inc(s, 1)

            def ln_a(seg, b, t, Ta, tile_a):
                dve.wait_ge(d_xa[tile_a % 2], 16 * (4 * (b + 1 if seg == "loop" else b) + tile_a // 2 + 1))
                ln_stats(xa[:, tile_a % 2, :], sta, mva, vea, lna, Ta)
                ln_scale(xa[:, tile_a % 2, :], mva, vea, xa[:, tile_a % 2, :], lna, lnap, Ta)

            def mod_copy(b, dst, first, ok):
                dve.tensor_copy(dst[:], modT[:, first:first + 2, :, b]).then_inc(ok, 1)

            def rope(seg, b, t, name):
                dve.wait_ge(*m_full_at(seg, b, name, t))
                if name == "Q":
                    dve.wait_ge(ckr_ok, NT * (b + 1 if seg == "loop" else 0) + t + 1)
                ps, done = m_bank(seg, b, name, t)
                q3 = ps[:].rearrange("p (h n) -> p h n", h=H)
                q4 = ps[:].rearrange("p (h n e) -> p h n e", h=H, e=2)
                r4 = rbf[:].rearrange("p (h n e) -> p h n e", h=H, e=2)
                dve.tensor_tensor((ra if name == "Q" else kr)[:].rearrange("p (h n) -> p h n", h=H), q3,
                                  rot[:, t, 0:HD].unsqueeze(1).broadcast_to([P, H, HD]), ALU.mult)
                for e in range(2):
                    half = HD // 2
                    w = rot[:, t, HD + e * half:HD + (e + 1) * half].unsqueeze(1).broadcast_to([P, H, half])
                    ins = dve.tensor_tensor(r4[:, :, :, e], q4[:, :, :, 1 - e], w, ALU.mult)
                ins.then_inc(done, 1)

            def sum_q(seg, b, t, Ta):
                dve.wait_ge(*m_done_at(seg, b, "QT", t))
                dve.tensor_reduce(qsum[:, :, t], qT[:, :, t * P:(t + 1) * P], AX.X, ALU.add).then_inc(qsum_ok, 1)

            def gates_soft(seg, b, t, Ta, part):
                if part == 1:
                    dve.wait_ge(g_exp, Ta + 2)
                    dve.reciprocal(gl[:, 7:8], gl[:, 7:8]).then_inc(g_ok, 1)
                    dve.wait_ge(g_ok, G_STEPS * Ta + 3)
                    dve.tensor_scalar(gates[:, t, :], gl[:, 3:6], gl[:, 7:8], None, ALU.mult).then_inc(g_ok, 1)
                    return
                dve.wait_ge(*m_full_at(seg, b, "G", t))
                ps, done = m_bank(seg, b, "G", t)
                dve.tensor_tensor(gl[:, 0:3], ps[:, 0:3], bg_s[:], ALU.add).then_inc(done, 1)
                dve.wait_ge(*m_done_at(seg, b, "G", t))
                dve.tensor_reduce(gl[:, 6:7], gl[:, 0:3], AX.X, ALU.max, negate=True).then_inc(g_ok, 1)

            def window_max(b, t, r):
                T = NT * b + t
                dve.wait_ge(s_full[s_bank(t, r)], s_before(T, t, r) + 2)
                if r == 4:
                    dve.wait_ge(s_done[11 % 3], 4 * T + 1)
                n = 2 * P if t else P
                dve.tensor_reduce(wmax[:, 2 * (r - 4):2 * (r - 3)],
                                  ps_s[s_bank(t, r)][:, 0:2 * n].rearrange("p (c n) -> p c n", c=2), AX.X, ALU.max,
                                  negate=True).then_inc(wmax_ok, 1)

            def window_norm(b, t, half):
                T = NT * b + t
                h0 = 8 * half
                r = 4 + 4 * half + 3
                dve.wait_ge(s_done[s_bank(t, r)], s_before(T, t, r) + 2)
                base = WN_STEPS * T + WN_STEPS // 2 * half
                dve.reciprocal(wden[:, 1, h0:h0 + 8], wden[:, 0, h0:h0 + 8]).then_inc(wn_ok, 1)
                dve.wait_ge(wn_ok, base + 2)
                dve.tensor_scalar(wden[:, 2, h0:h0 + 8], wden[:, 1, h0:h0 + 8], gates[:, t, 2:3], None, ALU.mult
                                  ).then_inc(wn_ok, 1)
                dve.wait_ge(wn_ok, base + 3)
                lo = 0 if t else P
                for h in range(h0, h0 + 8):
                    dve.tensor_scalar(pw[:, h, lo:2 * P], pw[:, h, lo:2 * P], wden[:, 2, h:h + 1], None, ALU.mult
                                      ).then_inc(wn_ok, 1)

            def cs_max(b, t):
                T = NT * b + t
                base = CS_STEPS * T
                dve.wait_ge(s_done[s_bank(t, 3)], s_before(T, t, 3) + 2)
                for w, (lo, hi) in enumerate(parts):
                    dve.tensor_reduce(cm[:, w, :], css[:, :, lo:hi], AX.X, ALU.max).then_inc(cs_ok, 1)
                dve.wait_ge(cs_ok, base + 3)
                dve.tensor_scalar(cm[:], cm[:], FLOOR, None, ALU.max).then_inc(cs_ok, 1)

            def cs_factor(b, t):
                T = NT * b + t
                base = CS_STEPS * T
                dve.wait_ge(cs_exp, 2 * T + 3)
                for w, (lo, n) in enumerate(((0, NSEL), (P - NB, NB))):
                    dve.tensor_reduce(cden[:, w, :], csp[:, :, lo:lo + n], AX.X, ALU.add).then_inc(cs_ok, 1)
                dve.wait_ge(cs_ok, base + 6)
                dve.tensor_scalar(cden[:, 0:2, :], cden[:, 0:2, :], 1e-30, None, ALU.max).then_inc(cs_ok, 1)
                dve.wait_ge(cs_ok, base + 7)
                dve.reciprocal(cden[:, 2:4, :], cden[:, 0:2, :]).then_inc(cs_ok, 1)
                dve.wait_ge(cs_ok, base + 8)
                for w, g in ((2, 1), (3, 0)):
                    dve.tensor_scalar(cden[:, w, :], cden[:, w, :], gates[:, t, g:g + 1], None, ALU.mult).then_inc(cs_ok, 1)

            def residual(seg, b, t):
                T = NT * b + t
                dve.wait_ge(*m_full_at(seg, b, "Y", t))
                ps, done = m_bank(seg, b, "Y", t)
                if t == 0:
                    dve.wait_ge(d_gbc, 16 * (3 * b + 3))
                dve.wait_ge(o_ok, T + 1)
                dve.wait_ge(d_out, 16 * (T + 1))
                dve.tensor_tensor(t1[:], ps[:], gbc[:, 0, :], ALU.mult).then_inc(done, 1)
                dve.wait_ge(*m_done_at(seg, b, "Y", t))
                dve.wait_ge(xb_ok, T + 2)
                dve.tensor_tensor(x1[:], t1[:], xc[:, t % 2, :], ALU.add).then_inc(y_ok, 1)
                dve.wait_ge(y_ok, T + 2)
                ln_stats(x1[:], stc, mvc, vec, lnc, T)

            def router(seg, b, t, part):
                T = NT * b + t
                base = R_STEPS * T
                n = [0 if part == 0 else 2]

                def step(ins):
                    n[0] += 1
                    ins.then_inc(r_ok, 1)
                    if n[0] != 2:
                        dve.wait_ge(r_ok, base + n[0] + 1)

                if part == 0:
                    dve.wait_ge(*m_done_at(seg, b, "Z", t))
                    step(dve.tensor_tensor(ro[:, 0:E], zs[:, NZ:NZ + E], rb_s[:], ALU.add))
                    step(dve.tensor_reduce(ro[:, 6:7], ro[:, 0:E], AX.X, ALU.max, negate=True))
                    return
                dve.wait_ge(r_exp, T + 2)
                step(dve.reciprocal(ro[:, 15:16], ro[:, 7:8]))
                step(dve.tensor_scalar(ro[:, 16:16 + E], ro[:, 8:8 + E], ro[:, 15:16], None, ALU.mult))
                hold()
                step(dve.max(ro[:, 24:32], ro[:, 16:24]))
                hold()
                step(dve.max_index(roi[:], ro[:, 24:32], ro[:, 16:24]))
                step(dve.tensor_copy(ro[:, 40:42], roi[:, 0:2]))
                step(dve.tensor_scalar(ro[:, 32:32 + E], cst[:, C_IO:C_IO + E], ro[:, 40:41], None, ALU.is_equal))
                step(dve.scalar_tensor_tensor(out=ro[:, 32:32 + E], in0=cst[:, C_IO:C_IO + E], scalar=ro[:, 41:42],
                                              in1=ro[:, 32:32 + E], op0=ALU.is_equal, op1=ALU.add))
                step(dve.tensor_tensor(ro[:, 32:32 + E], ro[:, 32:32 + E], ro[:, 16:16 + E], ALU.mult))
                step(dve.tensor_reduce(ro[:, 42:43], ro[:, 32:32 + E], AX.X, ALU.add))
                step(dve.tensor_scalar(ro[:, 42:43], ro[:, 42:43], 1e-6, None, ALU.add))
                step(dve.reciprocal(ro[:, 43:44], ro[:, 42:43]))
                step(dve.tensor_scalar(ro[:, 32:32 + E], ro[:, 32:32 + E], ro[:, 43:44], None, ALU.mult))
                step(dve.tensor_copy(zr[:, 0:R], zs[:, 0:R]))
                step(dve.tensor_tensor(zr[:, R:NZ].rearrange("p (e r) -> p e r", e=E),
                                       zs[:, R:NZ].rearrange("p (e r) -> p e r", e=E),
                                       ro[:, 32:32 + E].unsqueeze(2).broadcast_to([P, E, R]), ALU.mult))
                assert n[0] == R_STEPS

            def final(seg, b, t):
                T = NT * b + t
                dve.wait_ge(*m_full_at(seg, b, "F", t))
                ps, done = m_bank(seg, b, "F", t)
                dve.tensor_tensor(t1[:], ps[:], gbc[:, 1, :], ALU.mult).then_inc(done, 1)
                dve.wait_ge(*m_done_at(seg, b, "F", t))
                dve.tensor_tensor(t1[:], x1[:], t1[:], ALU.add).then_inc(o_ok, 1)

            def sum_keys(Ta, t):
                dve.wait_ge(ckp_ok, Ta + 2)
                nb = P // CB
                dve.tensor_reduce(ckn[:, :, nb * t:nb * t + nb], ra[:].rearrange("p (c m k) -> p c m k", c=NC, k=CB),
                                  AX.X, ALU.add).then_inc(ckr_ok, 1)

            def finish_keys(ba):
                dve.wait_ge(ckr_ok, NT * ba + NT + 1)
                dve.tensor_tensor(ckn[:], ckn[:], pewT[:].unsqueeze(2).broadcast_to([P, NC, NB]), ALU.add).then_inc(b_ok, 1)

            def sum_queries(ba):
                dve.wait_ge(qsum_ok, NT * ba + NT + 1)
                dve.tensor_reduce(qs[:], qsum[:], AX.X, ALU.add).then_inc(b_ok, 1)

            def choose(ba):
                base = B_STEPS * ba
                dve.wait_ge(c_full, C_UNITS * ba + 3)
                dve.tensor_copy(imp[:], ps_c[0:1, 0:NB]).then_inc(c_done, 1)
                dve.wait_ge(c_done, C_UNITS * ba + 3)
                hold()
                dve.max(top[:], imp[:]).then_inc(b_ok, 1)
                dve.wait_ge(b_ok, base + 4)
                hold()
                dve.max_index(topi[:], top[:], imp[:]).then_inc(b_ok, 1)
                dve.wait_ge(b_ok, base + 5)
                dve.tensor_scalar(pos[:], topi[:, 0:2], float(CB), None, ALU.mult).then_inc(b_ok, 1)

            def gather(ba):
                base = B_STEPS * ba
                dve.wait_ge(c_full, C_UNITS * ba + 4)
                dve.tensor_copy(posb[:], ps_c[:, 0:2]).then_inc(c_done, 1)
                dve.wait_ge(c_done, C_UNITS * ba + 4)
                hold()
                first = [dve.value_load(topi[0:1, j:j + 1], min_val=0, max_val=NB - 1) for j in range(TOPK)]
                for j in range(TOPK):
                    own, tile = slice(SB * j, SB * j + SB), bass.ds(first[j] // (P // CB), 1)
                    dve.tensor_copy(v_tiles[j][:], v_s[:, tile, :].squeeze(1)).then_inc(b_ok, 1)
                    dve.tensor_copy(tokj[:, j, :], token[:, tile, own].squeeze(1)).then_inc(b_ok, 1)
                    dve.wait_ge(b_ok, base + 8 + 3 * j)
                    dve.tensor_scalar(onehot[:, j, own], tokj[:, j, :], posb[:, j:j + 1], None, ALU.is_equal
                                      ).then_inc(b_ok, 1)
                for j in range(TOPK):
                    own = slice(SB * j, SB * j + SB)
                    for i in range(4):
                        rows = slice(HD * i, HD * i + HD)
                        dve.tensor_copy(csk[rows, :, CS * i + SB * j:CS * i + SB * j + SB],
                                        kT[rows, :, bass.ds(first[j] * CB, SB)]).then_inc(b_ok, 1)
                    dve.tensor_scalar(csmask[:, :, own], token[:, :, own], posb[:, j:j + 1], NEG, ALU.is_lt, ALU.mult
                                      ).then_inc(b_ok, 1)

            def slot(seg, b, s):
                c, a, t = seg != "pro", seg != "epi", s - 1
                ba = b + 1 if seg == "loop" else 0
                Ta = NT * ba + t
                if c and s == 1:
                    if a:
                        dve.wait_ge(hhi_ok, Ta + 2)
                        dve.tensor_tensor(h_lo[:], hT[:], h_hi[:], ALU.subtract).then_inc(hlo_ok, 1)
                    cs_factor(b, 0)
                    if a:
                        rope(seg, b, t, "Q")
                if c:
                    window_max(b, s, 4)
                    cs_max(b, s)
                if c and s == 1:
                    window_max(b, s, 5)
                    window_max(b, s, 6)
                    if a:
                        dve.wait_ge(rope_ok, 2 * Ta + 2)
                        rope(seg, b, t, "K")
                    cs_factor(b, s)
                    residual(seg, b, t)
                    window_max(b, s, 7)
                    ln_scale(x1[:], mvc, vec, xc[:, t % 2, :], lnc, lncp, NT * b + t)
                if c and s > 1:
                    residual(seg, b, t)
                    window_max(b, s, 5)
                    ln_scale(x1[:], mvc, vec, xc[:, t % 2, :], lnc, lncp, NT * b + t)
                if a and not (c and s == 1):
                    rope(seg, b, t, "Q")
                if c and s > 1:
                    window_max(b, s, 6)
                    window_max(b, s, 7)
                    cs_factor(b, s)
                if a and not (c and s == 1):
                    dve.wait_ge(rope_ok, 2 * Ta + 2)
                    rope(seg, b, t, "K")
                if c:
                    window_max(b, s, 8)
                    window_max(b, s, 9)
                    window_max(b, s, 10)
                    router(seg, b, t, 0)
                if a:
                    gates_soft(seg, b, t, Ta, 0)
                if c:
                    window_max(b, s, 11)
                    window_norm(b, s, 0)
                    window_norm(b, s, 1)
                    router(seg, b, t, 1)
                if a:
                    gates_soft(seg, b, t, Ta, 1)
                    sum_q(seg, b, t, Ta)
                    sum_keys(Ta, t)
                    ln_a(seg, b, s - 1, Ta + 1, s)
                if c:
                    final(seg, b, t)

            def turn(seg, b):
                c2, t = seg != "pro", NT - 1
                ba = b + 1 if seg == "loop" else 0
                Ta = NT * ba + t
                window_max(ba, 0, 4)
                window_max(ba, 0, 5)
                if c2:
                    residual(seg, b, t)
                rope(seg, b, t, "Q")
                if c2:
                    ln_scale(x1[:], mvc, vec, xc[:, t % 2, :], lnc, lncp, NT * b + t)
                window_max(ba, 0, 6)
                dve.wait_ge(rope_ok, 2 * Ta + 2)
                rope(seg, b, t, "K")
                window_max(ba, 0, 7)
                window_max(ba, 0, 8)
                window_max(ba, 0, 9)
                window_max(ba, 0, 10)
                sum_q(seg, b, t, Ta)
                sum_queries(ba)
                gates_soft(seg, b, t, Ta, 0)
                sum_keys(Ta, t)
                finish_keys(ba)
                window_max(ba, 0, 11)
                window_norm(ba, 0, 0)
                if c2:
                    router(seg, b, t, 0)
                choose(ba)
                window_norm(ba, 0, 1)
                gather(ba)
                if c2:
                    router(seg, b, t, 1)
                gates_soft(seg, b, t, Ta, 1)
                ln_a(seg, b + 1, t, Ta + 1, 0)
                mod_copy((ba + 1) % B, mod_a, 0, moda_ok)
                if c2:
                    final(seg, b, t)
                cs_max(ba, 0)

            def last(seg, b):
                t = NT - 1
                residual(seg, b, t)
                ln_scale(x1[:], mvc, vec, xc[:, t % 2, :], lnc, lncp, NT * b + t)
                router(seg, b, t, 0)
                router(seg, b, t, 1)
                final(seg, b, t)

            dve.wait_ge(set_g, SETUP_G + 1)
            dve.memset(ro[:, 16 + E:24], -1.0)
            dve.wait_ge(*m_done_at("pro", 0, "MODT", 0))
            mod_copy(0, mod_a, 0, moda_ok)
            ln_a("pro", 0, -1, 0, 0)
            ln_a("pro", 0, -1, 1, 1)
            for t in range(NT - 1):
                rope("pro", 0, t, "Q")
                dve.wait_ge(rope_ok, 2 * t + 2)
                rope("pro", 0, t, "K")
                gates_soft("pro", 0, t, t, 0)
                gates_soft("pro", 0, t, t, 1)
                sum_q("pro", 0, t, t)
                sum_keys(t, t)
                if t + 2 < NT:
                    ln_a("pro", 0, t, t + 2, t + 2)
            turn("pro", 0)
            with dve.Fori(0, B - 1) as b:
                mod_copy(b, mod_c, 2, modc_ok)
                for s in range(1, NT):
                    slot("loop", b, s)
                turn("loop", b)
            mod_copy(B - 1, mod_c, 2, modc_ok)
            for s in range(1, NT):
                slot("epi", B - 1, s)
            last("epi", B - 1)


def kernel(L0_attn_x, L0_attn_Wq, L0_attn_Wk, L0_attn_Wv, L0_attn_Wo, L0_attn_bo, L0_attn_wk_comp, L0_attn_wv_comp,
           L0_attn_pe, L0_attn_Wg, L0_attn_bg, L0_ffn_base_W, L0_ffn_base_b, L0_ffn_shared_A, L0_ffn_shared_B,
           L0_ffn_routed_A, L0_ffn_routed_B, L0_ffn_router_W, L0_ffn_router_b, L0_c, L0_wmod):
    import concourse.bacc as bacc
    from concourse.bass_utils import run_bass_kernel_spmd

    f = np.asarray
    arrays = {
        "x": f(L0_attn_x),
        "wqkv": np.concatenate([f(L0_attn_Wq), f(L0_attn_Wk), f(L0_attn_Wv)], axis=1),
        "wo": f(L0_attn_Wo),
        "wbt": f(L0_ffn_base_W).T,
        "wa": np.concatenate([f(L0_ffn_shared_A), f(L0_ffn_routed_A).reshape(E * R, D), f(L0_ffn_router_W)]).T,
        "wb": np.concatenate([f(L0_ffn_shared_B).T, f(L0_ffn_routed_B).transpose(0, 2, 1).reshape(E * R, D),
                              f(L0_ffn_base_b)[None]]),
        "cT": f(L0_c).T,
        "wmod": f(L0_wmod),
        "bo": f(L0_attn_bo),
        "bg": f(L0_attn_bg),
        "rb": f(L0_ffn_router_b),
        "wcomp": np.stack([f(L0_attn_wk_comp), f(L0_attn_wv_comp)]),
        "pe": f(L0_attn_pe),
        "pet": f(L0_attn_pe).T,
        "wg": f(L0_attn_Wg),
        "const": constants(),
    }
    arrays = {k: np.ascontiguousarray(a) for k, a in arrays.items()}
    nc = bacc.Bacc("TRN2", target_bir_lowering=False, num_devices=1)
    ins = {k: nc.dram_tensor(f"{k}_in", a.shape, mybir.dt.from_np(a.dtype), kind="ExternalInput").ap()
           for k, a in arrays.items()}
    gscr = nc.dram_tensor("gate_rows", [3, B, D], F32, kind="Internal").ap()
    out = nc.dram_tensor("out", [B, S, D], F32, kind="ExternalOutput").ap()
    program(nc, **ins, gscr=gscr, out=out)
    r = run_bass_kernel_spmd(nc, [{f"{k}_in": a for k, a in arrays.items()}], core_ids=[0])
    return r.results[0]["out"]
```
